# Optimizing a Trainium2 kernel written in Bass

```python
import numpy as np
import jax
import jax.numpy as jnp

def _softmax(x, axis=-1):
    return jax.nn.softmax(x, axis=axis)

def _gelu(x):
    return jax.nn.gelu(x, approximate=True)

def _silu(x):
    return jax.nn.silu(x)

def _sigmoid(x):
    return jax.nn.sigmoid(x)

def _layernorm(x, axis=-1, eps=1e-05):
    m = jnp.mean(x, axis=axis, keepdims=True)
    v = jnp.var(x, axis=axis, keepdims=True)
    return (x - m) / jnp.sqrt(v + eps)

def _scatter_add(tgt, idx, src, axis=0):
    return tgt.at[idx].add(src)

def _segment_sum(src, seg, n):
    return jax.ops.segment_sum(src, seg, n)
kernel_name = 'mk_gnn_preln_d2_gnn_r32_6c996a'

def setup_inputs(seed: int=0):
    np.random.seed(seed)
    _w = jnp.asarray

    def _rec_inputs():
        import jax
        import jax.numpy as jnp
        _gk = jax.random.key(seed)
        x = -0.0005121 + 1.001 * jax.random.normal(jax.random.fold_in(_gk, 1), (50000, 160), jnp.float32)
        src = jax.random.randint(jax.random.fold_in(_gk, 2), (25000,), 0, 50000, jnp.int32)
        dst = jax.random.randint(jax.random.fold_in(_gk, 3), (25000,), 0, 50000, jnp.int32)
        _o = jnp.argsort(dst, stable=True)
        src = src[_o]
        dst = dst[_o]
        edge_attr_16 = jax.random.uniform(jax.random.fold_in(_gk, 12), (25000, 16), jnp.float32, 0.0, 1)
        edge_attr_3 = 0.00262751 + 0.999568 * jax.random.normal(jax.random.fold_in(_gk, 13), (25000, 3), jnp.float32)
        edge_attr_4 = 0.000898722 + 1.00012 * jax.random.normal(jax.random.fold_in(_gk, 14), (25000, 4), jnp.float32)
        edge_attr_64 = jax.random.uniform(jax.random.fold_in(_gk, 15), (25000, 64), jnp.float32, 0.0, 1)
        node_vec1 = jax.random.uniform(jax.random.fold_in(_gk, 17), (50000, 1), jnp.float32, 0.0, 1)
        return (x, src, dst, edge_attr_16, edge_attr_3, edge_attr_4, edge_attr_64, node_vec1)
    x, src, dst, edge_attr_16, edge_attr_3, edge_attr_4, edge_attr_64, node_vec1 = _rec_inputs()

    def _L0_gnn_setup():
        import jax, jax.numpy as jnp
        import numpy as np
        N, E = (625, 10000)
        CS, CV = (64, 32)
        AS_, AV, H = (16, 8, 4)
        NB = 16
        SQRT3 = 1.7320508075688772
        SQRT2 = 1.4142135623730951
        EPS = 1e-05

        def _cg_tp(s, v, y0, y1, w_ss, w_sv, w_vs, w_vv0, w_vv1):
            out_s = jnp.concatenate([w_ss * s * y0[:, None], w_vv0 * (jnp.einsum('eci,ei->ec', v, y1) / SQRT3)], axis=-1)
            out_v = jnp.concatenate([(w_sv * s)[:, :, None] * y1[:, None, :], (w_vs * jnp.ones_like(v[..., 0]))[..., None] * v * y0[:, None, None], (w_vv1 * jnp.ones_like(v[..., 0]))[..., None] * (jnp.cross(v, y1[:, None, :]) / SQRT2)], axis=1)
            return (out_s, out_v)

        def _equiv_layernorm(s, v, gamma_s, beta_s, gamma_v):
            mu = jnp.mean(s, axis=-1, keepdims=True)
            var = jnp.var(s, axis=-1, keepdims=True)
            s_n = (s - mu) * jax.lax.rsqrt(var + EPS) * gamma_s + beta_s
            rms = jnp.sqrt(jnp.mean(jnp.sum(v * v, axis=-1), axis=-1, keepdims=True) + EPS)
            v_n = v / rms[..., None] * gamma_v[None, :, None]
            return (s_n, v_n)
        key = jax.random.key(seed)
        ks = jax.random.split(key, 26)

        def rn(k, shape, fan):
            return jax.random.normal(k, shape, jnp.float32) / np.sqrt(fan)
        D1S, D1V = (CS + CV, CS + 2 * CV)
        WN = 2 * CS + 3 * CV
        inp = {'node': jax.random.normal(ks[0], (N, CS + 3 * CV), jnp.float32), 'edge_index': jax.random.randint(ks[1], (2, E), 0, N, jnp.int64 if jax.config.jax_enable_x64 else jnp.int32), 'rbf': jax.random.uniform(ks[2], (E, NB), jnp.float32), 'rsh': jax.random.normal(ks[3], (E, 4), jnp.float32), 'gamma_s': jnp.ones((CS,), jnp.float32), 'beta_s': jnp.zeros((CS,), jnp.float32), 'gamma_v': jnp.ones((CV,), jnp.float32), 'Ws_src': rn(ks[4], (CS, CS), CS), 'Wv_src': rn(ks[5], (CV, CV), CV), 'Ws_dst': rn(ks[6], (CS, CS), CS), 'Wv_dst': rn(ks[7], (CV, CV), CV), 'W_rbf': rn(ks[8], (NB, WN), NB), 'W_alpha': rn(ks[9], (D1S, H * AS_), D1S), 'alpha_dot': rn(ks[10], (1, H, AS_), AS_), 'Ws_val': rn(ks[11], (D1S, CS), D1S), 'Wv_val': rn(ks[12], (D1V, CV), D1V), 'Wg': rn(ks[13], (CS, CV), CS), 'w2_ss': rn(ks[14], (CS,), 1), 'w2_sv': rn(ks[15], (CS,), 1), 'w2_vs': rn(ks[16], (CV,), 1), 'w2_vv0': rn(ks[17], (CV,), 1), 'w2_vv1': rn(ks[18], (CV,), 1), 'Ws_vlin': rn(ks[19], (D1S, H * AS_), D1S), 'Wv_vlin': rn(ks[20], (D1V, H * AV), D1V), 'Wps': rn(ks[21], (H * AS_, CS), H * AS_), 'Wpv': rn(ks[22], (H * AV, CV), H * AV)}
        return inp
    _L0_gnn_all = _L0_gnn_setup()
    _L0_gnn_in = {k: v for k, v in _L0_gnn_all.items() if k in ('gamma_s', 'beta_s', 'gamma_v', 'Ws_src', 'Wv_src', 'Ws_dst', 'Wv_dst', 'W_rbf', 'W_alpha', 'alpha_dot', 'Ws_val', 'Wv_val', 'Wg', 'w2_ss', 'w2_sv', 'w2_vs', 'w2_vv0', 'w2_vv1', 'Ws_vlin', 'Wv_vlin', 'Wps', 'Wpv')}
    del _L0_gnn_all

    def _L1_gnn_setup():
        import jax, jax.numpy as jnp
        import numpy as np
        N, E = (10000, 5000)
        C0, C1 = (64, 32)
        H, A = (8, 8)
        H0, H1 = (8, 4)
        M0, M1 = (128, 64)
        NG, RH = (64, 64)
        WN = C0 + C0 + C1 + C1 + C1
        DS, DV = (C0 + C1, C0 + 2 * C1)
        EPS = 1e-05
        SQ3 = np.float32(np.sqrt(3.0))
        SQ2 = np.float32(np.sqrt(2.0))

        def _split(x):
            return (x[:, :C0], x[:, C0:].reshape(x.shape[0], C1, 3))

        def _merge(s, v):
            return jnp.concatenate([s, v.reshape(v.shape[0], -1)], axis=1)

        def _eq_ln(x, w0, b0, w1):
            s, v = _split(x)
            s = s - s.mean(axis=1, keepdims=True)
            s = s * jax.lax.rsqrt(jnp.square(s).mean(axis=1, keepdims=True) + EPS) * w0 + b0
            v = v * jax.lax.rsqrt(jnp.square(v).mean(axis=(1, 2), keepdims=True) + EPS) * w1[None, :, None]
            return (s, v)

        def _eq_lin(s, v, ws, bs, wv):
            return (s @ ws + bs, jnp.einsum('nud,uk->nkd', v, wv))

        def _ln(x, g, b):
            xc = x - x.mean(-1, keepdims=True)
            return xc * jax.lax.rsqrt(jnp.square(xc).mean(-1, keepdims=True) + EPS) * g + b

        def _smooth_leaky(x, alpha=0.2):
            return 0.5 * (1 + alpha) * x + 0.5 * (1 - alpha) * x * (2.0 * jax.nn.sigmoid(x) - 1.0)

        def _forward(node_input, node_attr, edge_vec, edge_scalars, edge_src, edge_dst, ln1_w0, ln1_b0, ln1_w1, ln2_w0, ln2_b0, ln2_w1, msrc_ws, msrc_wv, mdst_ws, mdst_bs, mdst_wv, rw1, rb1, rg1, rbe1, rw2, rb2, rg2, rbe2, rw3, roff, lin_ws, lin_bs, lin_wv, alpha_dot, proj_ws, proj_bs, proj_wv, f1_ws, f1_bs, f1_wv, f2_ws, f2_bs, f2_wv):
            n = node_input.shape[0]
            s, v = _eq_ln(node_input, ln1_w0, ln1_b0, ln1_w1)
            src_s = s @ msrc_ws
            src_v = jnp.einsum('nud,uk->nkd', v, msrc_wv)
            dst_s = s @ mdst_ws + mdst_bs
            dst_v = jnp.einsum('nud,uk->nkd', v, mdst_wv)
            ms = src_s[edge_src] + dst_s[edge_dst]
            mv = src_v[edge_src] + dst_v[edge_dst]
            h = jax.nn.silu(_ln(edge_scalars @ rw1 + rb1, rg1, rbe1))
            h = jax.nn.silu(_ln(h @ rw2 + rb2, rg2, rbe2))
            w = h @ rw3 + roff
            rhat = edge_vec * jax.lax.rsqrt(jnp.sum(jnp.square(edge_vec), -1, keepdims=True) + 1e-12)
            Y1 = SQ3 * rhat
            w1, w2, w3, w4, w5 = jnp.split(w, [C0, 2 * C0, 2 * C0 + C1, 2 * C0 + 2 * C1], axis=1)
            o0a = w1 * ms
            o0b = w4 * (jnp.einsum('eud,ed->eu', mv, Y1) / SQ3)
            o1a = (w2 * ms)[:, :, None] * Y1[:, None, :]
            o1b = w3[:, :, None] * mv
            o1c = w5[:, :, None] * (jnp.cross(mv, Y1[:, None, :]) / SQ2)
            ds = jnp.concatenate([o0a, o0b], axis=1)
            dv = jnp.concatenate([o1a, o1b, o1c], axis=1)
            ls, lv = _eq_lin(ds, dv, lin_ws, lin_bs, lin_wv)
            e = ls.shape[0]
            alpha = ls[:, :H * A].reshape(e, H, A)
            vs = ls[:, H * A:].reshape(e, H, H0)
            vv = lv.reshape(e, H, H1, 3)
            a = jnp.einsum('ehk,hk->eh', _smooth_leaky(alpha), alpha_dot)
            amax = jax.lax.stop_gradient(jax.ops.segment_max(a, edge_dst, num_segments=n))
            a = jnp.exp(a - amax[edge_dst])
            a = a / (jax.ops.segment_sum(a, edge_dst, num_segments=n)[edge_dst] + 1e-12)
            ns = jax.ops.segment_sum(vs * a[..., None], edge_dst, num_segments=n).reshape(n, H * H0)
            nv = jax.ops.segment_sum(vv * a[..., None, None], edge_dst, num_segments=n).reshape(n, H * H1, 3)
            ps, pv = _eq_lin(ns, nv, proj_ws, proj_bs, proj_wv)
            x = node_input + _merge(ps, pv)
            s2, v2 = _eq_ln(x, ln2_w0, ln2_b0, ln2_w1)
            a0 = node_attr[:, :1]
            fs, fv = _eq_lin(s2, v2, f1_ws, f1_bs, f1_wv)
            fs = fs * a0
            fv = fv * a0[:, :, None]
            sc = jax.nn.silu(fs[:, :M0])
            fv = fv * jax.nn.sigmoid(fs[:, M0:])[:, :, None]
            os_, ov = _eq_lin(sc, fv, f2_ws, f2_bs, f2_wv)
            os_ = os_ * a0
            ov = ov * a0[:, :, None]
            return x + _merge(os_, ov)
        key = jax.random.key(seed)
        ks = iter(jax.random.split(key, 24))

        def nrm(shape, fan):
            return jax.random.normal(next(ks), shape, jnp.float32) / np.float32(np.sqrt(fan))
        inp = {}
        inp['node_input'] = jax.random.normal(next(ks), (N, C0 + 3 * C1), jnp.float32)
        inp['node_attr'] = jnp.ones((N, 1), jnp.float32)
        inp['edge_vec'] = jax.random.normal(next(ks), (E, 3), jnp.float32)
        inp['edge_scalars'] = jax.random.uniform(next(ks), (E, NG), dtype=jnp.float32)
        inp['edge_src'] = jax.random.randint(next(ks), (E,), 0, N)
        inp['edge_dst'] = jax.random.randint(next(ks), (E,), 0, N)
        inp['ln1_w0'] = jnp.ones((C0,), jnp.float32)
        inp['ln1_b0'] = jnp.zeros((C0,), jnp.float32)
        inp['ln1_w1'] = jnp.ones((C1,), jnp.float32)
        inp['ln2_w0'] = jnp.ones((C0,), jnp.float32)
        inp['ln2_b0'] = jnp.zeros((C0,), jnp.float32)
        inp['ln2_w1'] = jnp.ones((C1,), jnp.float32)
        inp['msrc_ws'] = nrm((C0, C0), C0)
        inp['msrc_wv'] = nrm((C1, C1), C1)
        inp['mdst_ws'] = nrm((C0, C0), C0)
        inp['mdst_bs'] = jnp.zeros((C0,), jnp.float32)
        inp['mdst_wv'] = nrm((C1, C1), C1)
        inp['rw1'] = nrm((NG, RH), NG)
        inp['rb1'] = jnp.zeros((RH,), jnp.float32)
        inp['rg1'] = jnp.ones((RH,), jnp.float32)
        inp['rbe1'] = jnp.zeros((RH,), jnp.float32)
        inp['rw2'] = nrm((RH, RH), RH)
        inp['rb2'] = jnp.zeros((RH,), jnp.float32)
        inp['rg2'] = jnp.ones((RH,), jnp.float32)
        inp['rbe2'] = jnp.zeros((RH,), jnp.float32)
        inp['rw3'] = nrm((RH, WN), RH)
        inp['roff'] = 0.1 * jax.random.normal(next(ks), (WN,), jnp.float32)
        inp['lin_ws'] = nrm((DS, H * A + H * H0), DS)
        inp['lin_bs'] = jnp.zeros((H * A + H * H0,), jnp.float32)
        inp['lin_wv'] = nrm((DV, H * H1), DV)
        inp['alpha_dot'] = nrm((H, A), A)
        inp['proj_ws'] = nrm((H * H0, C0), H * H0)
        inp['proj_bs'] = jnp.zeros((C0,), jnp.float32)
        inp['proj_wv'] = nrm((H * H1, C1), H * H1)
        inp['f1_ws'] = nrm((C0, M0 + M1), C0)
        inp['f1_bs'] = jnp.zeros((M0 + M1,), jnp.float32)
        inp['f1_wv'] = nrm((C1, M1), C1)
        inp['f2_ws'] = nrm((M0, C0), M0)
        inp['f2_bs'] = jnp.zeros((C0,), jnp.float32)
        inp['f2_wv'] = nrm((M1, C1), M1)
        return inp
    _L1_gnn_all = _L1_gnn_setup()
    _L1_gnn_in = {k: v for k, v in _L1_gnn_all.items() if k in ('ln1_w0', 'ln1_b0', 'ln1_w1', 'ln2_w0', 'ln2_b0', 'ln2_w1', 'msrc_ws', 'msrc_wv', 'mdst_ws', 'mdst_bs', 'mdst_wv', 'rw1', 'rb1', 'rg1', 'rbe1', 'rw2', 'rb2', 'rg2', 'rbe2', 'rw3', 'roff', 'lin_ws', 'lin_bs', 'lin_wv', 'alpha_dot', 'proj_ws', 'proj_bs', 'proj_wv', 'f1_ws', 'f1_bs', 'f1_wv', 'f2_ws', 'f2_bs', 'f2_wv')}
    del _L1_gnn_all
    return {'x': x, 'src': src, 'dst': dst, 'edge_attr_16': edge_attr_16, 'edge_attr_3': edge_attr_3, 'edge_attr_4': edge_attr_4, 'edge_attr_64': edge_attr_64, 'node_vec1': node_vec1, 'L0_gnn_gamma_s': _L0_gnn_in['gamma_s'], 'L0_gnn_beta_s': _L0_gnn_in['beta_s'], 'L0_gnn_gamma_v': _L0_gnn_in['gamma_v'], 'L0_gnn_Ws_src': _L0_gnn_in['Ws_src'], 'L0_gnn_Wv_src': _L0_gnn_in['Wv_src'], 'L0_gnn_Ws_dst': _L0_gnn_in['Ws_dst'], 'L0_gnn_Wv_dst': _L0_gnn_in['Wv_dst'], 'L0_gnn_W_rbf': _L0_gnn_in['W_rbf'], 'L0_gnn_W_alpha': _L0_gnn_in['W_alpha'], 'L0_gnn_alpha_dot': _L0_gnn_in['alpha_dot'], 'L0_gnn_Ws_val': _L0_gnn_in['Ws_val'], 'L0_gnn_Wv_val': _L0_gnn_in['Wv_val'], 'L0_gnn_Wg': _L0_gnn_in['Wg'], 'L0_gnn_w2_ss': _L0_gnn_in['w2_ss'], 'L0_gnn_w2_sv': _L0_gnn_in['w2_sv'], 'L0_gnn_w2_vs': _L0_gnn_in['w2_vs'], 'L0_gnn_w2_vv0': _L0_gnn_in['w2_vv0'], 'L0_gnn_w2_vv1': _L0_gnn_in['w2_vv1'], 'L0_gnn_Ws_vlin': _L0_gnn_in['Ws_vlin'], 'L0_gnn_Wv_vlin': _L0_gnn_in['Wv_vlin'], 'L0_gnn_Wps': _L0_gnn_in['Wps'], 'L0_gnn_Wpv': _L0_gnn_in['Wpv'], 'L1_gnn_ln1_w0': _L1_gnn_in['ln1_w0'], 'L1_gnn_ln1_b0': _L1_gnn_in['ln1_b0'], 'L1_gnn_ln1_w1': _L1_gnn_in['ln1_w1'], 'L1_gnn_ln2_w0': _L1_gnn_in['ln2_w0'], 'L1_gnn_ln2_b0': _L1_gnn_in['ln2_b0'], 'L1_gnn_ln2_w1': _L1_gnn_in['ln2_w1'], 'L1_gnn_msrc_ws': _L1_gnn_in['msrc_ws'], 'L1_gnn_msrc_wv': _L1_gnn_in['msrc_wv'], 'L1_gnn_mdst_ws': _L1_gnn_in['mdst_ws'], 'L1_gnn_mdst_bs': _L1_gnn_in['mdst_bs'], 'L1_gnn_mdst_wv': _L1_gnn_in['mdst_wv'], 'L1_gnn_rw1': _L1_gnn_in['rw1'], 'L1_gnn_rb1': _L1_gnn_in['rb1'], 'L1_gnn_rg1': _L1_gnn_in['rg1'], 'L1_gnn_rbe1': _L1_gnn_in['rbe1'], 'L1_gnn_rw2': _L1_gnn_in['rw2'], 'L1_gnn_rb2': _L1_gnn_in['rb2'], 'L1_gnn_rg2': _L1_gnn_in['rg2'], 'L1_gnn_rbe2': _L1_gnn_in['rbe2'], 'L1_gnn_rw3': _L1_gnn_in['rw3'], 'L1_gnn_roff': _L1_gnn_in['roff'], 'L1_gnn_lin_ws': _L1_gnn_in['lin_ws'], 'L1_gnn_lin_bs': _L1_gnn_in['lin_bs'], 'L1_gnn_lin_wv': _L1_gnn_in['lin_wv'], 'L1_gnn_alpha_dot': _L1_gnn_in['alpha_dot'], 'L1_gnn_proj_ws': _L1_gnn_in['proj_ws'], 'L1_gnn_proj_bs': _L1_gnn_in['proj_bs'], 'L1_gnn_proj_wv': _L1_gnn_in['proj_wv'], 'L1_gnn_f1_ws': _L1_gnn_in['f1_ws'], 'L1_gnn_f1_bs': _L1_gnn_in['f1_bs'], 'L1_gnn_f1_wv': _L1_gnn_in['f1_wv'], 'L1_gnn_f2_ws': _L1_gnn_in['f2_ws'], 'L1_gnn_f2_bs': _L1_gnn_in['f2_bs'], 'L1_gnn_f2_wv': _L1_gnn_in['f2_wv']}

def reference(x, src, dst, edge_attr_16, edge_attr_3, edge_attr_4, edge_attr_64, node_vec1, L0_gnn_gamma_s, L0_gnn_beta_s, L0_gnn_gamma_v, L0_gnn_Ws_src, L0_gnn_Wv_src, L0_gnn_Ws_dst, L0_gnn_Wv_dst, L0_gnn_W_rbf, L0_gnn_W_alpha, L0_gnn_alpha_dot, L0_gnn_Ws_val, L0_gnn_Wv_val, L0_gnn_Wg, L0_gnn_w2_ss, L0_gnn_w2_sv, L0_gnn_w2_vs, L0_gnn_w2_vv0, L0_gnn_w2_vv1, L0_gnn_Ws_vlin, L0_gnn_Wv_vlin, L0_gnn_Wps, L0_gnn_Wpv, L1_gnn_ln1_w0, L1_gnn_ln1_b0, L1_gnn_ln1_w1, L1_gnn_ln2_w0, L1_gnn_ln2_b0, L1_gnn_ln2_w1, L1_gnn_msrc_ws, L1_gnn_msrc_wv, L1_gnn_mdst_ws, L1_gnn_mdst_bs, L1_gnn_mdst_wv, L1_gnn_rw1, L1_gnn_rb1, L1_gnn_rg1, L1_gnn_rbe1, L1_gnn_rw2, L1_gnn_rb2, L1_gnn_rg2, L1_gnn_rbe2, L1_gnn_rw3, L1_gnn_roff, L1_gnn_lin_ws, L1_gnn_lin_bs, L1_gnn_lin_wv, L1_gnn_alpha_dot, L1_gnn_proj_ws, L1_gnn_proj_bs, L1_gnn_proj_wv, L1_gnn_f1_ws, L1_gnn_f1_bs, L1_gnn_f1_wv, L1_gnn_f2_ws, L1_gnn_f2_bs, L1_gnn_f2_wv):
    import jax
    import jax.numpy as jnp

    def _L0_gnn_ref(node, rbf, rsh, gamma_s, beta_s, gamma_v, Ws_src, Wv_src, Ws_dst, Wv_dst, W_rbf, W_alpha, alpha_dot, Ws_val, Wv_val, Wg, w2_ss, w2_sv, w2_vs, w2_vv0, w2_vv1, Ws_vlin, Wv_vlin, Wps, Wpv, edge_index):
        import jax, jax.numpy as jnp
        import numpy as np
        N, E = (625, 10000)
        CS, CV = (64, 32)
        AS_, AV, H = (16, 8, 4)
        NB = 16
        SQRT3 = 1.7320508075688772
        SQRT2 = 1.4142135623730951
        EPS = 1e-05

        def _cg_tp(s, v, y0, y1, w_ss, w_sv, w_vs, w_vv0, w_vv1):
            out_s = jnp.concatenate([w_ss * s * y0[:, None], w_vv0 * (jnp.einsum('eci,ei->ec', v, y1) / SQRT3)], axis=-1)
            out_v = jnp.concatenate([(w_sv * s)[:, :, None] * y1[:, None, :], (w_vs * jnp.ones_like(v[..., 0]))[..., None] * v * y0[:, None, None], (w_vv1 * jnp.ones_like(v[..., 0]))[..., None] * (jnp.cross(v, y1[:, None, :]) / SQRT2)], axis=1)
            return (out_s, out_v)

        def _equiv_layernorm(s, v, gamma_s, beta_s, gamma_v):
            mu = jnp.mean(s, axis=-1, keepdims=True)
            var = jnp.var(s, axis=-1, keepdims=True)
            s_n = (s - mu) * jax.lax.rsqrt(var + EPS) * gamma_s + beta_s
            rms = jnp.sqrt(jnp.mean(jnp.sum(v * v, axis=-1), axis=-1, keepdims=True) + EPS)
            v_n = v / rms[..., None] * gamma_v[None, :, None]
            return (s_n, v_n)
        n = node.shape[0]
        e = rsh.shape[0]
        s = node[:, :CS]
        v = node[:, CS:].reshape(n, CV, 3)
        s_n, v_n = _equiv_layernorm(s, v, gamma_s, beta_s, gamma_v)
        src, dst = (edge_index[0], edge_index[1])
        msg_s = (s_n @ Ws_src)[src] + (s_n @ Ws_dst)[dst]
        msg_v = jnp.einsum('ncx,cd->ndx', v_n, Wv_src)[src] + jnp.einsum('ncx,cd->ndx', v_n, Wv_dst)[dst]
        y0, y1 = (rsh[:, 0], rsh[:, 1:4])
        w1 = rbf @ W_rbf
        m1_s, m1_v = _cg_tp(msg_s, msg_v, y0, y1, w1[:, :CS], w1[:, CS:2 * CS], w1[:, 2 * CS:2 * CS + CV], w1[:, 2 * CS + CV:2 * CS + 2 * CV], w1[:, 2 * CS + 2 * CV:])
        a = (m1_s @ W_alpha).reshape(e, H, AS_)
        a = jnp.where(a > 0, a, 0.2 * a)
        a = jnp.sum(a * alpha_dot, axis=-1, keepdims=True)
        amax = jax.ops.segment_max(a, dst, num_segments=n)
        amax = jnp.where(jnp.isfinite(amax), amax, 0.0)
        ex = jnp.exp(a - amax[dst])
        den = jax.ops.segment_sum(ex, dst, num_segments=n)
        alpha = ex / (den[dst] + 1e-16)
        val_s = m1_s @ Ws_val
        val_v = jnp.einsum('ecx,cd->edx', m1_v, Wv_val)
        val_v = val_v * jax.nn.sigmoid(val_s @ Wg)[..., None]
        val_s = jax.nn.sigmoid(val_s)
        m2_s, m2_v = _cg_tp(val_s, val_v, y0, y1, w2_ss, w2_sv, w2_vs, w2_vv0, w2_vv1)
        hs = (m2_s @ Ws_vlin).reshape(e, H, AS_)
        hv = jnp.einsum('ecx,cd->edx', m2_v, Wv_vlin).reshape(e, H, AV, 3)
        h = jnp.concatenate([hs, hv.reshape(e, H, AV * 3)], axis=-1)
        agg = jax.ops.segment_sum(alpha * h, dst, num_segments=n)
        agg_s = agg[:, :, :AS_].reshape(n, H * AS_)
        agg_v = agg[:, :, AS_:].reshape(n, H * AV, 3)
        out = node + jnp.concatenate([agg_s @ Wps, jnp.einsum('ncx,cd->ndx', agg_v, Wpv).reshape(n, CV * 3)], axis=-1)
        return out

    def _L1_gnn_ref(node_input, node_attr, edge_vec, edge_scalars, edge_src, edge_dst, ln1_w0, ln1_b0, ln1_w1, ln2_w0, ln2_b0, ln2_w1, msrc_ws, msrc_wv, mdst_ws, mdst_bs, mdst_wv, rw1, rb1, rg1, rbe1, rw2, rb2, rg2, rbe2, rw3, roff, lin_ws, lin_bs, lin_wv, alpha_dot, proj_ws, proj_bs, proj_wv, f1_ws, f1_bs, f1_wv, f2_ws, f2_bs, f2_wv):
        import jax, jax.numpy as jnp
        import numpy as np
        N, E = (10000, 5000)
        C0, C1 = (64, 32)
        H, A = (8, 8)
        H0, H1 = (8, 4)
        M0, M1 = (128, 64)
        NG, RH = (64, 64)
        WN = C0 + C0 + C1 + C1 + C1
        DS, DV = (C0 + C1, C0 + 2 * C1)
        EPS = 1e-05
        SQ3 = np.float32(np.sqrt(3.0))
        SQ2 = np.float32(np.sqrt(2.0))

        def _split(x):
            return (x[:, :C0], x[:, C0:].reshape(x.shape[0], C1, 3))

        def _merge(s, v):
            return jnp.concatenate([s, v.reshape(v.shape[0], -1)], axis=1)

        def _eq_ln(x, w0, b0, w1):
            s, v = _split(x)
            s = s - s.mean(axis=1, keepdims=True)
            s = s * jax.lax.rsqrt(jnp.square(s).mean(axis=1, keepdims=True) + EPS) * w0 + b0
            v = v * jax.lax.rsqrt(jnp.square(v).mean(axis=(1, 2), keepdims=True) + EPS) * w1[None, :, None]
            return (s, v)

        def _eq_lin(s, v, ws, bs, wv):
            return (s @ ws + bs, jnp.einsum('nud,uk->nkd', v, wv))

        def _ln(x, g, b):
            xc = x - x.mean(-1, keepdims=True)
            return xc * jax.lax.rsqrt(jnp.square(xc).mean(-1, keepdims=True) + EPS) * g + b

        def _smooth_leaky(x, alpha=0.2):
            return 0.5 * (1 + alpha) * x + 0.5 * (1 - alpha) * x * (2.0 * jax.nn.sigmoid(x) - 1.0)

        def _forward(node_input, node_attr, edge_vec, edge_scalars, edge_src, edge_dst, ln1_w0, ln1_b0, ln1_w1, ln2_w0, ln2_b0, ln2_w1, msrc_ws, msrc_wv, mdst_ws, mdst_bs, mdst_wv, rw1, rb1, rg1, rbe1, rw2, rb2, rg2, rbe2, rw3, roff, lin_ws, lin_bs, lin_wv, alpha_dot, proj_ws, proj_bs, proj_wv, f1_ws, f1_bs, f1_wv, f2_ws, f2_bs, f2_wv):
            n = node_input.shape[0]
            s, v = _eq_ln(node_input, ln1_w0, ln1_b0, ln1_w1)
            src_s = s @ msrc_ws
            src_v = jnp.einsum('nud,uk->nkd', v, msrc_wv)
            dst_s = s @ mdst_ws + mdst_bs
            dst_v = jnp.einsum('nud,uk->nkd', v, mdst_wv)
            ms = src_s[edge_src] + dst_s[edge_dst]
            mv = src_v[edge_src] + dst_v[edge_dst]
            h = jax.nn.silu(_ln(edge_scalars @ rw1 + rb1, rg1, rbe1))
            h = jax.nn.silu(_ln(h @ rw2 + rb2, rg2, rbe2))
            w = h @ rw3 + roff
            rhat = edge_vec * jax.lax.rsqrt(jnp.sum(jnp.square(edge_vec), -1, keepdims=True) + 1e-12)
            Y1 = SQ3 * rhat
            w1, w2, w3, w4, w5 = jnp.split(w, [C0, 2 * C0, 2 * C0 + C1, 2 * C0 + 2 * C1], axis=1)
            o0a = w1 * ms
            o0b = w4 * (jnp.einsum('eud,ed->eu', mv, Y1) / SQ3)
            o1a = (w2 * ms)[:, :, None] * Y1[:, None, :]
            o1b = w3[:, :, None] * mv
            o1c = w5[:, :, None] * (jnp.cross(mv, Y1[:, None, :]) / SQ2)
            ds = jnp.concatenate([o0a, o0b], axis=1)
            dv = jnp.concatenate([o1a, o1b, o1c], axis=1)
            ls, lv = _eq_lin(ds, dv, lin_ws, lin_bs, lin_wv)
            e = ls.shape[0]
            alpha = ls[:, :H * A].reshape(e, H, A)
            vs = ls[:, H * A:].reshape(e, H, H0)
            vv = lv.reshape(e, H, H1, 3)
            a = jnp.einsum('ehk,hk->eh', _smooth_leaky(alpha), alpha_dot)
            amax = jax.lax.stop_gradient(jax.ops.segment_max(a, edge_dst, num_segments=n))
            a = jnp.exp(a - amax[edge_dst])
            a = a / (jax.ops.segment_sum(a, edge_dst, num_segments=n)[edge_dst] + 1e-12)
            ns = jax.ops.segment_sum(vs * a[..., None], edge_dst, num_segments=n).reshape(n, H * H0)
            nv = jax.ops.segment_sum(vv * a[..., None, None], edge_dst, num_segments=n).reshape(n, H * H1, 3)
            ps, pv = _eq_lin(ns, nv, proj_ws, proj_bs, proj_wv)
            x = node_input + _merge(ps, pv)
            s2, v2 = _eq_ln(x, ln2_w0, ln2_b0, ln2_w1)
            a0 = node_attr[:, :1]
            fs, fv = _eq_lin(s2, v2, f1_ws, f1_bs, f1_wv)
            fs = fs * a0
            fv = fv * a0[:, :, None]
            sc = jax.nn.silu(fs[:, :M0])
            fv = fv * jax.nn.sigmoid(fs[:, M0:])[:, :, None]
            os_, ov = _eq_lin(sc, fv, f2_ws, f2_bs, f2_wv)
            os_ = os_ * a0
            ov = ov * a0[:, :, None]
            return x + _merge(os_, ov)
        return _forward(node_input, node_attr, edge_vec, edge_scalars, edge_src, edge_dst, ln1_w0, ln1_b0, ln1_w1, ln2_w0, ln2_b0, ln2_w1, msrc_ws, msrc_wv, mdst_ws, mdst_bs, mdst_wv, rw1, rb1, rg1, rbe1, rw2, rb2, rg2, rbe2, rw3, roff, lin_ws, lin_bs, lin_wv, alpha_dot, proj_ws, proj_bs, proj_wv, f1_ws, f1_bs, f1_wv, f2_ws, f2_bs, f2_wv)
    edge_index = jnp.stack([src, dst])
    h = jnp.maximum(_layernorm(x, axis=-1), 0.0)
    x = x + _L0_gnn_ref(h, edge_attr_16, edge_attr_4, L0_gnn_gamma_s, L0_gnn_beta_s, L0_gnn_gamma_v, L0_gnn_Ws_src, L0_gnn_Wv_src, L0_gnn_Ws_dst, L0_gnn_Wv_dst, L0_gnn_W_rbf, L0_gnn_W_alpha, L0_gnn_alpha_dot, L0_gnn_Ws_val, L0_gnn_Wv_val, L0_gnn_Wg, L0_gnn_w2_ss, L0_gnn_w2_sv, L0_gnn_w2_vs, L0_gnn_w2_vv0, L0_gnn_w2_vv1, L0_gnn_Ws_vlin, L0_gnn_Wv_vlin, L0_gnn_Wps, L0_gnn_Wpv, edge_index)
    h = jnp.maximum(_layernorm(x, axis=-1), 0.0)
    x = x + _L1_gnn_ref(h, node_vec1, edge_attr_3, edge_attr_64, src, dst, L1_gnn_ln1_w0, L1_gnn_ln1_b0, L1_gnn_ln1_w1, L1_gnn_ln2_w0, L1_gnn_ln2_b0, L1_gnn_ln2_w1, L1_gnn_msrc_ws, L1_gnn_msrc_wv, L1_gnn_mdst_ws, L1_gnn_mdst_bs, L1_gnn_mdst_wv, L1_gnn_rw1, L1_gnn_rb1, L1_gnn_rg1, L1_gnn_rbe1, L1_gnn_rw2, L1_gnn_rb2, L1_gnn_rg2, L1_gnn_rbe2, L1_gnn_rw3, L1_gnn_roff, L1_gnn_lin_ws, L1_gnn_lin_bs, L1_gnn_lin_wv, L1_gnn_alpha_dot, L1_gnn_proj_ws, L1_gnn_proj_bs, L1_gnn_proj_wv, L1_gnn_f1_ws, L1_gnn_f1_bs, L1_gnn_f1_wv, L1_gnn_f2_ws, L1_gnn_f2_bs, L1_gnn_f2_wv)
    return x

_drawn_inputs = setup_inputs


def setup_inputs(seed=0):
    import zlib

    import numpy as np

    out = dict(_drawn_inputs(seed))
    spreads = {'L0_gnn_gamma_s': (1.0, 0.6),
     'L0_gnn_beta_s': (0.0, 0.8),
     'L0_gnn_gamma_v': (1.0, 0.6),
     'L1_gnn_ln1_w0': (1.0, 0.547),
     'L1_gnn_ln1_b0': (0.0, 0.425),
     'L1_gnn_ln1_w1': (1.0, 0.2),
     'L1_gnn_ln2_w0': (1.0, 0.6),
     'L1_gnn_ln2_b0': (0.0, 0.8),
     'L1_gnn_ln2_w1': (1.0, 0.6),
     'L1_gnn_mdst_bs': (0.0, 0.531),
     'L1_gnn_rb1': (0.0, 0.1),
     'L1_gnn_rg1': (1.0, 0.2),
     'L1_gnn_rbe1': (0.0, 0.335),
     'L1_gnn_rb2': (0.0, 0.1),
     'L1_gnn_rg2': (1.0, 0.2),
     'L1_gnn_rbe2': (0.0, 0.307),
     'L1_gnn_lin_bs': (0.0, 0.506),
     'L1_gnn_proj_bs': (0.0, 0.303),
     'L1_gnn_f1_bs': (0.0, 0.8),
     'L1_gnn_f2_bs': (0.0, 0.491)}
    factors = {'L0_gnn_W_alpha': 2.877, 'L0_gnn_alpha_dot': 2.796}
    for name, (base, spread) in spreads.items():
        noise = np.random.default_rng([zlib.crc32(name.encode()), seed]).standard_normal(out[name].shape)
        drawn = base * np.exp(spread * noise) if base else spread * noise
        out[name] = jnp.asarray(drawn.astype(out[name].dtype))
    for name, factor in factors.items():
        out[name] = (out[name] * factor).astype(out[name].dtype)
    return out
```

```python
from contextlib import ExitStack

import numpy as np

import concourse.bass as bass
from concourse import mybir

F32 = mybir.dt.float32
I32 = mybir.dt.int32
U32 = mybir.dt.uint32
ALU = mybir.AluOpType
ACT = mybir.ActivationFunctionType
AX_X = mybir.AxisListType.X

P = 128
C0, C1 = 64, 32
CV = 3 * C1
D = C0 + CV
WN = 2 * C0 + 3 * C1
EG = 4
NG = 8
FG = 4
RING = 2
EPS = 1e-5
BIG = 1e30
SKIP = 1e6
SQRT3 = float(np.sqrt(3.0))
SQRT2 = float(np.sqrt(2.0))
RSQRT_SEED = 1597463007.0
M0, M1 = 128, 64


W0 = dict(in0=(P, D), in1=(P, D), in2=(64, D), beta0=(P, 1), beta1=(P, 1), beta2=(64, 1), gam0=(P, 1),
          gam1=(P, 1), gam2=(64, 1), rad=(16, WN), first=(P, C1 + 160), second=(P, 160 + CV), third=(CV, CV), svT=(C0, P), wg=(C0, C1),
          out0=(P, 160), out0s=(C0, C0 + C1), dots=(P, 1), out1=(CV, 2 * CV), b2s=(CV, 1), c2s=(CV, 1), p0=(P, D), p1=(32, D), dot=(P, C0))
W1 = dict(in0=(P, D), in1=(P, D), in2=(64, D), beta0=(P, 1), beta1=(P, 1), beta2=(64, 1), gam0=(P, 1),
          gam1=(P, 1), gam2=(64, 1), mbias=(1, D), r1=(65, 64), r2=(65, 64), rad=(65, WN), rg1=(64, 1),
          rbe1=(64, 1), rg2=(64, 1), rbe2=(64, 1), first=(P, C1 + P), second=(P, P + CV), third=(CV, CV), sbias=(1, P),
          p0=(P, D), p1=(32, D), dot=(P, C0), fill=(P, D))
W2 = dict(s=(65, 256), gs=(65, 1), b0=(65, 65), v0=(CV, 128), v1=(CV, 64), gv=(CV, 1), o=(M0, C0),
          ov0=(P, CV), ov1=(65, D))
W_ALL = dict(ident=(P, P), low=(P, P))


def offsets(table):
    at, out = 0, {}
    for name, (rows, cols) in table.items():
        out[name] = (at, rows, cols)
        at += cols
    return out, at


def views(tile, table):
    return {n: tile[0:r, a:a + c] for n, (a, r, c) in offsets(table)[0].items()}


class Tick:

    def __init__(self, eng, sem, step=0, per_step=0, before=0):
        self.eng, self.sem, self.step, self.per_step, self.before = eng, sem, step, per_step, before
        self.n = 0

    def mark(self, instruction):
        instruction.then_inc(self.sem, 1)
        self.n += 1
        return self.n

    def wait(self, n):
        self.eng.wait_ge(self.sem, self.step * self.per_step + (self.before + n))

    def link(self, instruction):
        self.wait(self.mark(instruction))

    def done(self):
        self.wait(self.n)

    def close(self):
        assert self.n == self.per_step, (self.n, self.per_step)


def spread(ap, shape):
    return ap.to_broadcast(shape)


def moments(nc, t, stats, n, mean, var, tmp):
    last = None
    a = t.mark(nc.vector.tensor_tensor(tmp[0], stats[:, :, 1], stats[:, :, 4], ALU.subtract))
    b = t.mark(nc.vector.tensor_tensor(tmp[1], stats[:, :, 2], stats[:, :, 5], ALU.add))
    c = t.mark(nc.vector.tensor_tensor(mean, stats[:, :, 1], stats[:, :, 4], ALU.add))
    t.wait(a)
    d = t.mark(nc.vector.scalar_tensor_tensor(tmp[2], tmp[0], 0.25, tmp[0], ALU.mult, ALU.mult))
    t.wait(c)
    t.mark(nc.vector.tensor_scalar(mean, mean, 0.5, None, ALU.mult))
    if not isinstance(n, int):
        t.link(nc.vector.tensor_tensor(tmp[1], tmp[1], n, ALU.mult))
        return t.mark(nc.vector.tensor_tensor(var, tmp[1], tmp[2], ALU.add))
    t.wait(d)
    last = t.mark(nc.vector.scalar_tensor_tensor(var, tmp[1], 1.0 / n, tmp[2], ALU.mult, ALU.add))
    return last


MOMENTS = 6


def rsqrt(nc, t, y, v, tmp, ready, between=None, count=FG):
    at = 0

    def link(instruction):
        nonlocal at
        n = t.mark(instruction)
        if between and at < count:
            between(at)
            at += 1
        t.wait(n)

    link(nc.vector.tensor_scalar(y.bitcast(I32), v.bitcast(I32), -0.5, RSQRT_SEED, ALU.mult, ALU.add))
    for n in range(3):
        link(nc.vector.tensor_tensor(tmp, y, y, ALU.mult))
        link(nc.vector.scalar_tensor_tensor(tmp, tmp, -0.5, v, ALU.mult, ALU.mult))
        step = nc.vector.scalar_tensor_tensor(y, tmp, 1.5, y, ALU.add, ALU.mult)
        if n < 2:
            link(step)
    step.then_inc(ready, 1)


RSQRT = 9


def prepare(nc, io, w, flags, T):
    with ExitStack() as ctx:
        sem = lambda n: ctx.enter_context(nc.semaphore(n))
        loaded, vec, pe_done = sem("prep_loaded"), sem("prep_vec"), sem("prep_pe")
        ps = ctx.enter_context(nc.psum_tensor("prep_ps", [P, 3, 512], F32))
        dstf = ctx.enter_context(nc.sbuf_tensor("dstf", [P, T], F32))
        end = ctx.enter_context(nc.sbuf_tensor("endf", [P, T], F32))
        a, b, c = w["l0"], w["l1"], w["ff"]
        N_IN = 16 * 7
        with nc.Block() as block:
            @block.sync
            def _(sp):
                sp.dma_start(w["t_all"], io["w_all"]).then_inc(loaded, 16)
                sp.dma_start(w["t_l0"], io["w_l0"]).then_inc(loaded, 16)
                sp.dma_start(w["t_l1"], io["w_l1"]).then_inc(loaded, 16)
                sp.dma_start(w["t_ff"], io["w_ff"]).then_inc(loaded, 16)
                sp.dma_start(flags["src"][:, 0:T], io["src"]).then_inc(loaded, 16)
                sp.dma_start(flags["dst"][:, 0:T], io["dst"]).then_inc(loaded, 16)
                sp.dma_start(flags["y0"][:], io["attr4"]).then_inc(loaded, 16)

            @block.tensor
            def _(pe):
                pe.wait_ge(loaded, N_IN)
                for n, l in enumerate((a, b)):
                    for k in range(3):
                        last = nc.tensor.matmul(ps[0:1, n, 0:D], l[f"beta{k}"], l[f"in{k}"], start=(k == 0), stop=(k == 2))
                last.then_inc(pe_done, 1)
                nc.tensor.matmul(ps[:, 2, 0:C1], a["svT"], a["wg"], start=True, stop=True).then_inc(pe_done, 1)
                pe.wait_ge(vec, 2)
                nc.tensor.matmul(ps[0:65, 0, 0:256], c["b0"], c["s"], start=True, stop=True).then_inc(pe_done, 1)

            @block.vector
            def _(dve):
                t = Tick(dve, vec, 0, 0)
                v = nc.vector
                dve.wait_ge(loaded, N_IN)
                dve.wait_ge(pe_done, 1)
                t.mark(v.tensor_copy(w["mrow0"], ps[0:1, 0, 0:D]))
                t.mark(v.tensor_tensor(w["mrow1"], ps[0:1, 1, 0:D], b["mbias"], ALU.add))
                for l in (a, b):
                    for k in range(3):
                        t.mark(v.tensor_scalar(l[f"in{k}"], l[f"in{k}"], l[f"gam{k}"], None, ALU.mult))
                dve.wait_ge(pe_done, 2)
                t.mark(v.tensor_copy(a["first"][0:64, C1 + 128:], ps[0:64, 2, 0:C1]))
                t.link(v.tensor_copy(a["second"][96:128, 128:160], ps[96:128, 2, 0:C1]))
                m = a["second"][96:128, 0:160]
                t.mark(v.tensor_scalar(m, m, 1.0 / SQRT3, None, ALU.mult))
                t.mark(v.tensor_scalar(a["third"], a["third"], 1.0 / SQRT2, None, ALU.mult))
                m = a["out0"][0:64, 0:C0 + C1]
                t.mark(v.tensor_tensor(m, m, a["out0s"], ALU.mult))
                m = a["out0"][96:128, C0 + C1:]
                t.mark(v.tensor_scalar(m, m, a["dots"][96:128], 1.0 / SQRT3, ALU.mult, ALU.mult))
                m = a["out1"][:, 0:CV]
                t.mark(v.tensor_scalar(m, m, a["b2s"], None, ALU.mult))
                m = a["out1"][:, CV:]
                t.mark(v.tensor_scalar(m, m, a["c2s"], 1.0 / SQRT2, ALU.mult, ALU.mult))
                m = b["first"][64:128, 0:C1]
                t.mark(v.tensor_scalar(m, m, SQRT3, None, ALU.mult))
                t.mark(v.tensor_scalar(b["third"], b["third"], SQRT3 / SQRT2, None, ALU.mult))
                t.mark(v.tensor_scalar(b["dot"], b["dot"], 0.4, None, ALU.mult))
                dve.wait_ge(pe_done, 3)
                t.mark(v.tensor_scalar(c["s"][0:64], c["s"][0:64], c["gs"][0:64], None, ALU.mult))
                t.mark(v.tensor_copy(c["s"][64:65], ps[64:65, 0, 0:256]))
                t.mark(v.tensor_scalar(c["v0"], c["v0"], c["gv"], None, ALU.mult))
                t.mark(v.tensor_scalar(c["v1"], c["v1"], c["gv"], None, ALU.mult))
                t.mark(v.tensor_scalar(c["ov0"], c["ov0"], 0.5, None, ALU.mult))
                t.mark(v.tensor_scalar(c["ov1"][0:64], c["ov1"][0:64], 0.5, None, ALU.mult))
                d, src = flags["dst"], flags["src"]
                t.mark(v.memset(d[:, T:T + EG], 0))
                t.mark(v.memset(src[:, T:T + EG], 0))
                t.mark(v.memset(flags["same"][:, 0:1], 0.0))
                t.mark(v.memset(flags["nxt"][:, T - 1:T], 0.0))
                t.link(v.tensor_copy(dstf[:], d[:, 0:T]))
                t.mark(v.tensor_tensor(flags["same"][:, 1:T], dstf[:, 1:T], dstf[:, 0:T - 1], ALU.is_equal))
                t.mark(v.tensor_tensor(flags["nxt"][:, 0:T - 1], dstf[:, 1:T], dstf[:, 0:T - 1], ALU.is_equal))
                t.mark(v.tensor_scalar(flags["first"][:], dstf[:], dstf[:, 0:1], None, ALU.is_equal))
                t.link(v.tensor_scalar(flags["last"][:], dstf[:], dstf[:, T - 1:T], None, ALU.is_equal))
                t.link(v.tensor_tensor(flags["mid"][:], flags["first"][:], flags["last"][:], ALU.max))
                t.link(v.tensor_scalar(flags["mid"][:], flags["mid"][:], -1.0, 1.0, ALU.mult, ALU.add))
                t.link(v.tensor_tensor(end[:], flags["first"][:], flags["last"][:], ALU.mult))
                t.link(v.tensor_tensor(flags["last"][:], flags["last"][:], end[:], ALU.subtract))
                t.link(v.tensor_scalar(end[:], flags["nxt"][:], SKIP, None, ALU.mult))
                t.link(v.memset(end[:, T - 1:T], SKIP))
                t.link(v.tensor_tensor(flags["row"][:, 0:T], end[:], dstf[:], ALU.add))
                t.mark(v.tensor_copy(flags["tail"][:], dstf[:, T - 1:T]))
                t.mark(v.tensor_copy(flags["head"][:], dstf[:, 0:1]))
                t.mark(v.memset(flags["ones"][:], 1.0))


def nodes(nc, io, w, N_STEPS):
    with ExitStack() as ctx:
        sb = lambda n, s: ctx.enter_context(nc.sbuf_tensor(n, s, F32))
        sem = lambda n: ctx.enter_context(nc.semaphore(n))
        x = sb("n_x", [P, 2, NG, D])
        u = sb("n_u", [P, NG, D])
        x1 = sb("n_x1", [P, NG, D])
        g = sb("n_g", [P, NG, D])
        fill = sb("n_fill", [P, NG, D])
        stats = sb("n_stats", [P, NG, 6])
        stat2 = sb("n_stat2", [P, 2, NG, 6])
        mean, negm, var = sb("n_mean", [P, NG]), sb("n_negm", [P, NG]), sb("n_var", [P, NG])
        mean2, var2 = sb("n_mean2", [P, NG]), sb("n_var2", [P, NG])
        mean3, var3 = sb("n_mean3", [P, NG]), sb("n_var3", [P, NG])
        e = sb("n_e", [P, 3, NG])
        r = sb("n_r", [P, 3, NG])
        tmp = sb("n_tmp", [P, 4, 3 * NG])
        x_in = [sem("n_x_in0"), sem("n_x_in1")]
        vec, filled, fill_out = sem("n_vec"), sem("n_filled"), sem("n_fill_out")
        negm_ready, u_ready, gv_ready = sem("n_negm_ready"), sem("n_u_ready"), sem("n_gv_ready")
        r_ready, out_ready = sem("n_r_ready"), sem("n_out_ready")
        x1_out, g_out = sem("n_x1_out"), sem("n_g_out")
        grp = lambda a: a.rearrange("(g p j) c -> g p j c", p=P, j=NG)
        xs, x1s, gs, aggs = grp(io["x"]), grp(io["x1"]), grp(io["g"]), grp(io["agg"])
        STEP = NG + MOMENTS + 1 + 2 * NG + 2 * MOMENTS + 5 + RSQRT
        PAIRS = N_STEPS // 2
        ODD = N_STEPS % 2
        tmps = lambda k: [tmp[:, i, 0:k] for i in range(4)]

        with nc.Block() as block:
            @block.sync
            def _(sp):
                def load(step, b):
                    sp.dma_start(x[:, b], xs[step]).then_inc(x_in[b], 16)

                def store(step):
                    sp.wait_ge(out_ready, step + 1)
                    sp.dma_start(x1s[step], x1[:]).then_inc(x1_out, 16)
                    sp.wait_ge(gv_ready, step + 1)
                    sp.dma_start(gs[step], g[:]).then_inc(g_out, 16)
                    sp.dma_start(aggs[step], fill[:]).then_inc(fill_out, 16)

                load(0, 0)
                load(1, 1)
                sp.wait_ge(filled, NG)
                with sp.Fori(0, PAIRS - 1) as i:
                    for b in range(2):
                        store(2 * i + b)
                        load(2 * i + b + 2, b)
                store(2 * PAIRS - 2)
                if ODD:
                    load(2 * PAIRS, 0)
                store(2 * PAIRS - 1)
                if ODD:
                    store(2 * PAIRS)
                sp.wait_ge(x1_out, 16 * N_STEPS)
                sp.wait_ge(g_out, 16 * N_STEPS)
                sp.wait_ge(fill_out, 16 * N_STEPS)

            def act_step(act, step, b):
                act.wait_ge(gv_ready, step)
                act.wait_ge(negm_ready, step + 1)
                for j in range(NG):
                    k = nc.scalar.activation(u[:, j], x[:, b, j], ACT.Relu, bias=negm[:, j:j + 1])
                    k.then_inc(u_ready, 1)
                act.wait_ge(r_ready, step + 1)
                act.wait_ge(g_out, 16 * step)
                for j in range(NG):
                    k = nc.scalar.activation(g[:, j, C0:D], u[:, j, C0:D], ACT.Copy, scale=r[:, 2, j:j + 1])
                k.then_inc(gv_ready, 1)

            def dve_step(dve, step, b, half):
                v = nc.vector
                t = Tick(dve, vec, step, STEP)
                dve.wait_ge(out_ready, step)
                dve.wait_ge(x_in[b], 16 * half + 16)
                for j in range(NG):
                    k = t.mark(v.bn_stats(stats[:, j], x[:, b, j]))
                t.wait(k)
                k = moments(nc, t, stats[:], D, mean[:], var[:], tmps(NG))
                t.wait(k)
                t.mark(v.tensor_scalar(e[:, 0], var[:], EPS, None, ALU.add))
                v.tensor_scalar(negm[:], mean[:], -1.0, None, ALU.mult).then_inc(negm_ready, 1)
                for j in range(NG):
                    dve.wait_ge(u_ready, NG * step + j + 1)
                    t.mark(v.bn_stats(stat2[:, 0, j], u[:, j, 0:C0]))
                    k = t.mark(v.bn_stats(stat2[:, 1, j], u[:, j, C0:D]))
                t.wait(k)
                moments(nc, t, stat2[:, 0], C0, mean2[:], var2[:], tmps(NG))
                k = moments(nc, t, stat2[:, 1], CV, mean3[:], var3[:], [tmp[:, i, NG:2 * NG] for i in range(4)])
                t.wait(k)
                t.link(v.tensor_tensor(tmp[:, 3, 0:NG], mean3[:], mean3[:], ALU.mult))
                t.mark(v.scalar_tensor_tensor(e[:, 1], e[:, 0], EPS, var2[:], ALU.mult, ALU.add))
                t.mark(v.tensor_scalar(e[:, 2], e[:, 0], EPS, None, ALU.mult))
                t.link(v.tensor_tensor(tmp[:, 3, 0:NG], tmp[:, 3, 0:NG], var3[:], ALU.add))
                t.link(v.scalar_tensor_tensor(e[:, 2], tmp[:, 3, 0:NG], 3.0, e[:, 2], ALU.mult, ALU.add))
                flat = lambda a: a.rearrange("p a b -> p (a b)")
                rsqrt(nc, t, flat(r[:]), flat(e[:]), tmp[:, 0], r_ready)
                t.close()
                dve.wait_ge(r_ready, step + 1)
                dve.wait_ge(x1_out, 16 * step)
                for j in range(NG):
                    v.scalar_tensor_tensor(x1[:, j], u[:, j], r[:, 0, j:j + 1], x[:, b, j], ALU.mult, ALU.add)
                dve.wait_ge(g_out, 16 * step)
                for j in range(NG):
                    k = v.tensor_scalar(g[:, j, 0:C0], u[:, j, 0:C0], mean2[:, j:j + 1], r[:, 1, j:j + 1],
                                        ALU.subtract, ALU.mult)
                k.then_inc(out_ready, 1)

            @block.scalar
            def _(act):
                with act.Fori(0, PAIRS) as i:
                    for b in range(2):
                        act_step(act, 2 * i + b, b)
                if ODD:
                    act_step(act, N_STEPS - 1, 0)

            @block.vector
            def _(dve):
                for j in range(NG):
                    nc.vector.tensor_copy(fill[:, j], w["l1"]["fill"]).then_inc(filled, 1)
                with dve.Fori(0, PAIRS) as i:
                    for b in range(2):
                        dve_step(dve, 2 * i + b, b, i)
                if ODD:
                    dve_step(dve, N_STEPS - 1, 0, PAIRS)


def edges(nc, io, w, flags, T, layer, vals, logits):
    H = (4, 8)[layer]
    SW, VW = C0 // H, C1 // H
    STEPS = T // EG
    KINDS = ("A", "B", "C")[:3 - layer]
    U = EG * len(KINDS)
    l = w[("l0", "l1")[layer]]
    table = io[("g", "x1")[layer]]
    RADK = (16, 65)[layer]
    mrow = w[f"mrow{layer}"]
    with ExitStack() as ctx:
        name = lambda n: f"e{layer}_{n}"
        sb = lambda n, s, dt=F32: ctx.enter_context(nc.sbuf_tensor(name(n), s, dt))
        pb = lambda n, s: ctx.enter_context(nc.psum_tensor(name(n), s, F32))
        sem = lambda n: ctx.enter_context(nc.semaphore(name(n)))
        rows = sb("rows", [P, EG, 2, D])
        index = sb("index", [P, 2 * EG], I32)
        yg = sb("yg", [P, EG, 4])
        ny = sb("ny", [P, EG, 4])
        rad_in = sb("rad_in", [RADK, EG * P])
        turned = sb("turned", [P, RING, 3 * P])
        msg = sb("msg", [P, RING, D])
        prod = sb("prod", [P, RING, 352])
        act_a = sb("act_a", [P, EG, C0])
        value = sb("value", [P, EG, D])
        acc = sb("acc", [P, CV])
        dot = sb("dot", [P, C1])
        tp = pb("tp", [P, RING, 512])
        mm = pb("mm", [P, RING, 512])
        o1 = pb("o1", [P, RING, 512])
        if layer == 0:
            o2 = pb("o2", [P, RING, 512])
            val = sb("val", [P, EG, 224])
            val_ready, hc_ready = sem("val_ready"), sem("hc_ready")
        else:
            hz = pb("hz", [P, 2, EG * 64])
            zt = pb("zt", [64, EG * P])
            h1, h2 = sb("h1", [65, EG * P]), sb("h2", [65, EG * P])
            z = sb("z", [P, EG, 64])
            stats = sb("stats", [P, 2 * EG, 6])
            stat2 = sb("stat2", [P, 2, 2 * EG, 6])
            K = 2 * EG
            mean, var = sb("mean", [P, K]), sb("var", [P, K])
            mz, vz, rz = sb("mz", [P, EG]), sb("vz", [P, EG]), sb("rz", [P, EG])
            mean2, var2 = sb("mean2", [P, 2 * K]), sb("var2", [P, 2 * K])
            e, r, tmp = sb("e", [P, 2, K]), sb("r", [P, 2, K]), sb("tmp", [P, 4, 2 * K])
            edge_vec = sb("edge_vec", [P, T, 3])
            norm_ready, h_ready, z_ready = sem("norm_ready"), sem("h_ready"), sem("z_ready")
            zt_ready, ht_ready, r_ready = sem("zt_ready"), sem("ht_ready"), sem("r_ready")
        gathered = [sem(f"gathered{j}") for j in range(EG)]
        rad_ready, pool_gate, index_ready = sem("rad_ready"), sem("pool_gate"), sem("index_ready")
        tp_ready, tp_moved, mm_ready = sem("tp_ready"), sem("tp_moved"), sem("mm_ready")
        msg_ready, prod_ready, ab_ready = sem("msg_ready"), sem("prod_ready"), sem("ab_ready")
        value_ready, kept, logit_ready = sem("value_ready"), sem("kept"), sem("logit_ready")
        vec, zeroed, gate_pe, y_ready = sem("vec"), sem("zeroed"), sem("gate_pe"), sem("y_ready")

        TP_GRANT, TWO = U, 2
        S0, SN = C1, (160, 128)[layer]
        B0 = S0 + SN

        def heads(j):
            return value[:, j].rearrange("p (h c) -> p h c", h=H)

        with nc.Block() as block:
            @block.sync
            def _(sp):
                def load(g):
                    if layer == 0:
                        sp.dma_start(rad_in[:], io["attr16"][:, bass.ds(g * (EG * P), EG * P)]).then_inc(rad_ready, 16)
                    else:
                        sp.dma_start(rad_in[0:64], io["attr64"][:, bass.ds(g * (EG * P), EG * P)]).then_inc(rad_ready, 16)

                if layer == 1:
                    sp.dma_start(edge_vec[:], io["attr3"]).then_inc(y_ready, 16)
                load(0)
                with sp.Fori(0, STEPS - 1) as g:
                    if layer == 0:
                        sp.wait_ge(mm_ready, U * g + EG + TWO)
                    else:
                        sp.wait_ge(h_ready, 2 * g + 1)
                    load(g + 1)

            @block.gpsimd
            def _(pool):
                def hold(s, value):
                    pool.wait_ge(s, value)
                    pool.sem_inc(pool_gate, 1)

                bound = pool.to_reg(io["rows"] - 1)
                with pool.Fori(0, STEPS) as g:
                    for j in range(EG):
                        hold(gathered[j], 32 * g)
                    nc.gpsimd.tensor_copy(index[:, 0:EG], flags["src"][:, bass.ds(g * EG, EG)]).then_inc(index_ready, 1)
                    nc.gpsimd.tensor_copy(index[:, EG:2 * EG], flags["dst"][:, bass.ds(g * EG, EG)]).then_inc(index_ready, 1)
                    hold(index_ready, 2 * g + 2)
                    hold(tp_ready, U * g + EG)
                    for j in range(EG):
                        for s in range(2):
                            at = index[:, s * EG + j:s * EG + j + 1].bitcast(U32)
                            nc.gpsimd.indirect_dma_start(rows[:, j, s], None, table,
                                                         bass.IndirectOffsetOnAxis(ap=at, axis=0),
                                                         bounds_check=bound).then_inc(gathered[j], 16)

            @block.tensor
            def _(pe):
                pe.sem_inc(tp_ready, TP_GRANT)
                pe.sem_inc(mm_ready, TWO)
                pe.wait_ge(zeroed, 4)

                def turn(g, u):
                    kind, j = KINDS[u // EG], u % EG
                    pe.wait_ge(tp_moved, U * g + u + 1)
                    if kind == "A":
                        if layer == 0:
                            pe.wait_ge(gathered[j], 32 * g + 32)
                        else:
                            pe.wait_ge(norm_ready, EG * g + j + 1)
                        src, cuts = rows[:, j].rearrange("p s c -> p (s c)"), (0, 128, 256, 320)
                    elif kind == "B":
                        pe.wait_ge(prod_ready, EG * g + j + 1 + TWO)
                        src, cuts = prod[:, j % RING], (0, 128, 256, 352)
                    else:
                        pe.wait_ge(val_ready, EG * g + j + 1 + TWO)
                        src, cuts = val[:, j], (0, 128, 224)
                    for c in range(len(cuts) - 1):
                        n = cuts[c + 1] - cuts[c]
                        last = nc.tensor.transpose(tp[0:n, u % RING, c * P:(c + 1) * P], src[:, cuts[c]:cuts[c + 1]], w["ident"])
                    last.then_inc(tp_ready, 1)

                def multiply(g, u):
                    kind, j, q = KINDS[u // EG], u % EG, u % RING
                    T0, T1, T2 = (turned[:, q, c * P:(c + 1) * P] for c in range(3))
                    pe.wait_ge(tp_moved, U * g + u + 1 + TWO)
                    if kind == "A":
                        if j == 0 and layer == 0:
                            pe.wait_ge(rad_ready, 16 * g + 16)
                        if j == 0 and layer == 1:
                            pe.wait_ge(ht_ready, 2 * g + 2)
                        pe.wait_ge(prod_ready, EG * g + j + 1)
                        o = mm[:, j % RING]
                        nc.tensor.matmul(o[:, 0:D], T0, l["in0"], start=True, stop=False)
                        nc.tensor.matmul(o[:, 0:D], T1, l["in1"], start=False, stop=False)
                        nc.tensor.matmul(o[:, 0:D], T2[0:64], l["in2"], start=False, stop=False)
                        nc.tensor.matmul(o[:, 0:D], flags["ones"][0:1, :], mrow, start=False, stop=True)
                        rad_t = rad_in if layer == 0 else h2
                        last = nc.tensor.matmul(o[:, D:D + WN], rad_t[:, j * P:(j + 1) * P], l["rad"], start=True, stop=True)
                    elif kind == "B":
                        pe.wait_ge(val_ready if layer == 0 else value_ready, EG * g + j + 1)
                        o = o1[:, j % RING]
                        nc.tensor.matmul(o[:, 0:B0], T0, l["first"], start=True, stop=True)
                        nc.tensor.matmul(o[:, S0:B0 + CV], T1, l["second"], start=False, stop=True, skip_group_check=True)
                        if layer == 1:
                            nc.tensor.matmul(o[:, S0:B0], flags["ones"][0:1, :], l["sbias"], start=False, stop=True,
                                             skip_group_check=True)
                        last = nc.tensor.matmul(o[:, B0 + CV:B0 + 2 * CV], T2[0:CV], l["third"], start=False, stop=True,
                                                skip_group_check=True)
                    else:
                        pe.wait_ge(value_ready, EG * g + j + 1)
                        o = o2[:, j % RING]
                        nc.tensor.matmul(o[:, 0:160], T0, l["out0"], start=True, stop=True)
                        last = nc.tensor.matmul(o[:, 160:352], T1[0:CV], l["out1"], start=True, stop=True)
                    last.then_inc(mm_ready, 1)

                def radial(g):
                    for n, (inp, wt) in enumerate(((rad_in, l["r1"]), (h1, l["r2"]))):
                        pe.wait_ge(z_ready, 2 * g + n)
                        if n == 0:
                            pe.wait_ge(rad_ready, 16 * g + 16)
                        else:
                            pe.wait_ge(ht_ready, 2 * g + 1)
                        for j in range(EG):
                            last = nc.tensor.matmul(hz[:, n, j * 64:(j + 1) * 64], inp[:, j * P:(j + 1) * P], wt, start=True, stop=True)
                        last.then_inc(h_ready, 1)
                        pe.wait_ge(z_ready, 2 * g + n + 1)
                        pe.sem_inc(gate_pe, 1)
                        pe.wait_ge(ht_ready, 2 * g + n)
                        pe.sem_inc(gate_pe, 1)
                        for j in range(EG):
                            last = nc.tensor.transpose(zt[:, j * P:(j + 1) * P], z[:, j], w["ident"])
                        last.then_inc(zt_ready, 1)

                with pe.Fori(0, STEPS) as g:
                    if layer == 1:
                        radial(g)
                    turn(g, 0)
                    for u in range(U):
                        if u + 1 < U:
                            turn(g, u + 1)
                        multiply(g, u)

            @block.scalar
            def _(act):
                act.sem_inc(tp_moved, TWO)

                def move(g, u):
                    n = 2 if KINDS[u // EG] == "C" else 3
                    act.wait_ge(tp_ready, U * g + u + 1 + TP_GRANT)
                    act.wait_ge(mm_ready, U * g + u + 1)
                    nc.scalar.copy(turned[:, u % RING, 0:n * P], tp[:, u % RING, 0:n * P]).then_inc(tp_moved, 1)

                def after(g, u):
                    kind, j = KINDS[u // EG], u % EG
                    act.wait_ge(mm_ready, U * g + u + 1 + TWO)
                    if kind == "A":
                        act.wait_ge(prod_ready, EG * g + j + 1)
                        nc.scalar.copy(msg[:, j % RING], mm[:, j % RING, 0:D]).then_inc(msg_ready, 1)
                    elif kind == "B":
                        o = o1[:, j % RING]
                        act.wait_ge(logit_ready, g)
                        if layer == 0:
                            act.wait_ge(tp_ready, U * g + 2 * EG + j + 1)
                            nc.scalar.activation(act_a[:, j], o[:, S0:S0 + C0], ACT.Copy, scale=0.2)
                            nc.scalar.activation(val[:, j, 0:96], o[:, S0 + C0:B0], ACT.Sigmoid).then_inc(ab_ready, 1)
                        else:
                            act.wait_ge(kept, g)
                            nc.scalar.activation(act_a[:, j], o[:, S0:S0 + C0], ACT.Tanh, scale=0.5)
                            nc.scalar.copy(heads(j)[:, :, 0:SW], o[:, S0 + C0:B0].rearrange("p (h c) -> p h c", h=H)).then_inc(ab_ready, 1)
                    else:
                        act.wait_ge(kept, g)
                        nc.scalar.activation(heads(j)[:, :, 0:SW], o2[:, j % RING, 0:C0].rearrange("p (h c) -> p h c", h=H),
                                             ACT.Copy, scale=yg[:, j, 0:1]).then_inc(hc_ready, 1)

                def gates(g, n):
                    act.wait_ge(zt_ready, 2 * g + n + 1)
                    h = (h1, h2)[n]
                    nc.scalar.activation(h[0:64], zt[:], ACT.Silu, bias=l[f"rbe{n + 1}"], scale=l[f"rg{n + 1}"]).then_inc(ht_ready, 1)

                act.wait_ge(zeroed, 4)
                with act.Fori(0, STEPS) as g:
                    if layer == 1:
                        gates(g, 0)
                        gates(g, 1)
                    move(g, 0)
                    for u in range(U):
                        if u + 1 < U:
                            move(g, u + 1)
                        after(g, u)

            @block.vector
            def _(dve):
                v = nc.vector
                dve.sem_inc(prod_ready, TWO)
                dve.sem_inc(value_ready, TWO)
                if layer == 0:
                    dve.sem_inc(val_ready, TWO)
                for q in range(RING):
                    v.memset(tp[:, q], 0.0).then_inc(zeroed, 1)
                y, before = flags["y0"], 0
                if layer == 0:
                    v.memset(acc[:], 0.0).then_inc(zeroed, 2)
                else:
                    v.memset(h1[64:65], 1.0)
                    v.memset(h2[64:65], 1.0)
                    v.memset(rad_in[64:65], 1.0).then_inc(zeroed, 2)
                    dve.wait_ge(y_ready, 16)
                    t = Tick(dve, vec, 0, 0)
                    yy = edge_vec
                    sq, ln, length, inverse, spare = y[:, :, 0], *(logits[:, :, n] for n in range(4))
                    t.link(v.tensor_tensor(sq, yy[:, :, 0], yy[:, :, 0], ALU.mult))
                    for c in (1, 2):
                        t.link(v.tensor_tensor(ln, yy[:, :, c], yy[:, :, c], ALU.mult))
                        t.link(v.tensor_tensor(sq, sq, ln, ALU.add))
                    t.link(v.tensor_scalar(length, sq, 1e-12, None, ALU.add))
                    rsqrt(nc, t, inverse, length, spare, r_ready)
                    dve.wait_ge(r_ready, 1)
                    for c in range(3):
                        t.mark(v.tensor_tensor(y[:, :, c + 1], yy[:, :, c], inverse, ALU.mult))
                    t.wait(t.n)
                    before = t.n

                def dots(t, out, m, j, last):
                    t.link(v.tensor_scalar(out, m[:, 0:C1], yg[:, j, 1:2], None, ALU.mult))
                    for c in (1, 2):
                        step = v.scalar_tensor_tensor(out, m[:, c * C1:(c + 1) * C1], yg[:, j, c + 1:c + 2], out, ALU.mult, ALU.add)
                        if c == 2 and last is None:
                            return step
                        t.link(step)
                    return last()

                def vectors(t, o, b, j, outs):
                    sh = [P, 3, C1]
                    a3 = acc[:].rearrange("p (d c) -> p d c", d=3)
                    A = o[:, 0:C1] if b[0] is None else o[:, b[0]:b[0] + C1]
                    t.link(v.tensor_tensor(a3, A.unsqueeze(1).to_broadcast(sh), yg[:, j, 1:4].unsqueeze(2).to_broadcast(sh), ALU.mult))
                    B = o[:, b[1]:b[1] + CV]
                    if layer == 0:
                        t.link(v.scalar_tensor_tensor(acc[:], B, yg[:, j, 0:1], acc[:], ALU.mult, ALU.add))
                    else:
                        t.link(v.tensor_tensor(acc[:], B, acc[:], ALU.add))
                    C = lambda d: o[:, b[2] + (d % 3) * C1:b[2] + (d % 3 + 1) * C1]
                    for d in range(3):
                        k = t.mark(v.scalar_tensor_tensor(a3[:, d], C(d + 1), yg[:, j, 1 + (d + 2) % 3:2 + (d + 2) % 3],
                                                          a3[:, d], ALU.mult, ALU.add))
                    for d in range(3):
                        t.wait(k - 2 + d)
                        step = v.scalar_tensor_tensor(outs(d), C(d + 2), ny[:, j, 1 + (d + 1) % 3:2 + (d + 1) % 3],
                                                      a3[:, d], ALU.mult, ALU.add)
                        if d < 2:
                            t.mark(step)
                    return step

                def products(t, g, j):
                    dve.wait_ge(msg_ready, EG * g + j + 1)
                    dve.wait_ge(tp_ready, U * g + EG + j - 1 + TP_GRANT if j >= 2 else U * g + EG + j + 3)
                    dve.wait_ge(prod_ready, EG * g + j + TWO)
                    m, ww, x = msg[:, j % RING], mm[:, j % RING, D:D + WN], prod[:, j % RING]
                    ms, mv = m[:, 0:C0], m[:, C0:D]
                    t.link(v.tensor_scalar(dot[:], mv[:, 0:C1], yg[:, j, 1:2], None, ALU.mult))
                    if layer == 0:
                        v.scalar_tensor_tensor(x[:, 0:C0], ww[:, 0:C0], yg[:, j, 0:1], ms, ALU.mult, ALU.mult)
                    else:
                        v.tensor_tensor(x[:, 0:C0], ww[:, 0:C0], ms, ALU.mult)
                    k = t.mark(v.scalar_tensor_tensor(dot[:], mv[:, C1:2 * C1], yg[:, j, 2:3], dot[:], ALU.mult, ALU.add))
                    v.tensor_tensor(x[:, C0:2 * C0], ww[:, C0:2 * C0], ms, ALU.mult)
                    t.wait(k)
                    k = t.mark(v.scalar_tensor_tensor(dot[:], mv[:, 2 * C1:3 * C1], yg[:, j, 3:4], dot[:], ALU.mult, ALU.add))
                    for n, at in ((0, 128), (1, 256)):
                        wv = ww[:, 128 + 64 * n:160 + 64 * n].unsqueeze(1).to_broadcast([P, 3, C1])
                        v.tensor_tensor(x[:, at:at + CV].rearrange("p (d c) -> p d c", d=3), wv,
                                        mv.rearrange("p (d c) -> p d c", d=3), ALU.mult)
                    t.wait(k)
                    v.tensor_tensor(x[:, 224:256], ww[:, 160:192], dot[:], ALU.mult).then_inc(prod_ready, 1)

                def norms(t, g):
                    flat = lambda a: a.rearrange("p a b -> p (a b)")
                    R = rows[:].rearrange("p j s c -> p (j s) c")
                    for k in range(K):
                        if k % 2 == 0:
                            dve.wait_ge(gathered[k // 2], 32 * g + 32)
                        n = t.mark(v.bn_stats(stats[:, k], R[:, k]))
                    t.wait(n)
                    t.wait(moments(nc, t, stats[:], D, mean[:], var[:], [tmp[:, i, 0:K] for i in range(4)]))
                    for k in range(K):
                        n = t.mark(v.tensor_scalar(R[:, k], R[:, k], mean[:, k:k + 1], 0.0, ALU.subtract, ALU.max))
                    t.mark(v.tensor_scalar(var[:], var[:], EPS, EPS, ALU.add, ALU.mult))
                    for k in range(K):
                        t.wait(n - K + 1 + k)
                        t.mark(v.bn_stats(stat2[:, 0, k], R[:, k, 0:C0]))
                        m = t.mark(v.bn_stats(stat2[:, 1, k], R[:, k, C0:D]))
                    t.wait(m)
                    moments(nc, t, stat2[:, 0], C0, mean2[:, 0:K], var2[:, 0:K], [tmp[:, i, 0:K] for i in range(4)])
                    t.wait(moments(nc, t, stat2[:, 1], CV, mean2[:, K:2 * K], var2[:, K:2 * K], [tmp[:, i, K:2 * K] for i in range(4)]))
                    m = t.mark(v.tensor_tensor(tmp[:, 3, 0:K], mean2[:, K:2 * K], mean2[:, K:2 * K], ALU.mult))
                    t.mark(v.tensor_tensor(e[:, 0], var2[:, 0:K], var[:], ALU.add))
                    t.link(v.tensor_tensor(e[:, 1], var2[:, K:2 * K], var[:], ALU.add))
                    t.link(v.tensor_tensor(e[:, 1], e[:, 1], tmp[:, 3, 0:K], ALU.add))
                    rsqrt(nc, t, flat(r[:]), flat(e[:]), tmp[:, 0], r_ready)
                    dve.wait_ge(r_ready, 3 * g + 3)
                    for k in range(K):
                        v.tensor_scalar(R[:, k, 0:C0], R[:, k, 0:C0], mean2[:, k:k + 1], r[:, 0, k:k + 1], ALU.subtract, ALU.mult)
                        m = v.tensor_scalar(R[:, k, C0:D], R[:, k, C0:D], r[:, 1, k:k + 1], None, ALU.mult)
                        if k % 2:
                            m.then_inc(norm_ready, 1)

                def layer_norm(t, g, n):
                    dve.wait_ge(h_ready, 2 * g + n + 1)
                    for j in range(EG):
                        k = t.mark(v.bn_stats(stats[:, j], hz[:, n, j * 64:(j + 1) * 64]))
                    t.wait(k)
                    t.wait(moments(nc, t, stats[:, 0:EG], 64, mz[:], vz[:], [tmp[:, i, 0:EG] for i in range(4)]))
                    t.link(v.tensor_scalar(vz[:], vz[:], EPS, None, ALU.add))
                    rsqrt(nc, t, rz[:], vz[:], tmp[:, 0, 0:EG], r_ready)
                    dve.wait_ge(r_ready, 3 * g + 2 + (0, 2)[n])
                    dve.wait_ge(zt_ready, 2 * g + n)
                    for j in range(EG):
                        m = v.tensor_scalar(z[:, j], hz[:, n, j * 64:(j + 1) * 64], mz[:, j:j + 1], rz[:, j:j + 1],
                                            ALU.subtract, ALU.mult)
                    m.then_inc(z_ready, 1)

                VEC = 2 + 3 + 2
                if layer == 0:
                    STEP = 2 + EG * 3 + EG * (1 + VEC + 1 + 1 + 2) + 1 + EG * (1 + VEC)
                else:
                    LN = EG + MOMENTS + 1 + RSQRT
                    NORM = K + MOMENTS + K + 1 + 2 * K + 2 * MOMENTS + 4 + RSQRT
                    STEP = 2 + EG * 3 + 2 * LN + NORM + EG * (1 + VEC) + 1
                with dve.Fori(0, STEPS) as g:
                    t = Tick(dve, vec, g, STEP, before)
                    t.link(v.tensor_copy(yg[:], y[:, bass.ds(g * EG, EG), :]))
                    t.link(v.tensor_scalar(ny[:], yg[:], -1.0, None, ALU.mult))
                    if layer == 1:
                        layer_norm(t, g, 0)
                        norms(t, g)
                        layer_norm(t, g, 1)
                    for j in range(EG):
                        products(t, g, j)
                    for j in range(EG):
                        dve.wait_ge(ab_ready, EG * g + j + 1)
                        o = o1[:, j % RING]
                        if layer == 0:
                            z3 = val[:, j, 128:224].rearrange("p (d c) -> p d c", d=3)
                            t.mark(v.tensor_tensor(act_a[:, j], act_a[:, j], o[:, S0:S0 + C0], ALU.max))
                            t.link(vectors(t, o, (None, B0, B0 + CV), j, lambda d: acc[:, d * C1:(d + 1) * C1]))
                            t.link(v.tensor_tensor(z3, acc[:].rearrange("p (d c) -> p d c", d=3),
                                                   val[:, j, 64:96].unsqueeze(1).to_broadcast([P, 3, C1]), ALU.mult))
                            dots(t, val[:, j, 96:128], val[:, j, 128:224], j, None).then_inc(val_ready, 1)
                        else:
                            dve.wait_ge(value_ready, EG * g + j + TWO)
                            t.mark(v.scalar_tensor_tensor(act_a[:, j], act_a[:, j], 1.5, o[:, S0:S0 + C0], ALU.add, ALU.mult))
                            vh = heads(j)
                            vectors(t, o, (None, B0, B0 + CV), j,
                                    lambda d: vh[:, :, SW + d * VW:SW + (d + 1) * VW]).then_inc(value_ready, 1)
                    a3 = act_a[:].rearrange("p j c -> p j c")
                    t.link(v.tensor_tensor(a3, a3, l["dot"].unsqueeze(1).to_broadcast([P, EG, C0]), ALU.mult))
                    v.tensor_reduce(logits[:, bass.ds(g * EG, EG), :], act_a[:].rearrange("p j (h c) -> p j h c", h=H),
                                    AX_X, ALU.add).then_inc(logit_ready, 1)
                    if layer == 0:
                        for j in range(EG):
                            dve.wait_ge(hc_ready, EG * g + j + 1)
                            dve.wait_ge(value_ready, EG * g + j + TWO)
                            o = o2[:, j % RING]
                            vh = heads(j)
                            t.mark(v.tensor_tensor(vh[:, :, 0:SW], o[:, 96:160].rearrange("p (h c) -> p h c", h=H), vh[:, :, 0:SW], ALU.add))
                            vectors(t, o, (64, 160, 256), j,
                                    lambda d: vh[:, :, SW + d * VW:SW + (d + 1) * VW]).then_inc(value_ready, 1)
                    dve.wait_ge(value_ready, EG * g + EG + TWO)
                    v.tensor_copy(vals[:, bass.ds(g * EG, EG), :], value[:]).then_inc(kept, 1)
                    t.close()


def softmax(nc, w, flags, T, layer, logits):
    H = (4, 8)[layer]
    DEN_EPS = (1e-16, 1e-12)[layer]
    with ExitStack() as ctx:
        name = lambda n: f"s{layer}_{n}"
        sb = lambda n, s, dt=F32: ctx.enter_context(nc.sbuf_tensor(name(n), s, dt))
        sem = lambda n: ctx.enter_context(nc.semaphore(name(n)))
        fwd, total = sb("fwd", [P, T, H]), sb("total", [P, T, H])
        neg_same, neg_nxt, ends = sb("neg_same", [P, T]), sb("neg_nxt", [P, T]), sb("ends", [P, T])
        edge = sb("edge", [P, 2, H])
        wide = sb("wide", [P, 2 * H, P])
        keys = sb("keys", [P, 2, P])
        eq, neg_eq = sb("eq", [P, 2, 2, P]), sb("neg_eq", [P, 2, 2, P])
        work = sb("work", [P, H, P])
        part = sb("part", [P, 2, 2, H])
        whole = sb("whole", [P, 2, H])
        open_ = sb("open", [P, 1])
        turned = ctx.enter_context(nc.psum_tensor(name("turned"), [P, 2 * H, P], F32))
        keys_t = ctx.enter_context(nc.psum_tensor(name("keys_t"), [P, 2, P], F32))
        vec, wide_ready, turned_ready = sem("vec"), sem("wide_ready"), sem("turned_ready")
        shifted, exp_ready = sem("shifted"), sem("exp_ready")
        ths = [P, T, H]

        with nc.Block() as block:
            @block.tensor
            def _(pe):
                for n in range(3):
                    pe.wait_ge(wide_ready, n + 1)
                    src, out = (keys, keys_t) if n == 0 else (wide, turned)
                    for k in range(2 if n == 0 else 2 * H):
                        last = nc.tensor.transpose(out[:, k], src[:, k], w["ident"])
                    last.then_inc(turned_ready, 1)

            @block.scalar
            def _(act):
                act.wait_ge(shifted, 1)
                nc.scalar.activation(logits[:].rearrange("p t h -> p (t h)"), fwd[:].rearrange("p t h -> p (t h)"),
                                     ACT.Exp).then_inc(exp_ready, 1)

            @block.vector
            def _(dve):
                v = nc.vector
                t = Tick(dve, vec)
                first, last, mid = flags["first"], flags["last"], flags["mid"]
                for n, key in enumerate(("head", "tail")):
                    k = v.tensor_copy(keys[:, n], flags[key][:].to_broadcast([P, P]))
                k.then_inc(wide_ready, 1)
                t.mark(v.tensor_scalar(neg_same[:], flags["same"][:], 1.0, BIG, ALU.subtract, ALU.mult))
                t.mark(v.tensor_scalar(neg_nxt[:], flags["nxt"][:], 1.0, BIG, ALU.subtract, ALU.mult))
                t.mark(v.tensor_scalar(ends[:], flags["nxt"][:], -1.0, 1.0, ALU.mult, ALU.add))
                t.mark(v.tensor_scalar(open_[:], first[:, T - 1:T], -1.0, 1.0, ALU.mult, ALU.add))
                dve.wait_ge(turned_ready, 1)
                for q, key in enumerate(("head", "tail")):
                    for n in range(2):
                        t.mark(v.tensor_scalar(eq[:, q, n], keys_t[:, n], flags[key][:], None, ALU.is_equal))
                t.done()
                t.mark(v.tensor_scalar(neg_eq[:], eq[:], 1.0, BIG, ALU.subtract, ALU.mult))
                if layer == 0:
                    t.mark(v.tensor_copy(flags["tt"][:], eq[:, 1, 1]))
                    t.link(v.tensor_tensor(work[:, 0], eq[:, 1, 1], w["low"], ALU.mult))
                    t.link(v.tensor_reduce(flags["tail_row"][:], work[:, 0], AX_X, ALU.max))
                    t.link(v.scalar_tensor_tensor(open_[:], flags["tail_row"][:], SKIP, flags["tail"][:], ALU.mult, ALU.add))
                    t.link(v.tensor_copy(flags["tail_at"][:], open_[:]))
                    t.link(v.tensor_scalar(open_[:], first[:, T - 1:T], -1.0, 1.0, ALU.mult, ALU.add))

                def across(nth, op_mask, masks, op):
                    v.tensor_copy(wide[:].rearrange("p (n h) c -> p n h c", n=2),
                                  edge[:].unsqueeze(3).to_broadcast([P, 2, H, P])).then_inc(wide_ready, 1)
                    dve.wait_ge(turned_ready, nth)
                    for q in range(2):
                        for n in range(2):
                            t.link(v.tensor_tensor(work[:], turned[:, n * H:(n + 1) * H],
                                                   masks[:, q, n].unsqueeze(1).to_broadcast([P, H, P]), op_mask))
                            t.link(v.tensor_reduce(part[:, q, n], work[:], AX_X, op))
                    t.link(v.tensor_tensor(whole[:], part[:, :, 0], part[:, :, 1], op))

                def combine():
                    bc = lambda f: f[:].unsqueeze(2).to_broadcast(ths)
                    t.link(v.tensor_tensor(total[:], total[:], bc(mid), ALU.mult))
                    for q, f in enumerate((first, last)):
                        t.link(v.tensor_tensor(fwd[:], whole[:, q].unsqueeze(1).to_broadcast(ths), bc(f), ALU.mult))
                        t.link(v.tensor_tensor(total[:], total[:], fwd[:], ALU.add))

                for h in range(H):
                    k = t.mark(v.tensor_tensor_scan(fwd[:, :, h], neg_same[:], logits[:, :, h], -BIG, ALU.add, ALU.max))
                for h in range(H):
                    t.wait(k - H + 1 + h)
                    t.mark(v.tensor_tensor_scan(total[:, ::-1, h], neg_nxt[:, ::-1], fwd[:, ::-1, h], -BIG, ALU.add, ALU.max))
                t.done()
                t.mark(v.tensor_copy(edge[:, 0], total[:, 0]))
                t.link(v.tensor_copy(edge[:, 1], total[:, T - 1]))
                across(2, ALU.add, neg_eq, ALU.max)
                combine()
                v.tensor_tensor(fwd[:], logits[:], total[:], ALU.subtract).then_inc(shifted, 1)
                dve.wait_ge(exp_ready, 1)
                for h in range(H):
                    t.mark(v.tensor_tensor_scan(fwd[:, :, h], flags["same"][:], logits[:, :, h], 0.0, ALU.mult, ALU.add))
                t.done()
                t.link(v.tensor_tensor(fwd[:], fwd[:], ends[:].unsqueeze(2).to_broadcast(ths), ALU.mult))
                for h in range(H):
                    t.mark(v.tensor_tensor_scan(total[:, ::-1, h], flags["nxt"][:, ::-1], fwd[:, ::-1, h], 0.0, ALU.mult, ALU.add))
                t.done()
                t.mark(v.tensor_scalar(edge[:, 0], total[:, 0], open_[:], None, ALU.mult))
                t.link(v.tensor_copy(edge[:, 1], total[:, T - 1]))
                across(3, ALU.mult, eq, ALU.add)
                combine()
                t.link(v.tensor_scalar(total[:], total[:], DEN_EPS, None, ALU.add))
                t.link(v.reciprocal(total[:], total[:]))
                t.link(v.tensor_tensor(logits[:], logits[:], total[:], ALU.mult))


def scatter(nc, io, w, flags, T, layer, vals, alpha):
    H = (4, 8)[layer]
    STEPS = T // EG
    l = w[("l0", "l1")[layer]]
    table = io[("x1", "agg")[layer]]
    with ExitStack() as ctx:
        name = lambda n: f"a{layer}_{n}"
        sb = lambda n, s, dt=F32: ctx.enter_context(nc.sbuf_tensor(name(n), s, dt))
        pb = lambda n, s: ctx.enter_context(nc.psum_tensor(name(n), s, F32))
        sem = lambda n: ctx.enter_context(nc.semaphore(name(n)))
        weighted = sb("weighted", [P, EG, D])
        sums = sb("sums", [P, EG, D])
        merged = sb("merged", [P, D])
        same = sb("same", [P, EG])
        index = sb("index", [P, EG], I32)
        turned = sb("turned", [P, RING, 2 * P])
        rows = sb("rows", [P, EG, D])
        tp, out = pb("tp", [P, RING, 512]), pb("out", [P, RING, 512])
        vec, zeroed, sum_ready, tp_ready = sem("vec"), sem("zeroed"), sem("sum_ready"), sem("tp_ready")
        tp_moved, out_ready, row_ready = sem("tp_moved"), sem("out_ready"), sem("row_ready")
        index_ready, pool_gate = sem("index_ready"), sem("pool_gate")
        written = [sem(f"written{j}") for j in range(EG)]
        tails_ready, merged_ready, tails_written = sem("tails_ready"), sem("merged_ready"), sem("tails_written")
        tiles = EG * STEPS

        with nc.Block() as block:
            @block.gpsimd
            def _(pool):
                def hold(s, value):
                    pool.wait_ge(s, value)
                    pool.sem_inc(pool_gate, 1)

                bound = pool.to_reg(io["rows"] - 1)
                with pool.Fori(0, STEPS) as g:
                    for j in range(EG):
                        hold(written[j], 16 * g)
                        nc.gpsimd.tensor_copy(index[:, j:j + 1], flags["row"][:, bass.ds(g * EG + j, 1)]).then_inc(index_ready, 1)
                    for j in range(EG):
                        hold(index_ready, EG * g + j + 1)
                        hold(row_ready, EG * g + j + 1 + RING)
                        nc.gpsimd.indirect_dma_start(table, bass.IndirectOffsetOnAxis(ap=index[:, j:j + 1].bitcast(U32), axis=0),
                                                     rows[:, j], None, bounds_check=bound, oob_is_err=False,
                                                     compute_op=ALU.add).then_inc(written[j], 16)
                for j in range(EG):
                    pool.wait_ge(written[j], 16 * STEPS)
                pool.wait_ge(row_ready, tiles + 1 + RING)
                nc.gpsimd.indirect_dma_start(table, bass.IndirectOffsetOnAxis(ap=flags["tail_at"][:].bitcast(U32), axis=0),
                                             rows[:, 0], None, bounds_check=bound, oob_is_err=False,
                                             compute_op=ALU.add).then_inc(tails_written, 16)
                pool.wait_ge(tails_written, 16)

            @block.tensor
            def _(pe):
                pe.sem_inc(tp_ready, EG)

                def turn(i, j, src):
                    pe.wait_ge(tp_moved, i + 1)
                    for c, (a, b) in enumerate(((0, 128), (128, 160))):
                        last = nc.tensor.transpose(tp[0:b - a, j % RING, c * P:(c + 1) * P], src[:, a:b], w["ident"])
                    last.then_inc(tp_ready, 1)

                def turn_sums(g, j):
                    pe.wait_ge(sum_ready, EG * g + j + 1)
                    turn(EG * g + j, j, sums[:, j])

                def project(i, j):
                    pe.wait_ge(tp_moved, i + 1 + RING)
                    pe.wait_ge(row_ready, i + 1)
                    nc.tensor.matmul(out[:, j % RING, 0:D], turned[:, j % RING, 0:P], l["p0"], start=True, stop=False)
                    nc.tensor.matmul(out[:, j % RING, 0:D], turned[0:32, j % RING, P:2 * P], l["p1"],
                                     start=False, stop=True).then_inc(out_ready, 1)

                pe.wait_ge(zeroed, 3)
                turn_sums(0, 0)
                with pe.Fori(0, STEPS - 1) as g:
                    for j in range(EG):
                        turn_sums(g + (j + 1) // EG, (j + 1) % EG)
                        project(EG * g + j, j)
                for j in range(EG - 1):
                    turn_sums(STEPS - 1, j + 1)
                    project(tiles - EG + j, j)
                project(tiles - 1, EG - 1)
                pe.wait_ge(row_ready, tiles - 1 + RING)
                nc.tensor.matmul(out[:, 0, 256:256 + D], flags["tt"][:], sums[:, EG - 1], start=True, stop=True).then_inc(tails_ready, 1)
                pe.wait_ge(merged_ready, 1)
                turn(tiles, 0, merged[:])
                project(tiles, 0)

            @block.scalar
            def _(act):
                act.sem_inc(tp_moved, RING)
                act.sem_inc(row_ready, RING)

                def move(i, j):
                    act.wait_ge(tp_ready, i + 1 + EG)
                    nc.scalar.copy(turned[:, j % RING], tp[:, j % RING, 0:2 * P]).then_inc(tp_moved, 1)

                def keep(i, j, uses):
                    act.wait_ge(out_ready, i + 1)
                    act.wait_ge(written[j], 16 * uses)
                    nc.scalar.copy(rows[:, j], out[:, j % RING, 0:D]).then_inc(row_ready, 1)

                act.wait_ge(zeroed, 3)
                move(0, 0)
                with act.Fori(0, STEPS - 1) as g:
                    for j in range(EG):
                        move(EG * g + j + 1, j + 1)
                        keep(EG * g + j, j, g)
                for j in range(EG):
                    if j < EG - 1:
                        move(tiles - EG + j + 1, j + 1)
                    keep(tiles - EG + j, j, STEPS - 1)
                move(tiles, 0)
                keep(tiles, 0, STEPS)

            @block.vector
            def _(dve):
                v = nc.vector
                for q in range(RING):
                    v.memset(tp[:, q], 0.0).then_inc(zeroed, 1)
                v.memset(sums[:], 0.0).then_inc(zeroed, 1)
                dve.wait_ge(zeroed, 3)
                with dve.Fori(0, STEPS) as g:
                    t = Tick(dve, vec, g, 2)
                    dve.wait_ge(sum_ready, EG * g)
                    step = bass.ds(g * EG, EG)
                    t.mark(v.tensor_copy(same[:], flags["same"][:, step]))
                    t.mark(v.tensor_tensor(weighted[:].rearrange("p j (h c) -> p j h c", h=H),
                                           vals[:, step, :].rearrange("p j (h c) -> p j h c", h=H),
                                           alpha[:, step, :].unsqueeze(3).to_broadcast([P, EG, H, D // H]), ALU.mult))
                    t.done()
                    t.close()
                    for j in range(EG):
                        if j:
                            dve.wait_ge(sum_ready, EG * g + j)
                        dve.wait_ge(tp_ready, EG * g + j + 1)
                        v.scalar_tensor_tensor(sums[:, j], sums[:, (j - 1) % EG], same[:, j:j + 1], weighted[:, j],
                                               ALU.mult, ALU.add).then_inc(sum_ready, 1)
                dve.wait_ge(tails_ready, 1)
                v.tensor_copy(merged[:], out[:, 0, 256:256 + D]).then_inc(merged_ready, 1)


def feed(nc, io, w, STEPS):
    N2 = 2 * FG
    c = w["ff"]
    FN = FG * P
    with ExitStack() as ctx:
        sb = lambda n, s, dt=F32: ctx.enter_context(nc.sbuf_tensor("f_" + n, s, dt))
        pb = lambda n, s: ctx.enter_context(nc.psum_tensor("f_" + n, s, F32))
        sem = lambda n: ctx.enter_context(nc.semaphore("f_" + n))
        x, agg, a0 = sb("x", [P, 2, N2, D]), sb("agg", [P, 2, N2, D]), sb("a0", [P, 2, N2])
        u, y = sb("u", [P, N2, D]), sb("y", [P, 2, N2, D])
        norm = sb("norm", [P, 2, N2, 161])
        res, a0_kept = sb("res", [P, 2, N2, D]), sb("a0_kept", [P, 2, N2])
        stats, stat2 = sb("stats", [P, N2, 6]), sb("stat2", [P, 2, N2, 6])
        mean, negm, var = sb("mean", [P, N2]), sb("negm", [P, N2]), sb("var", [P, N2])
        share = sb("share", [P, 2 * N2])
        mean2, var2 = sb("mean2", [P, 2, N2]), sb("var2", [P, 2, N2])
        r, r2, tmp = sb("r", [P, N2]), sb("r2", [P, 2, N2]), sb("tmp", [P, 4, 2 * N2])
        sT, vT = sb("sT", [65, 2, FN]), sb("vT", [CV, 2, FN])
        hid, gate = sb("hid", [P, 2, FN]), sb("gate", [P, 2, FN])
        f0, f1 = sb("f0", [P, 2, FN]), sb("f1", [65, 2, FN])
        o = sb("o", [P, 2, FG, D])
        pS, pV = pb("pS", [65, FN]), pb("pV", [CV, FN])
        pH, pG, p0, p1 = pb("pH", [P, FN]), pb("pG", [P, FN]), pb("p0", [P, FN]), pb("p1", [64, FN])
        pO = pb("pO", [P, 2, 512])
        x_in, o_out = [sem("x_in0"), sem("x_in1")], [sem("o_out0"), sem("o_out1")]
        vec, negm_ready, u_ready, r_ready, y_ready = sem("vec"), sem("negm_ready"), sem("u_ready"), sem("r_ready"), sem("y_ready")
        scale_ready, ns_ready, nv_ready, res_ready = sem("scale_ready"), sem("ns_ready"), sem("nv_ready"), sem("res_ready")
        s_turned, v_turned, s_moved, v_moved = sem("s_turned"), sem("v_turned"), sem("s_moved"), sem("v_moved")
        g_mm, hid_mm, fv_mm, hid_ready, gate_ready = sem("g_mm"), sem("hid_mm"), sem("fv_mm"), sem("hid_ready"), sem("gate_ready")
        f_ready, o_mm, o_ready, gate_pe, pool_gate = sem("f_ready"), sem("o_mm"), sem("o_ready"), sem("gate_pe"), sem("pool_gate")
        grp = lambda a: a.rearrange("(g p j) c -> g p j c", p=P, j=N2)
        xs, aggs, outs = grp(io["x1"]), grp(io["agg"]), grp(io["out"])
        a0s = io["a0"].rearrange("(g p j) c -> g p (j c)", p=P, j=N2)
        FRONT = N2 + MOMENTS + 1 + RSQRT + 2 * N2 + (MOMENTS + 1) + 3 + RSQRT + 1
        HALVES = 2 * STEPS

        def known(n, low, high=STEPS):
            return isinstance(n, int) and low <= n < high

        assert STEPS % 2 and STEPS > 4

        def steps(run, step):
            step(0, 0, True, False)
            with run.Fori(0, (STEPS - 2) // 2) as i:
                step(2 * i + 1, 1, True, True)
                step(2 * i + 2, 0, True, True)
            step(STEPS - 2, 1, True, True)
            step(STEPS - 1, 0, False, True)

        with nc.Block() as block:
            @block.sync
            def _(sp):
                def load(s, b):
                    sp.dma_start(x[:, b], xs[s]).then_inc(x_in[b], 16)
                    sp.dma_start(agg[:, b], aggs[s]).then_inc(x_in[b], 16)
                    sp.dma_start(a0[:, b], a0s[s]).then_inc(x_in[b], 16)

                def store(k, step, h, slot):
                    sp.wait_ge(o_ready, FG * (k + 1))
                    sp.dma_start(outs[step][:, h * FG:(h + 1) * FG], o[:, slot]).then_inc(o_out[slot], 16)

                def step(s, b, front, back):
                    if not known(s, STEPS - 2):
                        sp.wait_ge(res_ready, s + 1)
                        load(s + 2, b)
                    if back:
                        store(2 * s - 2, s - 1, 0, 0)
                        store(2 * s - 1, s - 1, 1, 1)

                load(0, 0)
                load(1, 1)
                steps(sp, step)
                store(HALVES - 2, STEPS - 1, 0, 0)
                store(HALVES - 1, STEPS - 1, 1, 1)
                for slot in range(2):
                    sp.wait_ge(o_out[slot], 16 * STEPS)

            @block.gpsimd
            def _(pool):
                def hold(s, value):
                    pool.wait_ge(s, value)
                    pool.sem_inc(pool_gate, 1)

                def step(s, b, front, back):
                    hold(ns_ready, N2 * (s + 1))
                    if back:
                        hold(o_ready, FG * (2 * s - 2))
                    nc.gpsimd.tensor_copy(a0_kept[:, b], a0[:, b])
                    nc.gpsimd.tensor_tensor(res[:, b], x[:, b], y[:, b], ALU.add).then_inc(res_ready, 1)

                steps(pool, step)

            @block.vector
            def _(dve):
                v = nc.vector
                flat = lambda a: a.rearrange("p a b -> p (a b)")

                def first_moments(t, n, b, nth):
                    dve.wait_ge(x_in[b], 48 * nth + 48)
                    for j in range(N2):
                        k = t.mark(v.bn_stats(stats[:, j], x[:, b, j]))
                    t.wait(k)
                    t.wait(moments(nc, t, stats[:], D, mean[:], var[:], [tmp[:, i, 0:N2] for i in range(4)]))
                    v.tensor_scalar(negm[:], mean[:], -1.0, None, ALU.mult).then_inc(negm_ready, 1)
                    t.link(v.tensor_scalar(var[:], var[:], EPS, None, ALU.add))

                def sums(n, b):
                    dve.wait_ge(r_ready, 2 * n + 1)
                    for j in range(N2):
                        dve.wait_ge(u_ready, N2 * n + j + 1)
                        v.scalar_tensor_tensor(y[:, b, j], u[:, j], r[:, j:j + 1], agg[:, b, j],
                                               ALU.mult, ALU.add).then_inc(y_ready, 1)

                def sum_moments(t, n, b):
                    for j in range(N2):
                        dve.wait_ge(y_ready, N2 * n + j + 1)
                        t.mark(v.bn_stats(stat2[:, 0, j], y[:, b, j, 0:C0]))
                        k = t.mark(v.bn_stats(stat2[:, 1, j], y[:, b, j, C0:D]))
                    t.wait(k)

                def factors(t, n, b, between):
                    moments(nc, t, stat2[:].rearrange("p i j c -> p (i j) c"), share[:], flat(mean2[:]), flat(var2[:]),
                            [tmp[:, k] for k in range(4)])
                    t.done()
                    t.link(v.tensor_tensor(tmp[:, 3, 0:N2], mean2[:, 1], mean2[:, 1], ALU.mult))
                    t.link(v.tensor_tensor(var2[:, 1], var2[:, 1], tmp[:, 3, 0:N2], ALU.add))
                    t.link(v.tensor_scalar(var2[:], var2[:], EPS, None, ALU.add))
                    dve.wait_ge(nv_ready, N2 * n)
                    rsqrt(nc, t, flat(r2[:]), flat(var2[:]), tmp[:, 0], r_ready, between)
                    dve.wait_ge(r_ready, 2 * n + 2)
                    if not known(n, 0, 2):
                        dve.wait_ge(s_turned, 2 * n - 2)
                    t.mark(v.tensor_copy(norm[:, b, :, C0], a0[:, b]))
                    t.close()
                    v.tensor_tensor(r2[:], r2[:], a0[:, b].unsqueeze(1).to_broadcast([P, 2, N2]), ALU.mult).then_inc(scale_ready, 1)

                def scalars(n, b):
                    dve.wait_ge(scale_ready, n + 1)
                    for j in range(N2):
                        v.tensor_scalar(norm[:, b, j, 0:C0], y[:, b, j, 0:C0], mean2[:, 0, j:j + 1], r2[:, 0, j:j + 1],
                                        ALU.subtract, ALU.mult).then_inc(ns_ready, 1)

                def gated(k, slot):
                    dve.wait_ge(fv_mm, k + 1)
                    dve.wait_ge(gate_ready, k + 1)
                    if not known(k, 0, 1):
                        dve.wait_ge(o_mm, FG * (k - 1))
                    v.scalar_tensor_tensor(f0[:, slot], gate[:, slot], 1.0, p0[:], ALU.add, ALU.mult)
                    v.scalar_tensor_tensor(f1[0:64, slot], gate[0:64, slot], 1.0, p1[:], ALU.add, ALU.mult).then_inc(f_ready, 1)

                def outputs(k, step, b, h, uses):
                    def out(j):
                        if j == 0:
                            dve.wait_ge(res_ready, step + 1)
                            dve.wait_ge(o_out[h], 16 * uses)
                        dve.wait_ge(o_mm, FG * k + (j // 2) * 2 + 2)
                        i = h * FG + j
                        v.scalar_tensor_tensor(o[:, h, j], pO[:, j // 2, (j % 2) * D:(j % 2 + 1) * D], a0_kept[:, b, i:i + 1],
                                               res[:, b, i], ALU.mult, ALU.add).then_inc(o_ready, 1)
                    return out

                def step(s, b, front, back):
                    t = Tick(dve, vec, s + 1, FRONT)
                    if front:
                        first_moments(t, s + 1, 1 - b, (s + 1) // 2 if known(s, 0) else nth[b])
                        rsqrt(nc, t, r[:], var[:], tmp[:, 0, 0:N2], r_ready)
                    if back:
                        dve.wait_ge(res_ready, s)
                    if front:
                        sums(s + 1, 1 - b)
                    if back:
                        gated(2 * s - 1, 1)
                    if front:
                        sum_moments(t, s + 1, 1 - b)
                    if back:
                        first = outputs(2 * s - 2, s - 1, 1 - b, 0, s - 1)
                    if front:
                        factors(t, s + 1, 1 - b, first if back else None)
                    elif back:
                        for j in range(FG):
                            first(j)
                    gated(2 * s, 0)
                    if front:
                        scalars(s + 1, 1 - b)
                    if back:
                        second = outputs(2 * s - 1, s - 1, 1 - b, 1, s - 1)
                        for j in range(FG):
                            second(j)

                v.memset(f1[64:65], 1.0)
                v.memset(share[:, 0:N2], 1.0 / C0)
                v.memset(share[:, N2:], 1.0 / CV)
                t = Tick(dve, vec, 0, FRONT)
                first_moments(t, 0, 0, 0)
                rsqrt(nc, t, r[:], var[:], tmp[:, 0, 0:N2], r_ready)
                sums(0, 0)
                sum_moments(t, 0, 0)
                factors(t, 0, 0, None)
                scalars(0, 0)
                nth = {}
                step(0, 0, True, False)
                with dve.Fori(0, (STEPS - 2) // 2) as i:
                    nth[1], nth[0] = i + 1, i + 1
                    step(2 * i + 1, 1, True, True)
                    step(2 * i + 2, 0, True, True)
                step(STEPS - 2, 1, True, True)
                step(STEPS - 1, 0, False, True)
                gated(HALVES - 1, 1)
                for h in range(2):
                    out = outputs(HALVES - 2 + h, STEPS - 1, 0, h, STEPS - 1)
                    for j in range(FG):
                        out(j)

            @block.tensor
            def _(pe):
                def turn(k, step, b, h):
                    for part, ready, moved, rows, a, done in ((pS, ns_ready, s_moved, 65, 0, s_turned),
                                                              (pV, nv_ready, v_moved, CV, 65, v_turned)):
                        pe.wait_ge(ready, N2 * step + (h + 1) * FG)
                        pe.sem_inc(gate_pe, 1)
                        pe.wait_ge(moved, k)
                        pe.sem_inc(gate_pe, 1)
                        for j in range(FG):
                            last = nc.tensor.transpose(part[:, j * P:(j + 1) * P], norm[:, b, h * FG + j, a:a + rows], w["ident"])
                        last.then_inc(done, 1)

                def hidden(k, slot):
                    pe.wait_ge(s_moved, k + 1)
                    pe.wait_ge(gate_ready, k)
                    nc.tensor.matmul(pG[:], c["s"][:, 128:256], sT[:, slot], start=True, stop=True).then_inc(g_mm, 1)
                    pe.wait_ge(hid_ready, k)
                    nc.tensor.matmul(pH[:], c["s"][:, 0:128], sT[:, slot], start=True, stop=True).then_inc(hid_mm, 1)
                    pe.wait_ge(v_moved, k + 1)
                    pe.wait_ge(f_ready, k)
                    nc.tensor.matmul(p0[:], c["v0"], vT[:, slot], start=True, stop=True)
                    nc.tensor.matmul(p1[:], c["v1"], vT[:, slot], start=True, stop=True).then_inc(fv_mm, 1)

                def output(k, slot):
                    pe.wait_ge(hid_ready, k + 1)
                    pe.wait_ge(f_ready, k + 1)
                    pe.wait_ge(o_ready, FG * k)
                    for j in range(FG):
                        at = slice(j * P, (j + 1) * P)
                        out = pO[:, j // 2, (j % 2) * D:(j % 2 + 1) * D]
                        nc.tensor.matmul(out[:, 0:C0], hid[:, slot, at], c["o"], start=True, stop=True)
                        nc.tensor.matmul(out[:, C0:D], f0[:, slot, at], c["ov0"], start=False, stop=True, skip_group_check=True)
                        nc.tensor.matmul(out, f1[:, slot, at], c["ov1"], start=False, stop=True,
                                         skip_group_check=True).then_inc(o_mm, 1)

                def step(s, b, front, back):
                    turn(2 * s, s, b, 0)
                    if back:
                        hidden(2 * s - 1, 1)
                        output(2 * s - 2, 0)
                    turn(2 * s + 1, s, b, 1)
                    hidden(2 * s, 0)
                    if back:
                        output(2 * s - 1, 1)

                steps(pe, step)
                hidden(HALVES - 1, 1)
                output(HALVES - 2, 0)
                output(HALVES - 1, 1)

            @block.scalar
            def _(act):
                def move(k, slot):
                    act.wait_ge(s_turned, k + 1)
                    nc.scalar.copy(sT[:, slot], pS[:]).then_inc(s_moved, 1)
                    act.wait_ge(v_turned, k + 1)
                    if not known(k, 0, 2):
                        act.wait_ge(fv_mm, k - 1)
                    nc.scalar.copy(vT[:, slot], pV[:]).then_inc(v_moved, 1)

                def gates(k, slot):
                    act.wait_ge(g_mm, k + 1)
                    if not known(k, 0, 2):
                        act.wait_ge(f_ready, k - 1)
                        act.wait_ge(o_mm, FG * (k - 1))
                    nc.scalar.activation(gate[:, slot], pG[:], ACT.Tanh, scale=0.5).then_inc(gate_ready, 1)
                    act.wait_ge(hid_mm, k + 1)
                    nc.scalar.activation(hid[:, slot], pH[:], ACT.Silu).then_inc(hid_ready, 1)

                def relu(n, b):
                    act.wait_ge(negm_ready, n + 1)
                    act.wait_ge(y_ready, N2 * n)
                    for j in range(N2):
                        nc.scalar.activation(u[:, j], x[:, b, j], ACT.Relu, bias=negm[:, j:j + 1]).then_inc(u_ready, 1)

                def vectors(n, b):
                    act.wait_ge(scale_ready, n + 1)
                    if not known(n, 0, 2):
                        act.wait_ge(v_turned, 2 * n - 2)
                    for j in range(N2):
                        nc.scalar.activation(norm[:, b, j, C0 + 1:], y[:, b, j, C0:D], ACT.Copy,
                                             scale=r2[:, 1, j:j + 1]).then_inc(nv_ready, 1)

                def step(s, b, front, back):
                    move(2 * s, 0)
                    if front:
                        relu(s + 1, 1 - b)
                    if back:
                        gates(2 * s - 1, 1)
                    move(2 * s + 1, 1)
                    gates(2 * s, 0)
                    if front:
                        vectors(s + 1, 1 - b)

                relu(0, 0)
                vectors(0, 0)
                steps(act, step)
                gates(HALVES - 1, 1)


def build(nc, io, N_ROWS, T):
    with ExitStack() as ctx:
        sb = lambda n, s, dt=F32: ctx.enter_context(nc.sbuf_tensor(n, s, dt))
        w = {}
        for key, table in (("all", W_ALL), ("l0", W0), ("l1", W1), ("ff", W2)):
            tile = sb(f"weights_{key}", [P, offsets(table)[1]])
            w["t_" + key] = tile[:]
            w[key] = views(tile, table)
        w["ident"], w["low"] = w["all"]["ident"], w["all"]["low"]
        w["mrow0"], w["mrow1"] = sb("message_bias0", [1, D])[:], sb("message_bias1", [1, D])[:]
        flags = {n: sb(n, [P, T + EG], I32) for n in ("src", "dst", "row")}
        flags |= {n: sb(n, [P, T]) for n in ("same", "nxt", "first", "last", "mid")}
        flags |= {n: sb(n, [P, 1]) for n in ("head", "tail", "tail_row")}
        flags["tail_at"] = sb("tail_at", [P, 1], I32)
        flags["tt"] = sb("tails_equal", [P, P])
        flags["y0"] = sb("edge_y", [P, T, 4])
        flags["ones"] = sb("ones", [1, P])
        w["ones"] = flags["ones"]
        io["rows"] = N_ROWS
        prepare(nc, io, w, flags, T)
        nodes(nc, io, w, N_ROWS // (P * NG))
        for layer in range(2):
            with ExitStack() as own:
                H = (4, 8)[layer]
                logits = own.enter_context(nc.sbuf_tensor(f"logits{layer}", [P, T, H], F32))
                vals = own.enter_context(nc.sbuf_tensor(f"vals{layer}", [P, T, D], F32))
                edges(nc, io, w, flags, T, layer, vals, logits)
                softmax(nc, w, flags, T, layer, logits)
                scatter(nc, io, w, flags, T, layer, vals, logits)
        feed(nc, io, w, N_ROWS // (P * 2 * FG))


def place(table, parts):
    at, cols = offsets(table)
    out = np.zeros((P, cols), np.float32)
    for name, pieces in parts.items():
        a, rows, n = at[name]
        for r, c, m in pieces:
            m = np.asarray(m)
            m = m.reshape(-1, 1) if m.ndim == 1 else m
            assert r + m.shape[0] <= rows and c + m.shape[1] <= n, name
            out[r:r + m.shape[0], a + c:a + c + m.shape[1]] = m
    return out


def by_component(m, rows="cd", cols="dc", comps=(0, 1, 2)):
    C, K = m.shape
    n = len(comps)
    out = np.zeros((C, 3, n, K), np.float32)
    for at, d in enumerate(comps):
        out[:, d, at, :] = m
    if rows == "dc":
        out = out.transpose(1, 0, 2, 3)
    if cols == "cd":
        out = out.transpose(0, 1, 3, 2)
    out = out.reshape(3 * C, n * K)
    return out


def value_rows(H, ps, pv):
    SW, VW = C0 // H, C1 // H
    out = np.zeros((H, D // H, D), np.float32)
    out[:, 0:SW, 0:C0] = ps.reshape(H, SW, C0)
    for d in range(3):
        out[:, SW + d * VW:SW + (d + 1) * VW, C0 + d::3] = pv.reshape(H, VW, C1)
    return out.reshape(D, D)


def input_rows(s_src, s_dst, v_src, v_dst):
    out = np.zeros((2 * D, D), np.float32)
    for k, (s, v) in enumerate(((s_src, v_src), (s_dst, v_dst))):
        out[k * D:k * D + C0, 0:C0] = s
        out[k * D + C0:(k + 1) * D, C0:D] = by_component(v)
    return out


def columns(s, v):
    one = np.concatenate([s, np.repeat(v, 3)])
    return np.concatenate([one, one])


def cut(rows):
    return {k: rows[a:b] for k, (a, b) in enumerate(((0, 128), (128, 256), (256, 320)))}


def kernel(**inputs):
    import concourse.bacc as bacc
    from concourse.bass_utils import run_bass_kernel_spmd as run

    a = {k: np.ascontiguousarray(v) for k, v in inputs.items()}
    N, E = a["x"].shape[0], a["src"].shape[0]
    unit = P * max(NG, 2 * FG)
    N_ROWS = -(-N // unit) * unit
    T = -(-E // (P * EG)) * EG
    E_ROWS = P * T
    assert N_ROWS > N
    f32 = np.float32
    L0 = {k[7:]: v for k, v in a.items() if k.startswith("L0_gnn_")}
    L1 = {k[7:]: v for k, v in a.items() if k.startswith("L1_gnn_")}

    def padded(m, rows, fill=0):
        out = np.full((rows, *m.shape[1:]), fill, m.dtype)
        out[:m.shape[0]] = m
        return out

    def by_tile(m):
        return np.ascontiguousarray(padded(m, E_ROWS).reshape(P, T, -1).transpose(2, 1, 0).reshape(m.shape[1], -1))

    spread2 = lambda v: np.broadcast_to(v, (P, v.shape[-1]))
    none = np.zeros(C1, f32)
    in0, g0, b0 = (cut(m) for m in (input_rows(L0["Ws_src"], L0["Ws_dst"], L0["Wv_src"], L0["Wv_dst"]),
                                    columns(L0["gamma_s"], L0["gamma_v"]), columns(L0["beta_s"], none)))
    in1, g1, b1 = (cut(m) for m in (input_rows(L1["msrc_ws"], L1["mdst_ws"], L1["msrc_wv"], L1["mdst_wv"]),
                                    columns(L1["ln1_w0"], L1["ln1_w1"]), columns(L1["ln1_b0"], none)))
    wv, wl, wlin = L0["Wv_val"], L0["Wv_vlin"], L1["lin_wv"]
    val0 = np.concatenate([L0["W_alpha"], L0["Ws_val"]], 1)
    svT = L0["Ws_val"].T
    p0, p1 = value_rows(4, L0["Wps"], L0["Wpv"]), value_rows(8, L1["proj_ws"], L1["proj_wv"])
    diag = lambda m: by_component(m, "dc", "dc")
    w_l0 = place(W0, {
        **{f"in{k}": [(0, 0, in0[k])] for k in range(3)}, **{f"gam{k}": [(0, 0, g0[k])] for k in range(3)},
        **{f"beta{k}": [(0, 0, b0[k])] for k in range(3)}, "rad": [(0, 0, L0["W_rbf"])],
        "first": [(64, 0, wv[0:64]), (0, C1, val0[0:64])], "second": [(96, 0, val0[64:96]), (0, 160, diag(wv[64:96]))],
        "svT": [(0, 0, svT[:, 0:64]), (0, 96, svT[:, 64:96])], "wg": [(0, 0, L0["Wg"])],
        "third": [(0, 0, diag(wv[96:128]))],
        "out0": [(0, 0, L0["Ws_vlin"][0:64]), (0, 64, wl[0:64]), (96, 96, L0["Ws_vlin"][64:96])],
        "out0s": [(0, 0, np.broadcast_to(L0["w2_ss"][:, None], (C0, C0))), (0, 64, np.broadcast_to(L0["w2_sv"][:, None], (C0, C1)))],
        "dots": [(96, 0, L0["w2_vv0"])], "out1": [(0, 0, diag(wl[64:96])), (0, CV, diag(wl[96:128]))],
        "b2s": [(0, 0, np.tile(L0["w2_vs"], 3))], "c2s": [(0, 0, np.tile(L0["w2_vv1"], 3))],
        "p0": [(0, 0, p0[0:128])], "p1": [(0, 0, p0[128:160])], "dot": [(0, 0, spread2(L0["alpha_dot"].reshape(1, -1)))]})
    w_l1 = place(W1, {
        **{f"in{k}": [(0, 0, in1[k])] for k in range(3)}, **{f"gam{k}": [(0, 0, g1[k])] for k in range(3)},
        **{f"beta{k}": [(0, 0, b1[k])] for k in range(3)}, "mbias": [(0, 0, L1["mdst_bs"][None])],
        "r1": [(0, 0, L1["rw1"]), (64, 0, L1["rb1"][None])], "r2": [(0, 0, L1["rw2"]), (64, 0, L1["rb2"][None])],
        "rad": [(0, 0, L1["rw3"]), (64, 0, L1["roff"][None])],
        **{k: [(0, 0, L1[k])] for k in ("rg1", "rbe1", "rg2", "rbe2")},
        "first": [(64, 0, wlin[0:64]), (0, C1, L1["lin_ws"][0:64])],
        "second": [(96, 0, L1["lin_ws"][64:96]), (0, P, diag(wlin[64:96]))],
        "sbias": [(0, 0, L1["lin_bs"][None])], "third": [(0, 0, diag(wlin[96:128]))],
        "p0": [(0, 0, p1[0:128])], "p1": [(0, 0, p1[128:160])], "dot": [(0, 0, spread2(L1["alpha_dot"].reshape(1, -1)))],
        "fill": [(0, 0, spread2(L1["proj_bs"][None]))]})
    f1s, f1v, f2v = np.concatenate([L1["f1_ws"], L1["f1_ws"][:, 128:]], 1), L1["f1_wv"], L1["f2_wv"]
    f1b = np.concatenate([L1["f1_bs"], L1["f1_bs"][128:]])
    pick = by_component(f1v, "cd", "dc")
    back = by_component(f2v, "dc", "cd")
    w_ff = place(W2, {
        "s": [(0, 0, f1s), (64, 0, f1b[None])], "gs": [(0, 0, L1["ln2_w0"])],
        "b0": [(0, 64, L1["ln2_b0"]), (64, 64, np.ones((1, 1), f32))],
        "v0": [(0, 0, pick[:, 0:128])], "v1": [(0, 0, pick[:, 128:192])], "gv": [(0, 0, np.repeat(L1["ln2_w1"], 3))],
        "o": [(0, 0, L1["f2_ws"])], "ov0": [(0, 0, back[0:128])],
        "ov1": [(0, C0, back[128:192]), (64, 0, L1["f2_bs"][None])]})
    w_all = place(W_ALL, {"ident": [(0, 0, np.eye(P, dtype=f32))], "low": [(0, 0, np.tril(np.ones((P, P), f32), -1))]})

    arrays = dict(
        x=padded(a["x"], N_ROWS), a0=padded(a["node_vec1"], N_ROWS),
        src=padded(a["src"], E_ROWS, N).reshape(P, T), dst=padded(a["dst"], E_ROWS, N).reshape(P, T),
        attr16=by_tile(a["edge_attr_16"]), attr64=by_tile(a["edge_attr_64"]),
        attr4=padded(a["edge_attr_4"], E_ROWS).reshape(P, T, 4), attr3=padded(a["edge_attr_3"], E_ROWS).reshape(P, T, 3),
        w_all=w_all, w_l0=w_l0, w_l1=w_l1, w_ff=w_ff)
    nc = bacc.Bacc("TRN2", target_bir_lowering=False, num_devices=1)
    io = {}
    for name, m in arrays.items():
        io[name] = nc.dram_tensor(f"in_{name}", m.shape, mybir.dt.from_np(m.dtype), kind="ExternalInput").ap()
    for name in ("x1", "g", "agg"):
        io[name] = nc.dram_tensor(f"table_{name}", (N_ROWS, D), F32).ap()
    io["out"] = nc.dram_tensor("out", (N_ROWS, D), F32, kind="ExternalOutput").ap()
    build(nc, io, N_ROWS, T)
    got = run(nc, [{f"in_{k}": m for k, m in arrays.items()}], core_ids=[0]).results[0]["out"]
    return got[:N]
```

```python
from contextlib import ExitStack

import numpy as np

import concourse.bass as bass
from concourse import mybir

F32 = mybir.dt.float32
I32 = mybir.dt.int32
U32 = mybir.dt.uint32
ALU = mybir.AluOpType
ACT = mybir.ActivationFunctionType
AX_X = mybir.AxisListType.X

P = 128
C0, C1 = 64, 32
CV = 3 * C1
D = C0 + CV
WN = 2 * C0 + 3 * C1
EG = 4
NG = 8
FG = 4
RING = 2
EPS = 1e-5
BIG = 1e30
SKIP = 1e6
SQRT3 = float(np.sqrt(3.0))
SQRT2 = float(np.sqrt(2.0))
RSQRT_SEED = 1597463007.0
M0, M1 = 128, 64


W0 = dict(in0=(P, D), in1=(P, D), in2=(64, D), beta0=(P, 1), beta1=(P, 1), beta2=(64, 1), gam0=(P, 1),
          gam1=(P, 1), gam2=(64, 1), rad=(16, WN), first=(P, C1 + 160), second=(P, 160 + CV), third=(CV, CV), svT=(C0, P), wg=(C0, C1),
          out0=(P, 160), out0s=(C0, C0 + C1), dots=(P, 1), out1=(CV, 2 * CV), b2s=(CV, 1), c2s=(CV, 1), p0=(P, D), p1=(32, D), dot=(P, C0))
W1 = dict(in0=(P, D), in1=(P, D), in2=(64, D), beta0=(P, 1), beta1=(P, 1), beta2=(64, 1), gam0=(P, 1),
          gam1=(P, 1), gam2=(64, 1), mbias=(1, D), r1=(65, 64), r2=(65, 64), rad=(65, WN), rg1=(64, 1),
          rbe1=(64, 1), rg2=(64, 1), rbe2=(64, 1), first=(P, C1 + P), second=(P, P + CV), third=(CV, CV), sbias=(1, P),
          p0=(P, D), p1=(32, D), dot=(P, C0), fill=(P, D))
W2 = dict(s=(65, 256), gs=(65, 1), b0=(65, 65), v0=(CV, 128), v1=(CV, 64), gv=(CV, 1), o=(M0, C0),
          ov0=(P, CV), ov1=(65, D))
W_ALL = dict(ident=(P, P), low=(P, P))


def offsets(table):
    at, out = 0, {}
    for name, (rows, cols) in table.items():
        out[name] = (at, rows, cols)
        at += cols
    return out, at


def views(tile, table):
    return {n: tile[0:r, a:a + c] for n, (a, r, c) in offsets(table)[0].items()}


class Tick:

    def __init__(self, eng, sem, step=0, per_step=0, before=0):
        self.eng, self.sem, self.step, self.per_step, self.before = eng, sem, step, per_step, before
        self.n = 0

    def mark(self, instruction):
        instruction.then_inc(self.sem, 1)
        self.n += 1
        return self.n

    def wait(self, n):
        self.eng.wait_ge(self.sem, self.step * self.per_step + (self.before + n))

    def link(self, instruction):
        self.wait(self.mark(instruction))

    def done(self):
        self.wait(self.n)

    def close(self):
        assert self.n == self.per_step, (self.n, self.per_step)


def spread(ap, shape):
    return ap.to_broadcast(shape)


def moments(nc, t, stats, n, mean, var, tmp):
    last = None
    a = t.mark(nc.vector.tensor_tensor(tmp[0], stats[:, :, 1], stats[:, :, 4], ALU.subtract))
    b = t.mark(nc.vector.tensor_tensor(tmp[1], stats[:, :, 2], stats[:, :, 5], ALU.add))
    c = t.mark(nc.vector.tensor_tensor(mean, stats[:, :, 1], stats[:, :, 4], ALU.add))
    t.wait(a)
    d = t.mark(nc.vector.scalar_tensor_tensor(tmp[2], tmp[0], 0.25, tmp[0], ALU.mult, ALU.mult))
    t.wait(c)
    t.mark(nc.vector.tensor_scalar(mean, mean, 0.5, None, ALU.mult))
    if not isinstance(n, int):
        t.link(nc.vector.tensor_tensor(tmp[1], tmp[1], n, ALU.mult))
        return t.mark(nc.vector.tensor_tensor(var, tmp[1], tmp[2], ALU.add))
    t.wait(d)
    last = t.mark(nc.vector.scalar_tensor_tensor(var, tmp[1], 1.0 / n, tmp[2], ALU.mult, ALU.add))
    return last


MOMENTS = 6


def rsqrt(nc, t, y, v, tmp, ready, between=None, count=FG):
    at = 0

    def link(instruction):
        nonlocal at
        n = t.mark(instruction)
        if between and at < count:
            between(at)
            at += 1
        t.wait(n)

    link(nc.vector.tensor_scalar(y.bitcast(I32), v.bitcast(I32), -0.5, RSQRT_SEED, ALU.mult, ALU.add))
    for n in range(3):
        link(nc.vector.tensor_tensor(tmp, y, y, ALU.mult))
        link(nc.vector.scalar_tensor_tensor(tmp, tmp, -0.5, v, ALU.mult, ALU.mult))
        step = nc.vector.scalar_tensor_tensor(y, tmp, 1.5, y, ALU.add, ALU.mult)
        if n < 2:
            link(step)
    step.then_inc(ready, 1)


RSQRT = 9


def prepare(nc, io, w, flags, T):
    with ExitStack() as ctx:
        sem = lambda n: ctx.enter_context(nc.semaphore(n))
        loaded, vec, pe_done = sem("prep_loaded"), sem("prep_vec"), sem("prep_pe")
        ps = ctx.enter_context(nc.psum_tensor("prep_ps", [P, 3, 512], F32))
        dstf = ctx.enter_context(nc.sbuf_tensor("dstf", [P, T], F32))
        end = ctx.enter_context(nc.sbuf_tensor("endf", [P, T], F32))
        a, b, c = w["l0"], w["l1"], w["ff"]
        N_IN = 16 * 7
        with nc.Block() as block:
            @block.sync
            def _(sp):
                sp.dma_start(w["t_all"], io["w_all"]).then_inc(loaded, 16)
                sp.dma_start(w["t_l0"], io["w_l0"]).then_inc(loaded, 16)
                sp.dma_start(w["t_l1"], io["w_l1"]).then_inc(loaded, 16)
                sp.dma_start(w["t_ff"], io["w_ff"]).then_inc(loaded, 16)
                sp.dma_start(flags["src"][:, 0:T], io["src"]).then_inc(loaded, 16)
                sp.dma_start(flags["dst"][:, 0:T], io["dst"]).then_inc(loaded, 16)
                sp.dma_start(flags["y0"][:], io["attr4"]).then_inc(loaded, 16)

            @block.tensor
            def _(pe):
                pe.wait_ge(loaded, N_IN)
                for n, l in enumerate((a, b)):
                    for k in range(3):
                        last = nc.tensor.matmul(ps[0:1, n, 0:D], l[f"beta{k}"], l[f"in{k}"], start=(k == 0), stop=(k == 2))
                last.then_inc(pe_done, 1)
                nc.tensor.matmul(ps[:, 2, 0:C1], a["svT"], a["wg"], start=True, stop=True).then_inc(pe_done, 1)
                pe.wait_ge(vec, 2)
                nc.tensor.matmul(ps[0:65, 0, 0:256], c["b0"], c["s"], start=True, stop=True).then_inc(pe_done, 1)

            @block.vector
            def _(dve):
                t = Tick(dve, vec, 0, 0)
                v = nc.vector
                dve.wait_ge(loaded, N_IN)
                dve.wait_ge(pe_done, 1)
                t.mark(v.tensor_copy(w["mrow0"], ps[0:1, 0, 0:D]))
                t.mark(v.tensor_tensor(w["mrow1"], ps[0:1, 1, 0:D], b["mbias"], ALU.add))
                for l in (a, b):
                    for k in range(3):
                        t.mark(v.tensor_scalar(l[f"in{k}"], l[f"in{k}"], l[f"gam{k}"], None, ALU.mult))
                dve.wait_ge(pe_done, 2)
                t.mark(v.tensor_copy(a["first"][0:64, C1 + 128:], ps[0:64, 2, 0:C1]))
                t.link(v.tensor_copy(a["second"][96:128, 128:160], ps[96:128, 2, 0:C1]))
                m = a["second"][96:128, 0:160]
                t.mark(v.tensor_scalar(m, m, 1.0 / SQRT3, None, ALU.mult))
                t.mark(v.tensor_scalar(a["third"], a["third"], 1.0 / SQRT2, None, ALU.mult))
                m = a["out0"][0:64, 0:C0 + C1]
                t.mark(v.tensor_tensor(m, m, a["out0s"], ALU.mult))
                m = a["out0"][96:128, C0 + C1:]
                t.mark(v.tensor_scalar(m, m, a["dots"][96:128], 1.0 / SQRT3, ALU.mult, ALU.mult))
                m = a["out1"][:, 0:CV]
                t.mark(v.tensor_scalar(m, m, a["b2s"], None, ALU.mult))
                m = a["out1"][:, CV:]
                t.mark(v.tensor_scalar(m, m, a["c2s"], 1.0 / SQRT2, ALU.mult, ALU.mult))
                m = b["first"][64:128, 0:C1]
                t.mark(v.tensor_scalar(m, m, SQRT3, None, ALU.mult))
                t.mark(v.tensor_scalar(b["third"], b["third"], SQRT3 / SQRT2, None, ALU.mult))
                t.mark(v.tensor_scalar(b["dot"], b["dot"], 0.4, None, ALU.mult))
                dve.wait_ge(pe_done, 3)
                t.mark(v.tensor_scalar(c["s"][0:64], c["s"][0:64], c["gs"][0:64], None, ALU.mult))
                t.mark(v.tensor_copy(c["s"][64:65], ps[64:65, 0, 0:256]))
                t.mark(v.tensor_scalar(c["v0"], c["v0"], c["gv"], None, ALU.mult))
                t.mark(v.tensor_scalar(c["v1"], c["v1"], c["gv"], None, ALU.mult))
                t.mark(v.tensor_scalar(c["ov0"], c["ov0"], 0.5, None, ALU.mult))
                t.mark(v.tensor_scalar(c["ov1"][0:64], c["ov1"][0:64], 0.5, None, ALU.mult))
                d, src = flags["dst"], flags["src"]
                t.mark(v.memset(d[:, T:T + EG], 0))
                t.mark(v.memset(src[:, T:T + EG], 0))
                t.mark(v.memset(flags["same"][:, 0:1], 0.0))
                t.mark(v.memset(flags["nxt"][:, T - 1:T], 0.0))
                t.link(v.tensor_copy(dstf[:], d[:, 0:T]))
                t.mark(v.tensor_tensor(flags["same"][:, 1:T], dstf[:, 1:T], dstf[:, 0:T - 1], ALU.is_equal))
                t.mark(v.tensor_tensor(flags["nxt"][:, 0:T - 1], dstf[:, 1:T], dstf[:, 0:T - 1], ALU.is_equal))
                t.mark(v.tensor_scalar(flags["first"][:], dstf[:], dstf[:, 0:1], None, ALU.is_equal))
                t.link(v.tensor_scalar(flags["last"][:], dstf[:], dstf[:, T - 1:T], None, ALU.is_equal))
                t.link(v.tensor_tensor(flags["mid"][:], flags["first"][:], flags["last"][:], ALU.max))
                t.link(v.tensor_scalar(flags["mid"][:], flags["mid"][:], -1.0, 1.0, ALU.mult, ALU.add))
                t.link(v.tensor_tensor(end[:], flags["first"][:], flags["last"][:], ALU.mult))
                t.link(v.tensor_tensor(flags["last"][:], flags["last"][:], end[:], ALU.subtract))
                t.link(v.tensor_scalar(end[:], flags["nxt"][:], SKIP, None, ALU.mult))
                t.link(v.memset(end[:, T - 1:T], SKIP))
                t.link(v.tensor_tensor(flags["row"][:, 0:T], end[:], dstf[:], ALU.add))
                t.mark(v.tensor_copy(flags["tail"][:], dstf[:, T - 1:T]))
                t.mark(v.tensor_copy(flags["head"][:], dstf[:, 0:1]))
                t.mark(v.memset(flags["ones"][:], 1.0))


def nodes(nc, io, w, N_STEPS):
    with ExitStack() as ctx:
        sb = lambda n, s: ctx.enter_context(nc.sbuf_tensor(n, s, F32))
        sem = lambda n: ctx.enter_context(nc.semaphore(n))
        x = sb("n_x", [P, 2, NG, D])
        u = sb("n_u", [P, NG, D])
        x1 = sb("n_x1", [P, NG, D])
        g = sb("n_g", [P, NG, D])
        fill = sb("n_fill", [P, NG, D])
        stats = sb("n_stats", [P, NG, 6])
        stat2 = sb("n_stat2", [P, 2, NG, 6])
        mean, negm, var = sb("n_mean", [P, NG]), sb("n_negm", [P, NG]), sb("n_var", [P, NG])
        mean2, var2 = sb("n_mean2", [P, NG]), sb("n_var2", [P, NG])
        mean3, var3 = sb("n_mean3", [P, NG]), sb("n_var3", [P, NG])
        e = sb("n_e", [P, 3, NG])
        r = sb("n_r", [P, 3, NG])
        tmp = sb("n_tmp", [P, 4, 3 * NG])
        x_in = [sem("n_x_in0"), sem("n_x_in1")]
        vec, filled, fill_out = sem("n_vec"), sem("n_filled"), sem("n_fill_out")
        negm_ready, u_ready, gv_ready = sem("n_negm_ready"), sem("n_u_ready"), sem("n_gv_ready")
        r_ready, out_ready = sem("n_r_ready"), sem("n_out_ready")
        x1_out, g_out = sem("n_x1_out"), sem("n_g_out")
        grp = lambda a: a.rearrange("(g p j) c -> g p j c", p=P, j=NG)
        xs, x1s, gs, aggs = grp(io["x"]), grp(io["x1"]), grp(io["g"]), grp(io["agg"])
        STEP = NG + MOMENTS + 1 + 2 * NG + 2 * MOMENTS + 5 + RSQRT
        PAIRS = N_STEPS // 2
        ODD = N_STEPS % 2
        tmps = lambda k: [tmp[:, i, 0:k] for i in range(4)]

        with nc.Block() as block:
            @block.sync
            def _(sp):
                def load(step, b):
                    sp.dma_start(x[:, b], xs[step]).then_inc(x_in[b], 16)

                def store(step):
                    sp.wait_ge(out_ready, step + 1)
                    sp.dma_start(x1s[step], x1[:]).then_inc(x1_out, 16)
                    sp.wait_ge(gv_ready, step + 1)
                    sp.dma_start(gs[step], g[:]).then_inc(g_out, 16)
                    sp.dma_start(aggs[step], fill[:]).then_inc(fill_out, 16)

                load(0, 0)
                load(1, 1)
                sp.wait_ge(filled, NG)
                with sp.Fori(0, PAIRS - 1) as i:
                    for b in range(2):
                        store(2 * i + b)
                        load(2 * i + b + 2, b)
                store(2 * PAIRS - 2)
                if ODD:
                    load(2 * PAIRS, 0)
                store(2 * PAIRS - 1)
                if ODD:
                    store(2 * PAIRS)
                sp.wait_ge(x1_out, 16 * N_STEPS)
                sp.wait_ge(g_out, 16 * N_STEPS)
                sp.wait_ge(fill_out, 16 * N_STEPS)

            def act_step(act, step, b):
                act.wait_ge(gv_ready, step)
                act.wait_ge(negm_ready, step + 1)
                for j in range(NG):
                    k = nc.scalar.activation(u[:, j], x[:, b, j], ACT.Relu, bias=negm[:, j:j + 1])
                    k.then_inc(u_ready, 1)
                act.wait_ge(r_ready, step + 1)
                act.wait_ge(g_out, 16 * step)
                for j in range(NG):
                    k = nc.scalar.activation(g[:, j, C0:D], u[:, j, C0:D], ACT.Copy, scale=r[:, 2, j:j + 1])
                k.then_inc(gv_ready, 1)

            def dve_step(dve, step, b, half):
                v = nc.vector
                t = Tick(dve, vec, step, STEP)
                dve.wait_ge(out_ready, step)
                dve.wait_ge(x_in[b], 16 * half + 16)
                for j in range(NG):
                    k = t.mark(v.bn_stats(stats[:, j], x[:, b, j]))
                t.wait(k)
                k = moments(nc, t, stats[:], D, mean[:], var[:], tmps(NG))
                t.wait(k)
                t.mark(v.tensor_scalar(e[:, 0], var[:], EPS, None, ALU.add))
                v.tensor_scalar(negm[:], mean[:], -1.0, None, ALU.mult).then_inc(negm_ready, 1)
                for j in range(NG):
                    dve.wait_ge(u_ready, NG * step + j + 1)
                    t.mark(v.bn_stats(stat2[:, 0, j], u[:, j, 0:C0]))
                    k = t.mark(v.bn_stats(stat2[:, 1, j], u[:, j, C0:D]))
                t.wait(k)
                moments(nc, t, stat2[:, 0], C0, mean2[:], var2[:], tmps(NG))
                k = moments(nc, t, stat2[:, 1], CV, mean3[:], var3[:], [tmp[:, i, NG:2 * NG] for i in range(4)])
                t.wait(k)
                t.link(v.tensor_tensor(tmp[:, 3, 0:NG], mean3[:], mean3[:], ALU.mult))
                t.mark(v.scalar_tensor_tensor(e[:, 1], e[:, 0], EPS, var2[:], ALU.mult, ALU.add))
                t.mark(v.tensor_scalar(e[:, 2], e[:, 0], EPS, None, ALU.mult))
                t.link(v.tensor_tensor(tmp[:, 3, 0:NG], tmp[:, 3, 0:NG], var3[:], ALU.add))
                t.link(v.scalar_tensor_tensor(e[:, 2], tmp[:, 3, 0:NG], 3.0, e[:, 2], ALU.mult, ALU.add))
                flat = lambda a: a.rearrange("p a b -> p (a b)")
                rsqrt(nc, t, flat(r[:]), flat(e[:]), tmp[:, 0], r_ready)
                t.close()
                dve.wait_ge(r_ready, step + 1)
                dve.wait_ge(x1_out, 16 * step)
                for j in range(NG):
                    v.scalar_tensor_tensor(x1[:, j], u[:, j], r[:, 0, j:j + 1], x[:, b, j], ALU.mult, ALU.add)
                dve.wait_ge(g_out, 16 * step)
                for j in range(NG):
                    k = v.tensor_scalar(g[:, j, 0:C0], u[:, j, 0:C0], mean2[:, j:j + 1], r[:, 1, j:j + 1],
                                        ALU.subtract, ALU.mult)
                k.then_inc(out_ready, 1)

            @block.scalar
            def _(act):
                with act.Fori(0, PAIRS) as i:
                    for b in range(2):
                        act_step(act, 2 * i + b, b)
                if ODD:
                    act_step(act, N_STEPS - 1, 0)

            @block.vector
            def _(dve):
                for j in range(NG):
                    nc.vector.tensor_copy(fill[:, j], w["l1"]["fill"]).then_inc(filled, 1)
                with dve.Fori(0, PAIRS) as i:
                    for b in range(2):
                        dve_step(dve, 2 * i + b, b, i)
                if ODD:
                    dve_step(dve, N_STEPS - 1, 0, PAIRS)


def edges(nc, io, w, flags, T, layer, vals, logits):
    H = (4, 8)[layer]
    SW, VW = C0 // H, C1 // H
    STEPS = T // EG
    KINDS = ("CBA", "BA")[layer]
    U = EG * len(KINDS)
    LAST_KIND = KINDS[0]
    K = 2 * EG
    l = w[("l0", "l1")[layer]]
    table = io[("g", "x1")[layer]]
    RADK = (16, 65)[layer]
    mrow = w[f"mrow{layer}"]
    with ExitStack() as ctx:
        name = lambda n: f"e{layer}_{n}"
        sb = lambda n, s, dt=F32: ctx.enter_context(nc.sbuf_tensor(name(n), s, dt))
        pb = lambda n, s: ctx.enter_context(nc.psum_tensor(name(n), s, F32))
        sem = lambda n: ctx.enter_context(nc.semaphore(name(n)))
        rows = sb("rows", [P, K, D])
        index = sb("index", [P, K], I32)
        yg, ny = sb("yg", [P, 3 * EG, 4]), sb("ny", [P, 3 * EG, 4])
        rad_in = sb("rad_in", [RADK, EG * P])
        turned = sb("turned", [P, len(KINDS), RING, 3 * P])
        msg = sb("msg", [P, RING, D])
        prod = sb("prod", [P, EG, 384])
        act_a = sb("act_a", [P, EG, C0])
        value = sb("value", [P, EG, D])
        acc_b, acc_c = sb("acc_b", [P, CV]), sb("acc_c", [P, CV])
        dot = sb("dot", [P, C1])
        tp = pb("tp", [P, RING, 512])
        mm = pb("mm", [P, RING, 512])
        o1 = pb("o1", [P, RING, 512])
        if layer == 0:
            normed = rows
            o2 = pb("o2", [P, RING, 512])
            val = sb("val", [P, EG, 224])
            val_ready, hc_ready = sem("val_ready"), sem("hc_ready")
        else:
            u, normed = sb("u", [P, K, D]), sb("normed", [P, K, D])
            hz = pb("hz", [P, 2, EG * 64])
            zt = pb("zt", [64, EG * P])
            h1, h2 = sb("h1", [65, EG * P]), sb("h2", [65, EG * P])
            z = sb("z", [P, EG, 64])
            stats = sb("stats", [P, K, 6])
            stat2 = sb("stat2", [P, 2, K, 6])
            mean, negm, var = sb("mean", [P, K]), sb("negm", [P, K]), sb("var", [P, K])
            mz, vz, rz = sb("mz", [P, EG]), sb("vz", [P, EG]), sb("rz", [P, EG])
            mean2, var2 = sb("mean2", [P, 2, K]), sb("var2", [P, 2, K])
            share = sb("share", [P, 2 * K])
            e, r, tmp = sb("e", [P, 2, K]), sb("r", [P, 2, K]), sb("tmp", [P, 4, 2 * K])
            edge_vec = sb("edge_vec", [P, T, 3])
            negm_ready, u_ready, ns_ready, nv_ready = sem("negm_ready"), sem("u_ready"), sem("ns_ready"), sem("nv_ready")
            h_ready, z_ready, zt_ready, ht_ready = sem("h_ready"), sem("z_ready"), sem("zt_ready"), sem("ht_ready")
            r_ready = sem("r_ready")
        gathered = [sem(f"gathered{j}") for j in range(EG)]
        rad_ready, pool_gate, index_ready = sem("rad_ready"), sem("pool_gate"), sem("index_ready")
        tp_ready, mm_ready = {k: sem("tp_ready" + k) for k in KINDS}, {k: sem("mm_ready" + k) for k in KINDS}
        tp_moved, msg_ready, prod_ready, ab_ready = sem("tp_moved"), sem("msg_ready"), sem("prod_ready"), sem("ab_ready")
        value_ready, kept, logit_ready = sem("value_ready"), sem("kept"), sem("logit_ready")
        vec, zeroed, gate_pe = sem("vec"), sem("zeroed"), sem("gate_pe")
        y_ready, yg_ready = sem("y_ready"), sem("yg_ready")

        TWO = 2
        S0, SN = C1, (160, 128)[layer]
        B0 = S0 + SN

        def heads(j):
            return value[:, j].rearrange("p (h c) -> p h c", h=H)

        LAG = {"A": 0, "B": 1, "C": 2}
        DEPTH = len(KINDS)

        def kinds_at(g):
            return "".join(k for k in KINDS if 0 <= g - LAG[k] < STEPS)

        def units_before(g):
            return EG * sum(len(kinds_at(i)) for i in range(g))

        def groups(i, start):
            return {"A": i + start, "B": i + (start - 1), "C": i + (start - 2) if start > 1 or isinstance(i, int) else None,
                    "N": i + (start + 1), "since": i}

        def next_group(at, kind):
            return at[{"A": "N", "B": "A", "C": "B"}[kind]]

        LOOPED = range(DEPTH - 1, STEPS if layer == 0 else STEPS - 1)

        def run_steps(run, body):
            first = lambda g: kinds_at(g)[0] if kinds_at(g) else None
            for g in range(LOOPED.start):
                body(groups(g, 0), units_before(g), kinds_at(g), True, first(g + 1))
            with run.Fori(0, len(LOOPED)) as i:
                body(groups(i, LOOPED.start), i * U + units_before(LOOPED.start), KINDS, True, KINDS[0])
            for g in range(LOOPED.stop, STEPS + DEPTH - 1):
                body(groups(g, 0), units_before(g), kinds_at(g), False, first(g + 1))

        def units(kinds):
            return [(k, j) for j in range(EG) for k in kinds]

        with nc.Block() as block:
            @block.sync
            def _(sp):
                def load(g):
                    if layer == 0:
                        sp.dma_start(rad_in[:], io["attr16"][:, bass.ds(g * (EG * P), EG * P)]).then_inc(rad_ready, 16)
                    else:
                        sp.dma_start(rad_in[0:64], io["attr64"][:, bass.ds(g * (EG * P), EG * P)]).then_inc(rad_ready, 16)

                if layer == 1:
                    sp.dma_start(edge_vec[:], io["attr3"]).then_inc(y_ready, 16)
                load(0)
                with sp.Fori(0, STEPS - 1) as g:
                    if layer == 0:
                        sp.wait_ge(mm_ready["A"], EG * g + EG + TWO)
                    else:
                        sp.wait_ge(h_ready, 2 * g + 1)
                    load(g + 1)

            @block.gpsimd
            def _(pool):
                def hold(s, value):
                    pool.wait_ge(s, value)
                    pool.sem_inc(pool_gate, 1)

                bound = pool.to_reg(io["rows"] - 1)
                with pool.Fori(0, STEPS) as g:
                    for j in range(EG):
                        hold(gathered[j], 32 * g)
                    nc.gpsimd.tensor_copy(index[:, 0:EG], flags["src"][:, bass.ds(g * EG, EG)]).then_inc(index_ready, 1)
                    nc.gpsimd.tensor_copy(index[:, EG:K], flags["dst"][:, bass.ds(g * EG, EG)]).then_inc(index_ready, 1)
                    hold(index_ready, 2 * g + 2)
                    for j in range(EG):
                        if layer == 0:
                            hold(tp_ready["A"], EG * g + j + 1)
                        else:
                            hold(u_ready, K * g + 2 * j + 2)
                        for s in range(2):
                            at = index[:, s * EG + j:s * EG + j + 1].bitcast(U32)
                            nc.gpsimd.indirect_dma_start(rows[:, 2 * j + s], None, table,
                                                         bass.IndirectOffsetOnAxis(ap=at, axis=0),
                                                         bounds_check=bound).then_inc(gathered[j], 16)

            @block.tensor
            def _(pe):
                for k in KINDS:
                    pe.sem_inc(tp_ready[k], EG)
                    pe.sem_inc(mm_ready[k], TWO)
                pe.wait_ge(zeroed, 4)

                def turn(g, j, kind, n, slot):
                    pe.wait_ge(tp_moved, n + 1)
                    if kind == "A":
                        if layer == 0:
                            pe.wait_ge(gathered[j], 32 * g + 32)
                        else:
                            pe.wait_ge(ns_ready, K * g + 2 * j + 2)
                            pe.wait_ge(nv_ready, K * g + 2 * j + 2)
                        src, cuts = normed[:, 2 * j:2 * j + 2].rearrange("p s c -> p (s c)"), (0, 128, 256, 320)
                    elif kind == "B":
                        pe.wait_ge(prod_ready, EG * g + j + 1 + TWO)
                        src, cuts = prod[:, j], (0, 128, 256, 352)
                    else:
                        pe.wait_ge(val_ready, EG * g + j + 1 + TWO)
                        src, cuts = val[:, j], (0, 128, 224)
                    for c in range(len(cuts) - 1):
                        m = cuts[c + 1] - cuts[c]
                        last = nc.tensor.transpose(tp[0:m, slot, c * P:(c + 1) * P], src[:, cuts[c]:cuts[c + 1]], w["ident"])
                    last.then_inc(tp_ready[kind], 1)

                def multiply(g, j, kind, n):
                    q = j % RING
                    T0, T1, T2 = (turned[:, KINDS.index(kind), q, c * P:(c + 1) * P] for c in range(3))
                    pe.wait_ge(tp_moved, n + 1 + TWO)
                    if kind == "A":
                        if j == 0 and layer == 0:
                            pe.wait_ge(rad_ready, 16 * g + 16)
                        if j == 0 and layer == 1:
                            pe.wait_ge(ht_ready, 2 * g + 2)
                        pe.wait_ge(prod_ready, EG * g + j + 1)
                        o = mm[:, q]
                        nc.tensor.matmul(o[:, 0:D], T0, l["in0"], start=True, stop=False)
                        nc.tensor.matmul(o[:, 0:D], T1, l["in1"], start=False, stop=False)
                        nc.tensor.matmul(o[:, 0:D], T2[0:64], l["in2"], start=False, stop=False)
                        nc.tensor.matmul(o[:, 0:D], flags["ones"][0:1, :], mrow, start=False, stop=True)
                        rad_t = rad_in if layer == 0 else h2
                        last = nc.tensor.matmul(o[:, D:D + WN], rad_t[:, j * P:(j + 1) * P], l["rad"], start=True, stop=True)
                    elif kind == "B":
                        pe.wait_ge(val_ready if layer == 0 else value_ready, EG * g + j + 1)
                        o = o1[:, q]
                        nc.tensor.matmul(o[:, 0:B0], T0, l["first"], start=True, stop=True)
                        nc.tensor.matmul(o[:, S0:B0 + CV], T1, l["second"], start=False, stop=True, skip_group_check=True)
                        if layer == 1:
                            nc.tensor.matmul(o[:, S0:B0], flags["ones"][0:1, :], l["sbias"], start=False, stop=True,
                                             skip_group_check=True)
                        last = nc.tensor.matmul(o[:, B0 + CV:B0 + 2 * CV], T2[0:CV], l["third"], start=False, stop=True,
                                                skip_group_check=True)
                    else:
                        pe.wait_ge(value_ready, EG * g + j + 1)
                        o = o2[:, q]
                        nc.tensor.matmul(o[:, 0:160], T0, l["out0"], start=True, stop=True)
                        last = nc.tensor.matmul(o[:, 160:352], T1[0:CV], l["out1"], start=True, stop=True)
                    last.then_inc(mm_ready[kind], 1)

                def hidden(g, n):
                    pe.wait_ge(z_ready, 2 * g + n)
                    if n == 0:
                        pe.wait_ge(rad_ready, 16 * g + 16)
                    else:
                        pe.wait_ge(ht_ready, 2 * g + 1)
                    inp, wt = ((rad_in, l["r1"]), (h1, l["r2"]))[n]
                    for j in range(EG):
                        last = nc.tensor.matmul(hz[:, n, j * 64:(j + 1) * 64], inp[:, j * P:(j + 1) * P], wt, start=True, stop=True)
                    last.then_inc(h_ready, 1)

                def turn_hidden(g, n):
                    pe.wait_ge(z_ready, 2 * g + n + 1)
                    pe.sem_inc(gate_pe, 1)
                    pe.wait_ge(ht_ready, 2 * g + n)
                    pe.sem_inc(gate_pe, 1)
                    for j in range(EG):
                        last = nc.tensor.transpose(zt[:, j * P:(j + 1) * P], z[:, j], w["ident"])
                    last.then_inc(zt_ready, 1)

                def body(at, base, kinds, norm, ahead):
                    todo = units(kinds)
                    for i, (kind, j) in enumerate(todo):
                        if layer == 1 and norm and kind == kinds[0]:
                            if j % 2 == 0:
                                hidden(at["N"], j // 2)
                            else:
                                turn_hidden(at["N"], j // 2)
                        if i + 1 < len(todo):
                            k, jj = todo[i + 1]
                            turn(at[k], jj, k, base + (i + 1), (i + 1) % RING)
                        elif ahead:
                            turn(next_group(at, ahead), 0, ahead, base + len(todo), 0)
                        multiply(at[kind], j, kind, base + i)

                if layer == 1:
                    for n in range(2):
                        hidden(0, n)
                        turn_hidden(0, n)
                turn(0, 0, "A", 0, 0)
                run_steps(pe, body)

            @block.scalar
            def _(act):
                act.sem_inc(tp_moved, TWO)
                if layer == 1:
                    act.sem_inc(u_ready, K)

                def move(g, j, kind, n, slot):
                    cols = (2 if kind == "C" else 3) * P
                    act.wait_ge(tp_ready[kind], EG * g + j + 1 + EG)
                    act.wait_ge(mm_ready[kind], EG * g + j + 1)
                    nc.scalar.copy(turned[:, KINDS.index(kind), j % RING, 0:cols], tp[:, slot, 0:cols]).then_inc(tp_moved, 1)

                def after(g, j, kind):
                    act.wait_ge(mm_ready[kind], EG * g + j + 1 + TWO)
                    if kind == "A":
                        act.wait_ge(prod_ready, EG * g + j + 1)
                        nc.scalar.copy(msg[:, j % RING], mm[:, j % RING, 0:D]).then_inc(msg_ready, 1)
                    elif kind == "B":
                        o = o1[:, j % RING]
                        act.wait_ge(logit_ready, g)
                        if layer == 0:
                            act.wait_ge(tp_ready["C"], EG * g + j + 1)
                            nc.scalar.activation(act_a[:, j], o[:, S0:S0 + C0], ACT.Copy, scale=0.2)
                            nc.scalar.activation(val[:, j, 0:96], o[:, S0 + C0:B0], ACT.Sigmoid).then_inc(ab_ready, 1)
                        else:
                            act.wait_ge(kept, g)
                            nc.scalar.activation(act_a[:, j], o[:, S0:S0 + C0], ACT.Tanh, scale=0.5)
                            nc.scalar.copy(heads(j)[:, :, 0:SW], o[:, S0 + C0:B0].rearrange("p (h c) -> p h c", h=H)).then_inc(ab_ready, 1)
                    else:
                        act.wait_ge(kept, g)
                        act.wait_ge(yg_ready, g + (LAG["C"] + 1))
                        nc.scalar.activation(heads(j)[:, :, 0:SW], o2[:, j % RING, 0:C0].rearrange("p (h c) -> p h c", h=H),
                                             ACT.Copy, scale=yg[:, j, 0:1]).then_inc(hc_ready, 1)

                def gates(g, n):
                    act.wait_ge(zt_ready, 2 * g + n + 1)
                    if n:
                        act.wait_ge(mm_ready["A"], EG * g + TWO)
                    h = (h1, h2)[n]
                    nc.scalar.activation(h[0:64], zt[:], ACT.Silu, bias=l[f"rbe{n + 1}"], scale=l[f"rg{n + 1}"]).then_inc(ht_ready, 1)

                def relu(g):
                    act.wait_ge(negm_ready, g + 1)
                    act.wait_ge(ns_ready, K * g)
                    for k in range(K):
                        nc.scalar.activation(u[:, k], rows[:, k], ACT.Relu, bias=negm[:, k:k + 1]).then_inc(u_ready, 1)

                def vectors(g):
                    act.wait_ge(r_ready, 3 * g + 3)
                    for k in range(K):
                        if k % 2 == 0:
                            act.wait_ge(tp_ready["A"], EG * g + k // 2 + 1)
                        nc.scalar.activation(normed[:, k, C0:D], u[:, k, C0:D], ACT.Copy, scale=r[:, 1, k:k + 1]).then_inc(nv_ready, 1)

                def body(at, base, kinds, norm, ahead):
                    todo = units(kinds)
                    for i, (kind, j) in enumerate(todo):
                        if i + 1 < len(todo):
                            k, jj = todo[i + 1]
                            move(at[k], jj, k, base + (i + 1), (i + 1) % RING)
                        elif ahead:
                            move(next_group(at, ahead), 0, ahead, base + len(todo), 0)
                        after(at[kind], j, kind)
                        if layer == 1 and norm and kind == "A":
                            if j == 1:
                                relu(at["N"])
                                gates(at["N"], 0)
                            if j == 3:
                                gates(at["N"], 1)
                                vectors(at["N"])

                act.wait_ge(zeroed, 4)
                if layer == 1:
                    relu(0)
                    gates(0, 0)
                    gates(0, 1)
                    vectors(0)
                move(0, 0, "A", 0, 0)
                run_steps(act, body)

            @block.vector
            def _(dve):
                v = nc.vector
                dve.sem_inc(prod_ready, TWO)
                dve.sem_inc(value_ready, TWO)
                if layer == 0:
                    dve.sem_inc(val_ready, TWO)
                for q in range(RING):
                    v.memset(tp[:, q], 0.0).then_inc(zeroed, 1)
                y, before = flags["y0"], 0
                if layer == 0:
                    v.memset(dot[:], 0.0).then_inc(zeroed, 2)
                else:
                    v.memset(share[:, 0:K], 1.0 / C0)
                    v.memset(share[:, K:], 1.0 / CV)
                    v.memset(h1[64:65], 1.0)
                    v.memset(h2[64:65], 1.0)
                    v.memset(rad_in[64:65], 1.0).then_inc(zeroed, 2)
                    dve.wait_ge(y_ready, 16)
                    t = Tick(dve, vec, 0, 0)
                    yy = edge_vec
                    sq, ln, length, inverse, spare = y[:, :, 0], *(logits[:, :, n] for n in range(4))
                    t.link(v.tensor_tensor(sq, yy[:, :, 0], yy[:, :, 0], ALU.mult))
                    for c in (1, 2):
                        t.link(v.tensor_tensor(ln, yy[:, :, c], yy[:, :, c], ALU.mult))
                        t.link(v.tensor_tensor(sq, sq, ln, ALU.add))
                    t.link(v.tensor_scalar(length, sq, 1e-12, None, ALU.add))
                    rsqrt(nc, t, inverse, length, spare, r_ready)
                    dve.wait_ge(r_ready, 1)
                    for c in range(3):
                        t.mark(v.tensor_tensor(y[:, :, c + 1], yy[:, :, c], inverse, ALU.mult))
                    t.wait(t.n)
                    before = t.n

                vec3 = lambda a: a.rearrange("p (d c) -> p d c", d=3)
                wide = lambda a: a.unsqueeze(1).to_broadcast([P, 3, C1])

                class Vectors:

                    def __init__(self, t, acc, o, cols, at, outs):
                        self.t, self.acc, self.o, self.cols, self.at, self.outs = t, acc, o, cols, at, outs
                        self.y, self.ny = yg[:, at], ny[:, at]

                    def outer(self):
                        a = self.cols[0]
                        self.n = self.t.mark(v.tensor_tensor(vec3(self.acc[:]), wide(self.o[:, a:a + C1]),
                                                             self.y[:, 1:4].unsqueeze(2).to_broadcast([P, 3, C1]), ALU.mult))

                    def plus(self):
                        self.t.wait(self.n)
                        B, acc = self.o[:, self.cols[1]:self.cols[1] + CV], self.acc[:]
                        if layer == 0:
                            self.n = self.t.mark(v.scalar_tensor_tensor(acc, B, self.y[:, 0:1], acc, ALU.mult, ALU.add))
                        else:
                            self.n = self.t.mark(v.tensor_tensor(acc, B, acc, ALU.add))

                    def turns(self, d, sign, out):
                        m = self.cols[2] + ((d + (1 if sign else 2)) % 3) * C1
                        k = 1 + (d + (2 if sign else 1)) % 3
                        return v.scalar_tensor_tensor(out, self.o[:, m:m + C1], (self.y if sign else self.ny)[:, k:k + 1],
                                                      vec3(self.acc[:])[:, d], ALU.mult, ALU.add)

                    def cross(self):
                        self.t.wait(self.n)
                        for d in range(3):
                            self.n = self.t.mark(self.turns(d, True, vec3(self.acc[:])[:, d]))

                    def minus(self):
                        for d in range(3):
                            self.t.wait(self.n - 2 + d)
                            step = self.turns(d, False, self.outs(d))
                            if d < 2:
                                self.t.mark(step)
                        return step

                VECTORS = 7

                def dots(out, m, at, c):
                    s, part = yg[:, at, c + 1:c + 2], m[:, c * C1:(c + 1) * C1]
                    if c == 0:
                        return v.tensor_scalar(out, part, s, None, ALU.mult)
                    return v.scalar_tensor_tensor(out, part, s, out, ALU.mult, ALU.add)

                def tile(t, at, j, kinds):
                    b = Vectors(t, acc_b, o1[:, j % RING], (0, B0, B0 + CV), EG + j,
                                (lambda d: acc_b[:, d * C1:(d + 1) * C1]) if layer == 0 else
                                (lambda d: heads(j)[:, :, SW + d * VW:SW + (d + 1) * VW])) if "B" in kinds else None
                    c = Vectors(t, acc_c, o2[:, j % RING], (64, 160, 256), j,
                                lambda d: heads(j)[:, :, SW + d * VW:SW + (d + 1) * VW]) if "C" in kinds else None
                    a = "A" in kinds
                    if c:
                        dve.wait_ge(hc_ready, EG * at["C"] + j + 1)
                        dve.wait_ge(value_ready, EG * at["C"] + j + TWO)
                        t.mark(v.tensor_tensor(heads(j)[:, :, 0:SW], c.o[:, 96:160].rearrange("p (h c) -> p h c", h=H),
                                               heads(j)[:, :, 0:SW], ALU.add))
                        c.outer()
                    if b:
                        dve.wait_ge(ab_ready, EG * at["B"] + j + 1)
                        scalars = b.o[:, S0:S0 + C0]
                        if layer == 0:
                            t.mark(v.tensor_tensor(act_a[:, j], act_a[:, j], scalars, ALU.max))
                        else:
                            dve.wait_ge(value_ready, EG * at["B"] + j + TWO)
                            t.mark(v.scalar_tensor_tensor(act_a[:, j], act_a[:, j], 1.5, scalars, ALU.add, ALU.mult))
                        b.outer()
                    if c:
                        c.plus()
                    if b:
                        b.plus()
                    if a:
                        dve.wait_ge(msg_ready, EG * at["A"] + j + 1)
                        dve.wait_ge(tp_ready["B"], EG * at["A"] + j + 1)
                        dve.wait_ge(prod_ready, EG * at["A"] + j + TWO)
                        m, ww, x = msg[:, j % RING], mm[:, j % RING, D:D + 256], prod[:, j]
                        ms, mv = m[:, 0:C0], m[:, C0:D]
                        k = t.mark(dots(dot[:], mv, 2 * EG + j, 0))
                    if c:
                        c.cross()
                    if b:
                        b.cross()
                    if a:
                        t.wait(k)
                        k = t.mark(dots(dot[:], mv, 2 * EG + j, 1))
                    if c:
                        c.minus().then_inc(value_ready, 1)
                    if b:
                        step = b.minus()
                        if layer == 0:
                            z = t.mark(step)
                            dve.wait_ge(tp_ready["C"], EG * at["B"] + j + 1)
                        else:
                            step.then_inc(value_ready, 1)
                    if a:
                        t.wait(k)
                        k = t.mark(dots(dot[:], mv, 2 * EG + j, 2))
                        if layer == 0:
                            v.scalar_tensor_tensor(x[:, 0:C0], ww[:, 0:C0], yg[:, 2 * EG + j, 0:1], ms, ALU.mult, ALU.mult)
                    if b and layer == 0:
                        t.wait(z)
                        vectors = val[:, j, 128:224]
                        z = t.mark(v.tensor_tensor(vec3(vectors), vec3(acc_b[:]), wide(val[:, j, 64:96]), ALU.mult))
                    if a:
                        if layer == 0:
                            v.tensor_tensor(x[:, C0:2 * C0], ww[:, C0:2 * C0], ms, ALU.mult)
                        else:
                            v.tensor_tensor(x[:, 0:2 * C0].rearrange("p (n c) -> p n c", n=2), ww[:, 0:2 * C0].rearrange("p (n c) -> p n c", n=2),
                                            ms.unsqueeze(1).to_broadcast([P, 2, C0]), ALU.mult)
                    if b and layer == 0:
                        t.wait(z)
                        z = t.mark(dots(val[:, j, 96:128], vectors, EG + j, 0))
                    if a:
                        out = x[:, 128:384].rearrange("p (n q) -> p n q", n=2)[:, :, 0:CV].rearrange("p n (d c) -> p n d c", d=3)
                        by = ww[:, 128:256].rearrange("p (n q) -> p n q", n=2)[:, :, 0:C1].unsqueeze(2).to_broadcast([P, 2, 3, C1])
                        v.tensor_tensor(out, by, vec3(mv).unsqueeze(1).to_broadcast([P, 2, 3, C1]), ALU.mult)
                    if b and layer == 0:
                        t.wait(z)
                        z = t.mark(dots(val[:, j, 96:128], vectors, EG + j, 1))
                    if a:
                        t.wait(k)
                        v.tensor_tensor(x[:, 224:256], ww[:, 160:192], dot[:], ALU.mult).then_inc(prod_ready, 1)
                    if b and layer == 0:
                        t.wait(z)
                        dots(val[:, j, 96:128], vectors, EG + j, 2).then_inc(val_ready, 1)

                TILE = {"A": 3, "B": 1 + VECTORS + (4 if layer == 0 else 0), "C": 1 + VECTORS}

                def row_moments(t, g):
                    for k in range(K):
                        if k % 2 == 0:
                            dve.wait_ge(gathered[k // 2], 32 * g + 32)
                        n = t.mark(v.bn_stats(stats[:, k], rows[:, k]))
                    t.wait(n)
                    t.wait(moments(nc, t, stats[:], D, mean[:], var[:], [tmp[:, i, 0:K] for i in range(4)]))
                    v.tensor_scalar(negm[:], mean[:], -1.0, None, ALU.mult).then_inc(negm_ready, 1)
                    t.mark(v.tensor_scalar(var[:], var[:], EPS, EPS, ALU.add, ALU.mult))

                def row_factors(t, g):
                    flat = lambda a: a.rearrange("p a b -> p (a b)")
                    for k in range(K):
                        dve.wait_ge(u_ready, K * g + k + 1 + K)
                        t.mark(v.bn_stats(stat2[:, 0, k], u[:, k, 0:C0]))
                        m = t.mark(v.bn_stats(stat2[:, 1, k], u[:, k, C0:D]))
                    t.wait(m)
                    t.wait(moments(nc, t, stat2[:].rearrange("p i k c -> p (i k) c"), share[:], flat(mean2[:]), flat(var2[:]),
                                   [tmp[:, i] for i in range(4)]))
                    m = t.mark(v.tensor_tensor(tmp[:, 3, 0:K], mean2[:, 1], mean2[:, 1], ALU.mult))
                    t.link(v.tensor_tensor(e[:], var2[:], var[:].unsqueeze(1).to_broadcast([P, 2, K]), ALU.add))
                    t.link(v.tensor_tensor(e[:, 1], e[:, 1], tmp[:, 3, 0:K], ALU.add))
                    dve.wait_ge(nv_ready, K * g)
                    rsqrt(nc, t, flat(r[:]), flat(e[:]), tmp[:, 0], r_ready)

                def row_scalars(g):
                    dve.wait_ge(r_ready, 3 * g + 3)
                    for k in range(K):
                        if k % 2 == 0:
                            dve.wait_ge(tp_ready["A"], EG * g + k // 2 + 1)
                        v.tensor_scalar(normed[:, k, 0:C0], u[:, k, 0:C0], mean2[:, 0, k:k + 1], r[:, 0, k:k + 1],
                                        ALU.subtract, ALU.mult).then_inc(ns_ready, 1)

                def layer_norm(t, g, n):
                    dve.wait_ge(h_ready, 2 * g + n + 1)
                    for j in range(EG):
                        k = t.mark(v.bn_stats(stats[:, j], hz[:, n, j * 64:(j + 1) * 64]))
                    t.wait(k)
                    t.wait(moments(nc, t, stats[:, 0:EG], 64, mz[:], vz[:], [tmp[:, i, 0:EG] for i in range(4)]))
                    t.link(v.tensor_scalar(vz[:], vz[:], EPS, None, ALU.add))
                    rsqrt(nc, t, rz[:], vz[:], tmp[:, 0, 0:EG], r_ready)
                    dve.wait_ge(r_ready, 3 * g + (2, 4)[n])
                    dve.wait_ge(zt_ready, 2 * g + n)
                    for j in range(EG):
                        m = v.tensor_scalar(z[:, j], hz[:, n, j * 64:(j + 1) * 64], mz[:, j:j + 1], rz[:, j:j + 1],
                                            ALU.subtract, ALU.mult)
                    m.then_inc(z_ready, 1)

                def norms(t, g, part):
                    if part == 0:
                        layer_norm(t, g, 0)
                    elif part == 1:
                        row_moments(t, g)
                    elif part == 2:
                        row_factors(t, g)
                    else:
                        layer_norm(t, g, 1)

                NORMS = 0 if layer == 0 else (2 * (EG + MOMENTS + 1 + RSQRT) + K + MOMENTS + 1
                                              + 2 * K + (MOMENTS + 1) + 3 + RSQRT)
                SUMS = 1

                def ticks(kinds, norm):
                    return 1 + EG * sum(TILE[k] for k in kinds) + (NORMS if norm else 0) + (SUMS if "B" in kinds else 0)

                def norm_at(g):
                    return layer == 1 and g < STEPS - 1

                ahead_ticks = before + NORMS
                def ticks_before(g):
                    return ahead_ticks + sum(ticks(kinds_at(i), norm_at(i)) for i in range(g))

                def body(at, base, kinds, norm, ahead):
                    g, peeled = at["A"], isinstance(base, int)
                    if peeled:
                        t = Tick(dve, vec, 0, 0, ticks_before(g))
                    else:
                        t = Tick(dve, vec, at["since"], ticks(kinds, norm), ticks_before(LOOPED.start))
                    if not peeled or g > 0:
                        dve.wait_ge(prod_ready, EG * (min(g, STEPS) if peeled else g) + TWO)
                        if layer == 0:
                            dve.wait_ge(val_ready, EG * at["B"] + TWO)
                    lo = max(3 - DEPTH, 2 - g) if peeled else 3 - DEPTH
                    hi = min(3, STEPS - g + 2) if peeled else 3
                    part = slice(lo * EG, hi * EG)
                    t.link(v.tensor_copy(yg[:, part], y[:, bass.ds(at["CBA"[lo]] * EG, (hi - lo) * EG), :]))
                    v.tensor_scalar(ny[:, part], yg[:, part], -1.0, None, ALU.mult).then_inc(yg_ready, 1)
                    dve.wait_ge(yg_ready, g + 1)
                    for j in range(EG):
                        if norm and layer == 1:
                            norms(t, at["N"], j)
                        tile(t, at, j, kinds)
                    if "B" in kinds:
                        k = t.mark(v.tensor_tensor(act_a[:], act_a[:], l["dot"].unsqueeze(1).to_broadcast([P, EG, C0]), ALU.mult))
                    if LAST_KIND in kinds:
                        done = at[LAST_KIND]
                        dve.wait_ge(value_ready, EG * done + EG + TWO)
                        v.tensor_copy(vals[:, bass.ds(done * EG, EG), :], value[:]).then_inc(kept, 1)
                    if "B" in kinds:
                        t.wait(k)
                        v.tensor_reduce(logits[:, bass.ds(at["B"] * EG, EG), :], act_a[:].rearrange("p j (h c) -> p j h c", h=H),
                                        AX_X, ALU.add).then_inc(logit_ready, 1)
                    assert t.n == ticks(kinds, norm and layer == 1), (t.n, ticks(kinds, norm))
                    if norm and layer == 1:
                        row_scalars(at["N"])

                if layer == 1:
                    t = Tick(dve, vec, 0, 0, before)
                    for part in range(4):
                        norms(t, 0, part)
                    assert t.n == NORMS
                    row_scalars(0)
                run_steps(dve, body)


def softmax(nc, w, flags, T, layer, logits):
    H = (4, 8)[layer]
    DEN_EPS = (1e-16, 1e-12)[layer]
    with ExitStack() as ctx:
        name = lambda n: f"s{layer}_{n}"
        sb = lambda n, s, dt=F32: ctx.enter_context(nc.sbuf_tensor(name(n), s, dt))
        sem = lambda n: ctx.enter_context(nc.semaphore(name(n)))
        fwd, total = sb("fwd", [P, T, H]), sb("total", [P, T, H])
        neg_same, neg_nxt, ends = sb("neg_same", [P, T]), sb("neg_nxt", [P, T]), sb("ends", [P, T])
        edge = sb("edge", [P, 2, H])
        wide = sb("wide", [P, 2 * H, P])
        keys = sb("keys", [P, 2, P])
        eq, neg_eq = sb("eq", [P, 2, 2, P]), sb("neg_eq", [P, 2, 2, P])
        work = sb("work", [P, H, P])
        part = sb("part", [P, 2, 2, H])
        whole = sb("whole", [P, 2, H])
        open_ = sb("open", [P, 1])
        turned = ctx.enter_context(nc.psum_tensor(name("turned"), [P, 2 * H, P], F32))
        keys_t = ctx.enter_context(nc.psum_tensor(name("keys_t"), [P, 2, P], F32))
        vec, wide_ready, turned_ready = sem("vec"), sem("wide_ready"), sem("turned_ready")
        shifted, exp_ready = sem("shifted"), sem("exp_ready")
        ths = [P, T, H]

        with nc.Block() as block:
            @block.tensor
            def _(pe):
                for n in range(3):
                    pe.wait_ge(wide_ready, n + 1)
                    src, out = (keys, keys_t) if n == 0 else (wide, turned)
                    for k in range(2 if n == 0 else 2 * H):
                        last = nc.tensor.transpose(out[:, k], src[:, k], w["ident"])
                    last.then_inc(turned_ready, 1)

            @block.scalar
            def _(act):
                act.wait_ge(shifted, 1)
                nc.scalar.activation(logits[:].rearrange("p t h -> p (t h)"), fwd[:].rearrange("p t h -> p (t h)"),
                                     ACT.Exp).then_inc(exp_ready, 1)

            @block.vector
            def _(dve):
                v = nc.vector
                t = Tick(dve, vec)
                first, last, mid = flags["first"], flags["last"], flags["mid"]
                for n, key in enumerate(("head", "tail")):
                    k = v.tensor_copy(keys[:, n], flags[key][:].to_broadcast([P, P]))
                k.then_inc(wide_ready, 1)
                t.mark(v.tensor_scalar(neg_same[:], flags["same"][:], 1.0, BIG, ALU.subtract, ALU.mult))
                t.mark(v.tensor_scalar(neg_nxt[:], flags["nxt"][:], 1.0, BIG, ALU.subtract, ALU.mult))
                t.mark(v.tensor_scalar(ends[:], flags["nxt"][:], -1.0, 1.0, ALU.mult, ALU.add))
                t.mark(v.tensor_scalar(open_[:], first[:, T - 1:T], -1.0, 1.0, ALU.mult, ALU.add))
                dve.wait_ge(turned_ready, 1)
                for q, key in enumerate(("head", "tail")):
                    for n in range(2):
                        t.mark(v.tensor_scalar(eq[:, q, n], keys_t[:, n], flags[key][:], None, ALU.is_equal))
                t.done()
                t.mark(v.tensor_scalar(neg_eq[:], eq[:], 1.0, BIG, ALU.subtract, ALU.mult))
                if layer == 0:
                    t.mark(v.tensor_copy(flags["tt"][:], eq[:, 1, 1]))
                    t.link(v.tensor_tensor(work[:, 0], eq[:, 1, 1], w["low"], ALU.mult))
                    t.link(v.tensor_reduce(flags["tail_row"][:], work[:, 0], AX_X, ALU.max))
                    t.link(v.scalar_tensor_tensor(open_[:], flags["tail_row"][:], SKIP, flags["tail"][:], ALU.mult, ALU.add))
                    t.link(v.tensor_copy(flags["tail_at"][:], open_[:]))
                    t.link(v.tensor_scalar(open_[:], first[:, T - 1:T], -1.0, 1.0, ALU.mult, ALU.add))

                def across(nth, op_mask, masks, op):
                    v.tensor_copy(wide[:].rearrange("p (n h) c -> p n h c", n=2),
                                  edge[:].unsqueeze(3).to_broadcast([P, 2, H, P])).then_inc(wide_ready, 1)
                    dve.wait_ge(turned_ready, nth)
                    for q in range(2):
                        for n in range(2):
                            t.link(v.tensor_tensor(work[:], turned[:, n * H:(n + 1) * H],
                                                   masks[:, q, n].unsqueeze(1).to_broadcast([P, H, P]), op_mask))
                            t.link(v.tensor_reduce(part[:, q, n], work[:], AX_X, op))
                    t.link(v.tensor_tensor(whole[:], part[:, :, 0], part[:, :, 1], op))

                def combine():
                    bc = lambda f: f[:].unsqueeze(2).to_broadcast(ths)
                    t.link(v.tensor_tensor(total[:], total[:], bc(mid), ALU.mult))
                    for q, f in enumerate((first, last)):
                        t.link(v.tensor_tensor(fwd[:], whole[:, q].unsqueeze(1).to_broadcast(ths), bc(f), ALU.mult))
                        t.link(v.tensor_tensor(total[:], total[:], fwd[:], ALU.add))

                for h in range(H):
                    k = t.mark(v.tensor_tensor_scan(fwd[:, :, h], neg_same[:], logits[:, :, h], -BIG, ALU.add, ALU.max))
                for h in range(H):
                    t.wait(k - H + 1 + h)
                    t.mark(v.tensor_tensor_scan(total[:, ::-1, h], neg_nxt[:, ::-1], fwd[:, ::-1, h], -BIG, ALU.add, ALU.max))
                t.done()
                t.mark(v.tensor_copy(edge[:, 0], total[:, 0]))
                t.link(v.tensor_copy(edge[:, 1], total[:, T - 1]))
                across(2, ALU.add, neg_eq, ALU.max)
                combine()
                v.tensor_tensor(fwd[:], logits[:], total[:], ALU.subtract).then_inc(shifted, 1)
                dve.wait_ge(exp_ready, 1)
                for h in range(H):
                    t.mark(v.tensor_tensor_scan(fwd[:, :, h], flags["same"][:], logits[:, :, h], 0.0, ALU.mult, ALU.add))
                t.done()
                t.link(v.tensor_tensor(fwd[:], fwd[:], ends[:].unsqueeze(2).to_broadcast(ths), ALU.mult))
                for h in range(H):
                    t.mark(v.tensor_tensor_scan(total[:, ::-1, h], flags["nxt"][:, ::-1], fwd[:, ::-1, h], 0.0, ALU.mult, ALU.add))
                t.done()
                t.mark(v.tensor_scalar(edge[:, 0], total[:, 0], open_[:], None, ALU.mult))
                t.link(v.tensor_copy(edge[:, 1], total[:, T - 1]))
                across(3, ALU.mult, eq, ALU.add)
                combine()
                t.link(v.tensor_scalar(total[:], total[:], DEN_EPS, None, ALU.add))
                t.link(v.reciprocal(total[:], total[:]))
                t.link(v.tensor_tensor(logits[:], logits[:], total[:], ALU.mult))


def scatter(nc, io, w, flags, T, layer, vals, alpha):
    H = (4, 8)[layer]
    STEPS = T // EG
    l = w[("l0", "l1")[layer]]
    table = io[("x1", "agg")[layer]]
    with ExitStack() as ctx:
        name = lambda n: f"a{layer}_{n}"
        sb = lambda n, s, dt=F32: ctx.enter_context(nc.sbuf_tensor(name(n), s, dt))
        pb = lambda n, s: ctx.enter_context(nc.psum_tensor(name(n), s, F32))
        sem = lambda n: ctx.enter_context(nc.semaphore(name(n)))
        weighted = sb("weighted", [P, EG, D])
        sums = sb("sums", [P, EG, D])
        merged = sb("merged", [P, D])
        same = sb("same", [P, EG])
        index = sb("index", [P, EG], I32)
        turned = sb("turned", [P, RING, 2 * P])
        rows = sb("rows", [P, EG, D])
        tp, out = pb("tp", [P, RING, 512]), pb("out", [P, RING, 512])
        vec, zeroed, sum_ready, tp_ready = sem("vec"), sem("zeroed"), sem("sum_ready"), sem("tp_ready")
        tp_moved, out_ready, row_ready = sem("tp_moved"), sem("out_ready"), sem("row_ready")
        index_ready, pool_gate = sem("index_ready"), sem("pool_gate")
        written = [sem(f"written{j}") for j in range(EG)]
        tails_ready, merged_ready, tails_written = sem("tails_ready"), sem("merged_ready"), sem("tails_written")
        tiles = EG * STEPS

        with nc.Block() as block:
            @block.gpsimd
            def _(pool):
                def hold(s, value):
                    pool.wait_ge(s, value)
                    pool.sem_inc(pool_gate, 1)

                bound = pool.to_reg(io["rows"] - 1)
                with pool.Fori(0, STEPS) as g:
                    for j in range(EG):
                        hold(written[j], 16 * g)
                        nc.gpsimd.tensor_copy(index[:, j:j + 1], flags["row"][:, bass.ds(g * EG + j, 1)]).then_inc(index_ready, 1)
                    for j in range(EG):
                        hold(index_ready, EG * g + j + 1)
                        hold(row_ready, EG * g + j + 1 + RING)
                        nc.gpsimd.indirect_dma_start(table, bass.IndirectOffsetOnAxis(ap=index[:, j:j + 1].bitcast(U32), axis=0),
                                                     rows[:, j], None, bounds_check=bound, oob_is_err=False,
                                                     compute_op=ALU.add).then_inc(written[j], 16)
                for j in range(EG):
                    pool.wait_ge(written[j], 16 * STEPS)
                pool.wait_ge(row_ready, tiles + 1 + RING)
                nc.gpsimd.indirect_dma_start(table, bass.IndirectOffsetOnAxis(ap=flags["tail_at"][:].bitcast(U32), axis=0),
                                             rows[:, 0], None, bounds_check=bound, oob_is_err=False,
                                             compute_op=ALU.add).then_inc(tails_written, 16)
                pool.wait_ge(tails_written, 16)

            @block.tensor
            def _(pe):
                pe.sem_inc(tp_ready, EG)

                def turn(i, j, src):
                    pe.wait_ge(tp_moved, i + 1)
                    for c, (a, b) in enumerate(((0, 128), (128, 160))):
                        last = nc.tensor.transpose(tp[0:b - a, j % RING, c * P:(c + 1) * P], src[:, a:b], w["ident"])
                    last.then_inc(tp_ready, 1)

                def turn_sums(g, j):
                    pe.wait_ge(sum_ready, EG * g + j + 1)
                    turn(EG * g + j, j, sums[:, j])

                def project(i, j):
                    pe.wait_ge(tp_moved, i + 1 + RING)
                    pe.wait_ge(row_ready, i + 1)
                    nc.tensor.matmul(out[:, j % RING, 0:D], turned[:, j % RING, 0:P], l["p0"], start=True, stop=False)
                    nc.tensor.matmul(out[:, j % RING, 0:D], turned[0:32, j % RING, P:2 * P], l["p1"],
                                     start=False, stop=True).then_inc(out_ready, 1)

                pe.wait_ge(zeroed, 3)
                turn_sums(0, 0)
                with pe.Fori(0, STEPS - 1) as g:
                    for j in range(EG):
                        turn_sums(g + (j + 1) // EG, (j + 1) % EG)
                        project(EG * g + j, j)
                for j in range(EG - 1):
                    turn_sums(STEPS - 1, j + 1)
                    project(tiles - EG + j, j)
                project(tiles - 1, EG - 1)
                pe.wait_ge(row_ready, tiles - 1 + RING)
                nc.tensor.matmul(out[:, 0, 256:256 + D], flags["tt"][:], sums[:, EG - 1], start=True, stop=True).then_inc(tails_ready, 1)
                pe.wait_ge(merged_ready, 1)
                turn(tiles, 0, merged[:])
                project(tiles, 0)

            @block.scalar
            def _(act):
                act.sem_inc(tp_moved, RING)
                act.sem_inc(row_ready, RING)

                def move(i, j):
                    act.wait_ge(tp_ready, i + 1 + EG)
                    nc.scalar.copy(turned[:, j % RING], tp[:, j % RING, 0:2 * P]).then_inc(tp_moved, 1)

                def keep(i, j, uses):
                    act.wait_ge(out_ready, i + 1)
                    act.wait_ge(written[j], 16 * uses)
                    nc.scalar.copy(rows[:, j], out[:, j % RING, 0:D]).then_inc(row_ready, 1)

                act.wait_ge(zeroed, 3)
                move(0, 0)
                with act.Fori(0, STEPS - 1) as g:
                    for j in range(EG):
                        move(EG * g + j + 1, j + 1)
                        keep(EG * g + j, j, g)
                for j in range(EG):
                    if j < EG - 1:
                        move(tiles - EG + j + 1, j + 1)
                    keep(tiles - EG + j, j, STEPS - 1)
                move(tiles, 0)
                keep(tiles, 0, STEPS)

            @block.vector
            def _(dve):
                v = nc.vector
                for q in range(RING):
                    v.memset(tp[:, q], 0.0).then_inc(zeroed, 1)
                v.memset(sums[:], 0.0).then_inc(zeroed, 1)
                dve.wait_ge(zeroed, 3)
                with dve.Fori(0, STEPS) as g:
                    t = Tick(dve, vec, g, 2)
                    dve.wait_ge(sum_ready, EG * g)
                    step = bass.ds(g * EG, EG)
                    t.mark(v.tensor_copy(same[:], flags["same"][:, step]))
                    t.mark(v.tensor_tensor(weighted[:].rearrange("p j (h c) -> p j h c", h=H),
                                           vals[:, step, :].rearrange("p j (h c) -> p j h c", h=H),
                                           alpha[:, step, :].unsqueeze(3).to_broadcast([P, EG, H, D // H]), ALU.mult))
                    t.done()
                    t.close()
                    for j in range(EG):
                        if j:
                            dve.wait_ge(sum_ready, EG * g + j)
                        dve.wait_ge(tp_ready, EG * g + j + 1)
                        v.scalar_tensor_tensor(sums[:, j], sums[:, (j - 1) % EG], same[:, j:j + 1], weighted[:, j],
                                               ALU.mult, ALU.add).then_inc(sum_ready, 1)
                dve.wait_ge(tails_ready, 1)
                v.tensor_copy(merged[:], out[:, 0, 256:256 + D]).then_inc(merged_ready, 1)


def feed(nc, io, w, STEPS):
    N2 = 2 * FG
    c = w["ff"]
    FN = FG * P
    with ExitStack() as ctx:
        sb = lambda n, s, dt=F32: ctx.enter_context(nc.sbuf_tensor("f_" + n, s, dt))
        pb = lambda n, s: ctx.enter_context(nc.psum_tensor("f_" + n, s, F32))
        sem = lambda n: ctx.enter_context(nc.semaphore("f_" + n))
        x, agg, a0 = sb("x", [P, 2, N2, D]), sb("agg", [P, 2, N2, D]), sb("a0", [P, 2, N2])
        u, y = sb("u", [P, N2, D]), sb("y", [P, 2, N2, D])
        norm = sb("norm", [P, 2, N2, 161])
        res, a0_kept = sb("res", [P, 2, N2, D]), sb("a0_kept", [P, 2, N2])
        stats, stat2 = sb("stats", [P, N2, 6]), sb("stat2", [P, 2, N2, 6])
        mean, negm, var = sb("mean", [P, N2]), sb("negm", [P, N2]), sb("var", [P, N2])
        share = sb("share", [P, 2 * N2])
        mean2, var2 = sb("mean2", [P, 2, N2]), sb("var2", [P, 2, N2])
        r, r2, tmp = sb("r", [P, N2]), sb("r2", [P, 2, N2]), sb("tmp", [P, 4, 2 * N2])
        sT, vT = sb("sT", [65, 2, FN]), sb("vT", [CV, 2, FN])
        hid, gate = sb("hid", [P, 2, FN]), sb("gate", [P, 2, FN])
        f0, f1 = sb("f0", [P, 2, FN]), sb("f1", [65, 2, FN])
        o = sb("o", [P, 2, FG, D])
        pS, pV = pb("pS", [65, FN]), pb("pV", [CV, FN])
        pH, pG, p0, p1 = pb("pH", [P, FN]), pb("pG", [P, FN]), pb("p0", [P, FN]), pb("p1", [64, FN])
        pO = pb("pO", [P, 2, 512])
        x_in, o_out = [sem("x_in0"), sem("x_in1")], [sem("o_out0"), sem("o_out1")]
        vec, negm_ready, u_ready, r_ready, y_ready = sem("vec"), sem("negm_ready"), sem("u_ready"), sem("r_ready"), sem("y_ready")
        scale_ready, ns_ready, nv_ready, res_ready = sem("scale_ready"), sem("ns_ready"), sem("nv_ready"), sem("res_ready")
        s_turned, v_turned, s_moved, v_moved = sem("s_turned"), sem("v_turned"), sem("s_moved"), sem("v_moved")
        g_mm, hid_mm, fv_mm, hid_ready, gate_ready = sem("g_mm"), sem("hid_mm"), sem("fv_mm"), sem("hid_ready"), sem("gate_ready")
        f_ready, o_mm, o_ready, gate_pe, pool_gate = sem("f_ready"), sem("o_mm"), sem("o_ready"), sem("gate_pe"), sem("pool_gate")
        grp = lambda a: a.rearrange("(g p j) c -> g p j c", p=P, j=N2)
        xs, aggs, outs = grp(io["x1"]), grp(io["agg"]), grp(io["out"])
        a0s = io["a0"].rearrange("(g p j) c -> g p (j c)", p=P, j=N2)
        FRONT = N2 + MOMENTS + 1 + RSQRT + 2 * N2 + (MOMENTS + 1) + 3 + RSQRT + 1
        HALVES = 2 * STEPS

        def known(n, low, high=STEPS):
            return isinstance(n, int) and low <= n < high

        assert STEPS % 2 and STEPS > 4

        def steps(run, step):
            step(0, 0, True, False)
            with run.Fori(0, (STEPS - 2) // 2) as i:
                step(2 * i + 1, 1, True, True)
                step(2 * i + 2, 0, True, True)
            step(STEPS - 2, 1, True, True)
            step(STEPS - 1, 0, False, True)

        with nc.Block() as block:
            @block.sync
            def _(sp):
                def load(s, b):
                    sp.dma_start(x[:, b], xs[s]).then_inc(x_in[b], 16)
                    sp.dma_start(agg[:, b], aggs[s]).then_inc(x_in[b], 16)
                    sp.dma_start(a0[:, b], a0s[s]).then_inc(x_in[b], 16)

                def store(k, step, h, slot):
                    sp.wait_ge(o_ready, FG * (k + 1))
                    sp.dma_start(outs[step][:, h * FG:(h + 1) * FG], o[:, slot]).then_inc(o_out[slot], 16)

                def step(s, b, front, back):
                    if not known(s, STEPS - 2):
                        sp.wait_ge(res_ready, s + 1)
                        load(s + 2, b)
                    if back:
                        store(2 * s - 2, s - 1, 0, 0)
                        store(2 * s - 1, s - 1, 1, 1)

                load(0, 0)
                load(1, 1)
                steps(sp, step)
                store(HALVES - 2, STEPS - 1, 0, 0)
                store(HALVES - 1, STEPS - 1, 1, 1)
                for slot in range(2):
                    sp.wait_ge(o_out[slot], 16 * STEPS)

            @block.gpsimd
            def _(pool):
                def hold(s, value):
                    pool.wait_ge(s, value)
                    pool.sem_inc(pool_gate, 1)

                def step(s, b, front, back):
                    hold(ns_ready, N2 * (s + 1))
                    if back:
                        hold(o_ready, FG * (2 * s - 2))
                    nc.gpsimd.tensor_copy(a0_kept[:, b], a0[:, b])
                    nc.gpsimd.tensor_tensor(res[:, b], x[:, b], y[:, b], ALU.add).then_inc(res_ready, 1)

                steps(pool, step)

            @block.vector
            def _(dve):
                v = nc.vector
                flat = lambda a: a.rearrange("p a b -> p (a b)")

                def first_moments(t, n, b, nth):
                    dve.wait_ge(x_in[b], 48 * nth + 48)
                    for j in range(N2):
                        k = t.mark(v.bn_stats(stats[:, j], x[:, b, j]))
                    t.wait(k)
                    t.wait(moments(nc, t, stats[:], D, mean[:], var[:], [tmp[:, i, 0:N2] for i in range(4)]))
                    v.tensor_scalar(negm[:], mean[:], -1.0, None, ALU.mult).then_inc(negm_ready, 1)
                    t.link(v.tensor_scalar(var[:], var[:], EPS, None, ALU.add))

                def sums(n, b):
                    dve.wait_ge(r_ready, 2 * n + 1)
                    for j in range(N2):
                        dve.wait_ge(u_ready, N2 * n + j + 1)
                        v.scalar_tensor_tensor(y[:, b, j], u[:, j], r[:, j:j + 1], agg[:, b, j],
                                               ALU.mult, ALU.add).then_inc(y_ready, 1)

                def sum_moments(t, n, b):
                    for j in range(N2):
                        dve.wait_ge(y_ready, N2 * n + j + 1)
                        t.mark(v.bn_stats(stat2[:, 0, j], y[:, b, j, 0:C0]))
                        k = t.mark(v.bn_stats(stat2[:, 1, j], y[:, b, j, C0:D]))
                    t.wait(k)

                def factors(t, n, b, between):
                    moments(nc, t, stat2[:].rearrange("p i j c -> p (i j) c"), share[:], flat(mean2[:]), flat(var2[:]),
                            [tmp[:, k] for k in range(4)])
                    t.done()
                    t.link(v.tensor_tensor(tmp[:, 3, 0:N2], mean2[:, 1], mean2[:, 1], ALU.mult))
                    t.link(v.tensor_tensor(var2[:, 1], var2[:, 1], tmp[:, 3, 0:N2], ALU.add))
                    t.link(v.tensor_scalar(var2[:], var2[:], EPS, None, ALU.add))
                    dve.wait_ge(nv_ready, N2 * n)
                    rsqrt(nc, t, flat(r2[:]), flat(var2[:]), tmp[:, 0], r_ready, between)
                    dve.wait_ge(r_ready, 2 * n + 2)
                    if not known(n, 0, 2):
                        dve.wait_ge(s_turned, 2 * n - 2)
                    t.mark(v.tensor_copy(norm[:, b, :, C0], a0[:, b]))
                    t.close()
                    v.tensor_tensor(r2[:], r2[:], a0[:, b].unsqueeze(1).to_broadcast([P, 2, N2]), ALU.mult).then_inc(scale_ready, 1)

                def scalars(n, b):
                    dve.wait_ge(scale_ready, n + 1)
                    for j in range(N2):
                        v.tensor_scalar(norm[:, b, j, 0:C0], y[:, b, j, 0:C0], mean2[:, 0, j:j + 1], r2[:, 0, j:j + 1],
                                        ALU.subtract, ALU.mult).then_inc(ns_ready, 1)

                def gated(k, slot):
                    dve.wait_ge(fv_mm, k + 1)
                    dve.wait_ge(gate_ready, k + 1)
                    if not known(k, 0, 1):
                        dve.wait_ge(o_mm, FG * (k - 1))
                    v.scalar_tensor_tensor(f0[:, slot], gate[:, slot], 1.0, p0[:], ALU.add, ALU.mult)
                    v.scalar_tensor_tensor(f1[0:64, slot], gate[0:64, slot], 1.0, p1[:], ALU.add, ALU.mult).then_inc(f_ready, 1)

                def outputs(k, step, b, h, uses):
                    def out(j):
                        if j == 0:
                            dve.wait_ge(res_ready, step + 1)
                            dve.wait_ge(o_out[h], 16 * uses)
                        dve.wait_ge(o_mm, FG * k + (j // 2) * 2 + 2)
                        i = h * FG + j
                        v.scalar_tensor_tensor(o[:, h, j], pO[:, j // 2, (j % 2) * D:(j % 2 + 1) * D], a0_kept[:, b, i:i + 1],
                                               res[:, b, i], ALU.mult, ALU.add).then_inc(o_ready, 1)
                    return out

                def step(s, b, front, back):
                    t = Tick(dve, vec, s + 1, FRONT)
                    if front:
                        first_moments(t, s + 1, 1 - b, (s + 1) // 2 if known(s, 0) else nth[b])
                        rsqrt(nc, t, r[:], var[:], tmp[:, 0, 0:N2], r_ready)
                    if back:
                        dve.wait_ge(res_ready, s)
                    if front:
                        sums(s + 1, 1 - b)
                    if back:
                        gated(2 * s - 1, 1)
                    if front:
                        sum_moments(t, s + 1, 1 - b)
                    if back:
                        first = outputs(2 * s - 2, s - 1, 1 - b, 0, s - 1)
                    if front:
                        factors(t, s + 1, 1 - b, first if back else None)
                    elif back:
                        for j in range(FG):
                            first(j)
                    gated(2 * s, 0)
                    if front:
                        scalars(s + 1, 1 - b)
                    if back:
                        second = outputs(2 * s - 1, s - 1, 1 - b, 1, s - 1)
                        for j in range(FG):
                            second(j)

                v.memset(f1[64:65], 1.0)
                v.memset(share[:, 0:N2], 1.0 / C0)
                v.memset(share[:, N2:], 1.0 / CV)
                t = Tick(dve, vec, 0, FRONT)
                first_moments(t, 0, 0, 0)
                rsqrt(nc, t, r[:], var[:], tmp[:, 0, 0:N2], r_ready)
                sums(0, 0)
                sum_moments(t, 0, 0)
                factors(t, 0, 0, None)
                scalars(0, 0)
                nth = {}
                step(0, 0, True, False)
                with dve.Fori(0, (STEPS - 2) // 2) as i:
                    nth[1], nth[0] = i + 1, i + 1
                    step(2 * i + 1, 1, True, True)
                    step(2 * i + 2, 0, True, True)
                step(STEPS - 2, 1, True, True)
                step(STEPS - 1, 0, False, True)
                gated(HALVES - 1, 1)
                for h in range(2):
                    out = outputs(HALVES - 2 + h, STEPS - 1, 0, h, STEPS - 1)
                    for j in range(FG):
                        out(j)

            @block.tensor
            def _(pe):
                def turn(k, step, b, h):
                    for part, ready, moved, rows, a, done in ((pS, ns_ready, s_moved, 65, 0, s_turned),
                                                              (pV, nv_ready, v_moved, CV, 65, v_turned)):
                        pe.wait_ge(ready, N2 * step + (h + 1) * FG)
                        pe.sem_inc(gate_pe, 1)
                        pe.wait_ge(moved, k)
                        pe.sem_inc(gate_pe, 1)
                        for j in range(FG):
                            last = nc.tensor.transpose(part[:, j * P:(j + 1) * P], norm[:, b, h * FG + j, a:a + rows], w["ident"])
                        last.then_inc(done, 1)

                def hidden(k, slot):
                    pe.wait_ge(s_moved, k + 1)
                    pe.wait_ge(gate_ready, k)
                    nc.tensor.matmul(pG[:], c["s"][:, 128:256], sT[:, slot], start=True, stop=True).then_inc(g_mm, 1)
                    pe.wait_ge(hid_ready, k)
                    nc.tensor.matmul(pH[:], c["s"][:, 0:128], sT[:, slot], start=True, stop=True).then_inc(hid_mm, 1)
                    pe.wait_ge(v_moved, k + 1)
                    pe.wait_ge(f_ready, k)
                    nc.tensor.matmul(p0[:], c["v0"], vT[:, slot], start=True, stop=True)
                    nc.tensor.matmul(p1[:], c["v1"], vT[:, slot], start=True, stop=True).then_inc(fv_mm, 1)

                def output(k, slot):
                    pe.wait_ge(hid_ready, k + 1)
                    pe.wait_ge(f_ready, k + 1)
                    pe.wait_ge(o_ready, FG * k)
                    for j in range(FG):
                        at = slice(j * P, (j + 1) * P)
                        out = pO[:, j // 2, (j % 2) * D:(j % 2 + 1) * D]
                        nc.tensor.matmul(out[:, 0:C0], hid[:, slot, at], c["o"], start=True, stop=True)
                        nc.tensor.matmul(out[:, C0:D], f0[:, slot, at], c["ov0"], start=False, stop=True, skip_group_check=True)
                        nc.tensor.matmul(out, f1[:, slot, at], c["ov1"], start=False, stop=True,
                                         skip_group_check=True).then_inc(o_mm, 1)

                def step(s, b, front, back):
                    turn(2 * s, s, b, 0)
                    if back:
                        hidden(2 * s - 1, 1)
                        output(2 * s - 2, 0)
                    turn(2 * s + 1, s, b, 1)
                    hidden(2 * s, 0)
                    if back:
                        output(2 * s - 1, 1)

                steps(pe, step)
                hidden(HALVES - 1, 1)
                output(HALVES - 2, 0)
                output(HALVES - 1, 1)

            @block.scalar
            def _(act):
                def move(k, slot):
                    act.wait_ge(s_turned, k + 1)
                    nc.scalar.copy(sT[:, slot], pS[:]).then_inc(s_moved, 1)
                    act.wait_ge(v_turned, k + 1)
                    if not known(k, 0, 2):
                        act.wait_ge(fv_mm, k - 1)
                    nc.scalar.copy(vT[:, slot], pV[:]).then_inc(v_moved, 1)

                def gates(k, slot):
                    act.wait_ge(g_mm, k + 1)
                    if not known(k, 0, 2):
                        act.wait_ge(f_ready, k - 1)
                        act.wait_ge(o_mm, FG * (k - 1))
                    nc.scalar.activation(gate[:, slot], pG[:], ACT.Tanh, scale=0.5).then_inc(gate_ready, 1)
                    act.wait_ge(hid_mm, k + 1)
                    nc.scalar.activation(hid[:, slot], pH[:], ACT.Silu).then_inc(hid_ready, 1)

                def relu(n, b):
                    act.wait_ge(negm_ready, n + 1)
                    act.wait_ge(y_ready, N2 * n)
                    for j in range(N2):
                        nc.scalar.activation(u[:, j], x[:, b, j], ACT.Relu, bias=negm[:, j:j + 1]).then_inc(u_ready, 1)

                def vectors(n, b):
                    act.wait_ge(scale_ready, n + 1)
                    if not known(n, 0, 2):
                        act.wait_ge(v_turned, 2 * n - 2)
                    for j in range(N2):
                        nc.scalar.activation(norm[:, b, j, C0 + 1:], y[:, b, j, C0:D], ACT.Copy,
                                             scale=r2[:, 1, j:j + 1]).then_inc(nv_ready, 1)

                def step(s, b, front, back):
                    move(2 * s, 0)
                    if front:
                        relu(s + 1, 1 - b)
                    if back:
                        gates(2 * s - 1, 1)
                    move(2 * s + 1, 1)
                    gates(2 * s, 0)
                    if front:
                        vectors(s + 1, 1 - b)

                relu(0, 0)
                vectors(0, 0)
                steps(act, step)
                gates(HALVES - 1, 1)


def build(nc, io, N_ROWS, T):
    with ExitStack() as ctx:
        sb = lambda n, s, dt=F32: ctx.enter_context(nc.sbuf_tensor(n, s, dt))
        w = {}
        for key, table in (("all", W_ALL), ("l0", W0), ("l1", W1), ("ff", W2)):
            tile = sb(f"weights_{key}", [P, offsets(table)[1]])
            w["t_" + key] = tile[:]
            w[key] = views(tile, table)
        w["ident"], w["low"] = w["all"]["ident"], w["all"]["low"]
        w["mrow0"], w["mrow1"] = sb("message_bias0", [1, D])[:], sb("message_bias1", [1, D])[:]
        flags = {n: sb(n, [P, T + EG], I32) for n in ("src", "dst", "row")}
        flags |= {n: sb(n, [P, T]) for n in ("same", "nxt", "first", "last", "mid")}
        flags |= {n: sb(n, [P, 1]) for n in ("head", "tail", "tail_row")}
        flags["tail_at"] = sb("tail_at", [P, 1], I32)
        flags["tt"] = sb("tails_equal", [P, P])
        flags["y0"] = sb("edge_y", [P, T, 4])
        flags["ones"] = sb("ones", [1, P])
        w["ones"] = flags["ones"]
        io["rows"] = N_ROWS
        prepare(nc, io, w, flags, T)
        nodes(nc, io, w, N_ROWS // (P * NG))
        for layer in range(2):
            with ExitStack() as own:
                H = (4, 8)[layer]
                logits = own.enter_context(nc.sbuf_tensor(f"logits{layer}", [P, T, H], F32))
                vals = own.enter_context(nc.sbuf_tensor(f"vals{layer}", [P, T, D], F32))
                edges(nc, io, w, flags, T, layer, vals, logits)
                softmax(nc, w, flags, T, layer, logits)
                scatter(nc, io, w, flags, T, layer, vals, logits)
        feed(nc, io, w, N_ROWS // (P * 2 * FG))


def place(table, parts):
    at, cols = offsets(table)
    out = np.zeros((P, cols), np.float32)
    for name, pieces in parts.items():
        a, rows, n = at[name]
        for r, c, m in pieces:
            m = np.asarray(m)
            m = m.reshape(-1, 1) if m.ndim == 1 else m
            assert r + m.shape[0] <= rows and c + m.shape[1] <= n, name
            out[r:r + m.shape[0], a + c:a + c + m.shape[1]] = m
    return out


def by_component(m, rows="cd", cols="dc", comps=(0, 1, 2)):
    C, K = m.shape
    n = len(comps)
    out = np.zeros((C, 3, n, K), np.float32)
    for at, d in enumerate(comps):
        out[:, d, at, :] = m
    if rows == "dc":
        out = out.transpose(1, 0, 2, 3)
    if cols == "cd":
        out = out.transpose(0, 1, 3, 2)
    out = out.reshape(3 * C, n * K)
    return out


def value_rows(H, ps, pv):
    SW, VW = C0 // H, C1 // H
    out = np.zeros((H, D // H, D), np.float32)
    out[:, 0:SW, 0:C0] = ps.reshape(H, SW, C0)
    for d in range(3):
        out[:, SW + d * VW:SW + (d + 1) * VW, C0 + d::3] = pv.reshape(H, VW, C1)
    return out.reshape(D, D)


def input_rows(s_src, s_dst, v_src, v_dst):
    out = np.zeros((2 * D, D), np.float32)
    for k, (s, v) in enumerate(((s_src, v_src), (s_dst, v_dst))):
        out[k * D:k * D + C0, 0:C0] = s
        out[k * D + C0:(k + 1) * D, C0:D] = by_component(v)
    return out


def columns(s, v):
    one = np.concatenate([s, np.repeat(v, 3)])
    return np.concatenate([one, one])


def cut(rows):
    return {k: rows[a:b] for k, (a, b) in enumerate(((0, 128), (128, 256), (256, 320)))}


def kernel(**inputs):
    import concourse.bacc as bacc
    from concourse.bass_utils import run_bass_kernel_spmd as run

    a = {k: np.ascontiguousarray(v) for k, v in inputs.items()}
    N, E = a["x"].shape[0], a["src"].shape[0]
    unit = P * max(NG, 2 * FG)
    N_ROWS = -(-N // unit) * unit
    T = -(-E // (P * EG)) * EG
    E_ROWS = P * T
    assert N_ROWS > N
    f32 = np.float32
    L0 = {k[7:]: v for k, v in a.items() if k.startswith("L0_gnn_")}
    L1 = {k[7:]: v for k, v in a.items() if k.startswith("L1_gnn_")}

    def padded(m, rows, fill=0):
        out = np.full((rows, *m.shape[1:]), fill, m.dtype)
        out[:m.shape[0]] = m
        return out

    def by_tile(m):
        return np.ascontiguousarray(padded(m, E_ROWS).reshape(P, T, -1).transpose(2, 1, 0).reshape(m.shape[1], -1))

    spread2 = lambda v: np.broadcast_to(v, (P, v.shape[-1]))
    none = np.zeros(C1, f32)
    in0, g0, b0 = (cut(m) for m in (input_rows(L0["Ws_src"], L0["Ws_dst"], L0["Wv_src"], L0["Wv_dst"]),
                                    columns(L0["gamma_s"], L0["gamma_v"]), columns(L0["beta_s"], none)))
    in1, g1, b1 = (cut(m) for m in (input_rows(L1["msrc_ws"], L1["mdst_ws"], L1["msrc_wv"], L1["mdst_wv"]),
                                    columns(L1["ln1_w0"], L1["ln1_w1"]), columns(L1["ln1_b0"], none)))
    wv, wl, wlin = L0["Wv_val"], L0["Wv_vlin"], L1["lin_wv"]
    val0 = np.concatenate([L0["W_alpha"], L0["Ws_val"]], 1)
    svT = L0["Ws_val"].T
    p0, p1 = value_rows(4, L0["Wps"], L0["Wpv"]), value_rows(8, L1["proj_ws"], L1["proj_wv"])
    diag = lambda m: by_component(m, "dc", "dc")
    w_l0 = place(W0, {
        **{f"in{k}": [(0, 0, in0[k])] for k in range(3)}, **{f"gam{k}": [(0, 0, g0[k])] for k in range(3)},
        **{f"beta{k}": [(0, 0, b0[k])] for k in range(3)}, "rad": [(0, 0, L0["W_rbf"])],
        "first": [(64, 0, wv[0:64]), (0, C1, val0[0:64])], "second": [(96, 0, val0[64:96]), (0, 160, diag(wv[64:96]))],
        "svT": [(0, 0, svT[:, 0:64]), (0, 96, svT[:, 64:96])], "wg": [(0, 0, L0["Wg"])],
        "third": [(0, 0, diag(wv[96:128]))],
        "out0": [(0, 0, L0["Ws_vlin"][0:64]), (0, 64, wl[0:64]), (96, 96, L0["Ws_vlin"][64:96])],
        "out0s": [(0, 0, np.broadcast_to(L0["w2_ss"][:, None], (C0, C0))), (0, 64, np.broadcast_to(L0["w2_sv"][:, None], (C0, C1)))],
        "dots": [(96, 0, L0["w2_vv0"])], "out1": [(0, 0, diag(wl[64:96])), (0, CV, diag(wl[96:128]))],
        "b2s": [(0, 0, np.tile(L0["w2_vs"], 3))], "c2s": [(0, 0, np.tile(L0["w2_vv1"], 3))],
        "p0": [(0, 0, p0[0:128])], "p1": [(0, 0, p0[128:160])], "dot": [(0, 0, spread2(L0["alpha_dot"].reshape(1, -1)))]})
    w_l1 = place(W1, {
        **{f"in{k}": [(0, 0, in1[k])] for k in range(3)}, **{f"gam{k}": [(0, 0, g1[k])] for k in range(3)},
        **{f"beta{k}": [(0, 0, b1[k])] for k in range(3)}, "mbias": [(0, 0, L1["mdst_bs"][None])],
        "r1": [(0, 0, L1["rw1"]), (64, 0, L1["rb1"][None])], "r2": [(0, 0, L1["rw2"]), (64, 0, L1["rb2"][None])],
        "rad": [(0, 0, L1["rw3"]), (64, 0, L1["roff"][None])],
        **{k: [(0, 0, L1[k])] for k in ("rg1", "rbe1", "rg2", "rbe2")},
        "first": [(64, 0, wlin[0:64]), (0, C1, L1["lin_ws"][0:64])],
        "second": [(96, 0, L1["lin_ws"][64:96]), (0, P, diag(wlin[64:96]))],
        "sbias": [(0, 0, L1["lin_bs"][None])], "third": [(0, 0, diag(wlin[96:128]))],
        "p0": [(0, 0, p1[0:128])], "p1": [(0, 0, p1[128:160])], "dot": [(0, 0, spread2(L1["alpha_dot"].reshape(1, -1)))],
        "fill": [(0, 0, spread2(L1["proj_bs"][None]))]})
    f1s, f1v, f2v = np.concatenate([L1["f1_ws"], L1["f1_ws"][:, 128:]], 1), L1["f1_wv"], L1["f2_wv"]
    f1b = np.concatenate([L1["f1_bs"], L1["f1_bs"][128:]])
    pick = by_component(f1v, "cd", "dc")
    back = by_component(f2v, "dc", "cd")
    w_ff = place(W2, {
        "s": [(0, 0, f1s), (64, 0, f1b[None])], "gs": [(0, 0, L1["ln2_w0"])],
        "b0": [(0, 64, L1["ln2_b0"]), (64, 64, np.ones((1, 1), f32))],
        "v0": [(0, 0, pick[:, 0:128])], "v1": [(0, 0, pick[:, 128:192])], "gv": [(0, 0, np.repeat(L1["ln2_w1"], 3))],
        "o": [(0, 0, L1["f2_ws"])], "ov0": [(0, 0, back[0:128])],
        "ov1": [(0, C0, back[128:192]), (64, 0, L1["f2_bs"][None])]})
    w_all = place(W_ALL, {"ident": [(0, 0, np.eye(P, dtype=f32))], "low": [(0, 0, np.tril(np.ones((P, P), f32), -1))]})

    arrays = dict(
        x=padded(a["x"], N_ROWS), a0=padded(a["node_vec1"], N_ROWS),
        src=padded(a["src"], E_ROWS, N).reshape(P, T), dst=padded(a["dst"], E_ROWS, N).reshape(P, T),
        attr16=by_tile(a["edge_attr_16"]), attr64=by_tile(a["edge_attr_64"]),
        attr4=padded(a["edge_attr_4"], E_ROWS).reshape(P, T, 4), attr3=padded(a["edge_attr_3"], E_ROWS).reshape(P, T, 3),
        w_all=w_all, w_l0=w_l0, w_l1=w_l1, w_ff=w_ff)
    nc = bacc.Bacc("TRN2", target_bir_lowering=False, num_devices=1)
    io = {}
    for name, m in arrays.items():
        io[name] = nc.dram_tensor(f"in_{name}", m.shape, mybir.dt.from_np(m.dtype), kind="ExternalInput").ap()
    for name in ("x1", "g", "agg"):
        io[name] = nc.dram_tensor(f"table_{name}", (N_ROWS, D), F32).ap()
    io["out"] = nc.dram_tensor("out", (N_ROWS, D), F32, kind="ExternalOutput").ap()
    build(nc, io, N_ROWS, T)
    got = run(nc, [{f"in_{k}": m for k, m in arrays.items()}], core_ids=[0]).results[0]["out"]
    return got[:N]
```

```python
from contextlib import ExitStack
from itertools import zip_longest

import numpy as np

import concourse.bass as bass
from concourse import mybir

F32 = mybir.dt.float32
I32 = mybir.dt.int32
U32 = mybir.dt.uint32
ALU = mybir.AluOpType
ACT = mybir.ActivationFunctionType
AX_X = mybir.AxisListType.X

P = 128
C0, C1 = 64, 32
CV = 3 * C1
D = C0 + CV
WN = 2 * C0 + 3 * C1
EG = 4
NG = 8
FG = 4
RING = 2
EPS = 1e-5
BIG = 1e30
SKIP = 1e6
SQRT3 = float(np.sqrt(3.0))
SQRT2 = float(np.sqrt(2.0))
RSQRT_SEED = 1597463007.0
M0, M1 = 128, 64


W0 = dict(in0=(P, D), in1=(P, D), in2=(64, D), beta0=(P, 1), beta1=(P, 1), beta2=(64, 1), gam0=(P, 1),
          gam1=(P, 1), gam2=(64, 1), rad=(16, WN), first=(P, C1 + 160), second=(P, 160 + CV), third=(CV, CV + 2 * C1), svT=(C0, P), wg=(C0, C1),
          out0=(P, 160), out0s=(C0, C0 + C1), dots=(P, 1), out1=(CV, 2 * CV + 2 * C1), b2s=(CV, 1), c2s=(CV, 1), p0=(P, D), p1=(32, D), dot=(P, C0))
W1 = dict(in0=(P, D), in1=(P, D), in2=(64, D), beta0=(P, 1), beta1=(P, 1), beta2=(64, 1), gam0=(P, 1),
          gam1=(P, 1), gam2=(64, 1), mbias=(1, D), r1=(65, 64), r2=(65, 64), rad=(65, WN), rg1=(64, 1),
          rbe1=(64, 1), rg2=(64, 1), rbe2=(64, 1), first=(P, C1 + P), second=(P, P + CV), third=(CV, CV + 2 * C1), sbias=(1, P),
          p0=(P, D), p1=(32, D), dot=(P, C0), fill=(P, D))
W2 = dict(s=(65, 256), gs=(65, 1), b0=(65, 65), v0=(CV, 128), v1=(CV, 64), gv=(CV, 1), o=(M0, C0),
          ov0=(P, CV), ov1=(65, D))
W_ALL = dict(ident=(P, P), low=(P, P))


def offsets(table):
    at, out = 0, {}
    for name, (rows, cols) in table.items():
        out[name] = (at, rows, cols)
        at += cols
    return out, at


def views(tile, table):
    return {n: tile[0:r, a:a + c] for n, (a, r, c) in offsets(table)[0].items()}


class Tick:

    def __init__(self, eng, sem, step=0, per_step=0, before=0):
        self.eng, self.sem, self.step, self.per_step, self.before = eng, sem, step, per_step, before
        self.n = 0

    def mark(self, instruction):
        instruction.then_inc(self.sem, 1)
        self.n += 1
        return self.n

    def wait(self, n):
        self.eng.wait_ge(self.sem, self.step * self.per_step + (self.before + n))

    def link(self, instruction):
        self.wait(self.mark(instruction))

    def done(self):
        self.wait(self.n)

    def close(self):
        assert self.n == self.per_step, (self.n, self.per_step)


def straight(pieces):
    for _ in pieces:
        pass


def link(t, instruction):
    n = t.mark(instruction)
    yield
    t.wait(n)


def moments(nc, t, stats, n, mean, var, tmp):
    a = t.mark(nc.vector.tensor_tensor(tmp[0], stats[:, :, 1], stats[:, :, 4], ALU.subtract))
    b = t.mark(nc.vector.tensor_tensor(tmp[1], stats[:, :, 2], stats[:, :, 5], ALU.add))
    c = t.mark(nc.vector.tensor_tensor(mean, stats[:, :, 1], stats[:, :, 4], ALU.add))
    t.wait(a)
    d = t.mark(nc.vector.scalar_tensor_tensor(tmp[2], tmp[0], 0.25, tmp[0], ALU.mult, ALU.mult))
    t.wait(c)
    t.mark(nc.vector.tensor_scalar(mean, mean, 0.5, None, ALU.mult))
    if isinstance(n, int):
        yield
        t.wait(d)
        last = nc.vector.scalar_tensor_tensor(var, tmp[1], 1.0 / n, tmp[2], ALU.mult, ALU.add)
    else:
        yield from link(t, nc.vector.tensor_tensor(tmp[1], tmp[1], n, ALU.mult))
        last = nc.vector.tensor_tensor(var, tmp[1], tmp[2], ALU.add)
    yield from link(t, last)


MOMENTS = 6


def rsqrt(nc, t, y, v, tmp, ready):
    yield from link(t, nc.vector.tensor_scalar(y.bitcast(I32), v.bitcast(I32), -0.5, RSQRT_SEED, ALU.mult, ALU.add))
    for n in range(3):
        yield from link(t, nc.vector.tensor_tensor(tmp, y, y, ALU.mult))
        yield from link(t, nc.vector.scalar_tensor_tensor(tmp, tmp, -0.5, v, ALU.mult, ALU.mult))
        step = nc.vector.scalar_tensor_tensor(y, tmp, 1.5, y, ALU.add, ALU.mult)
        if n < 2:
            yield from link(t, step)
    step.then_inc(ready, 1)


RSQRT = 9


def prepare(nc, io, w, flags, T):
    with ExitStack() as ctx:
        sem = lambda n: ctx.enter_context(nc.semaphore(n))
        loaded, vec, pe_done = sem("prep_loaded"), sem("prep_vec"), sem("prep_pe")
        ps = ctx.enter_context(nc.psum_tensor("prep_ps", [P, 3, 512], F32))
        dstf = ctx.enter_context(nc.sbuf_tensor("dstf", [P, T], F32))
        end = ctx.enter_context(nc.sbuf_tensor("endf", [P, T], F32))
        y_in = ctx.enter_context(nc.sbuf_tensor("y_in", [P, T, 4], F32))
        a, b, c = w["l0"], w["l1"], w["ff"]
        N_IN = 16 * 7
        with nc.Block() as block:
            @block.sync
            def _(sp):
                sp.dma_start(w["t_all"], io["w_all"]).then_inc(loaded, 16)
                sp.dma_start(w["t_l0"], io["w_l0"]).then_inc(loaded, 16)
                sp.dma_start(w["t_l1"], io["w_l1"]).then_inc(loaded, 16)
                sp.dma_start(w["t_ff"], io["w_ff"]).then_inc(loaded, 16)
                sp.dma_start(flags["src"][:, 0:T], io["src"]).then_inc(loaded, 16)
                sp.dma_start(flags["dst"][:, 0:T], io["dst"]).then_inc(loaded, 16)
                sp.dma_start(y_in[:], io["attr4"]).then_inc(loaded, 16)

            @block.tensor
            def _(pe):
                pe.wait_ge(loaded, N_IN)
                for n, l in enumerate((a, b)):
                    for k in range(3):
                        last = nc.tensor.matmul(ps[0:1, n, 0:D], l[f"beta{k}"], l[f"in{k}"], start=(k == 0), stop=(k == 2))
                last.then_inc(pe_done, 1)
                nc.tensor.matmul(ps[:, 2, 0:C1], a["svT"], a["wg"], start=True, stop=True).then_inc(pe_done, 1)
                pe.wait_ge(vec, 4)
                nc.tensor.matmul(ps[0:65, 0, 0:256], c["b0"], c["s"], start=True, stop=True).then_inc(pe_done, 1)

            @block.vector
            def _(dve):
                t = Tick(dve, vec, 0, 0)
                v = nc.vector
                dve.wait_ge(loaded, N_IN)
                dve.wait_ge(pe_done, 1)
                t.mark(v.tensor_copy(flags["y"][:, :, 0:4], y_in[:]))
                t.mark(v.tensor_copy(flags["y"][:, :, 4:6], y_in[:, :, 1:3]))
                t.mark(v.tensor_copy(w["mrow0"], ps[0:1, 0, 0:D]))
                t.mark(v.tensor_tensor(w["mrow1"], ps[0:1, 1, 0:D], b["mbias"], ALU.add))
                for l in (a, b):
                    for k in range(3):
                        t.mark(v.tensor_scalar(l[f"in{k}"], l[f"in{k}"], l[f"gam{k}"], None, ALU.mult))
                dve.wait_ge(pe_done, 2)
                t.mark(v.tensor_copy(a["first"][0:64, C1 + 128:], ps[0:64, 2, 0:C1]))
                t.link(v.tensor_copy(a["second"][96:128, 128:160], ps[96:128, 2, 0:C1]))
                m = a["second"][96:128, 0:160]
                t.mark(v.tensor_scalar(m, m, 1.0 / SQRT3, None, ALU.mult))
                t.mark(v.tensor_scalar(a["third"], a["third"], 1.0 / SQRT2, None, ALU.mult))
                m = a["out0"][0:64, 0:C0 + C1]
                t.mark(v.tensor_tensor(m, m, a["out0s"], ALU.mult))
                m = a["out0"][96:128, C0 + C1:]
                t.mark(v.tensor_scalar(m, m, a["dots"][96:128], 1.0 / SQRT3, ALU.mult, ALU.mult))
                m = a["out1"][:, 0:CV]
                t.mark(v.tensor_scalar(m, m, a["b2s"], None, ALU.mult))
                m = a["out1"][:, CV:]
                t.mark(v.tensor_scalar(m, m, a["c2s"], 1.0 / SQRT2, ALU.mult, ALU.mult))
                m = b["first"][64:128, 0:C1]
                t.mark(v.tensor_scalar(m, m, SQRT3, None, ALU.mult))
                t.mark(v.tensor_scalar(b["third"], b["third"], SQRT3 / SQRT2, None, ALU.mult))
                t.mark(v.tensor_scalar(b["dot"], b["dot"], 0.4, None, ALU.mult))
                dve.wait_ge(pe_done, 3)
                t.mark(v.tensor_scalar(c["s"][0:64], c["s"][0:64], c["gs"][0:64], None, ALU.mult))
                t.mark(v.tensor_copy(c["s"][64:65], ps[64:65, 0, 0:256]))
                t.mark(v.tensor_scalar(c["v0"], c["v0"], c["gv"], None, ALU.mult))
                t.mark(v.tensor_scalar(c["v1"], c["v1"], c["gv"], None, ALU.mult))
                t.mark(v.tensor_scalar(c["ov0"], c["ov0"], 0.5, None, ALU.mult))
                t.mark(v.tensor_scalar(c["ov1"][0:64], c["ov1"][0:64], 0.5, None, ALU.mult))
                d, src = flags["dst"], flags["src"]
                t.mark(v.memset(d[:, T:T + EG], 0))
                t.mark(v.memset(src[:, T:T + EG], 0))
                t.mark(v.memset(flags["same"][:, 0:1], 0.0))
                t.mark(v.memset(flags["nxt"][:, T - 1:T], 0.0))
                t.link(v.tensor_copy(dstf[:], d[:, 0:T]))
                t.mark(v.tensor_tensor(flags["same"][:, 1:T], dstf[:, 1:T], dstf[:, 0:T - 1], ALU.is_equal))
                t.mark(v.tensor_tensor(flags["nxt"][:, 0:T - 1], dstf[:, 1:T], dstf[:, 0:T - 1], ALU.is_equal))
                t.mark(v.tensor_scalar(flags["first"][:], dstf[:], dstf[:, 0:1], None, ALU.is_equal))
                t.link(v.tensor_scalar(flags["last"][:], dstf[:], dstf[:, T - 1:T], None, ALU.is_equal))
                t.link(v.tensor_tensor(flags["mid"][:], flags["first"][:], flags["last"][:], ALU.max))
                t.link(v.tensor_scalar(flags["mid"][:], flags["mid"][:], -1.0, 1.0, ALU.mult, ALU.add))
                t.link(v.tensor_tensor(end[:], flags["first"][:], flags["last"][:], ALU.mult))
                t.link(v.tensor_tensor(flags["last"][:], flags["last"][:], end[:], ALU.subtract))
                t.link(v.tensor_scalar(end[:], flags["nxt"][:], SKIP, None, ALU.mult))
                t.link(v.memset(end[:, T - 1:T], SKIP))
                t.link(v.tensor_tensor(flags["row"][:, 0:T], end[:], dstf[:], ALU.add))
                t.mark(v.tensor_copy(flags["tail"][:], dstf[:, T - 1:T]))
                t.mark(v.tensor_copy(flags["head"][:], dstf[:, 0:1]))
                t.mark(v.memset(flags["ones"][:], 1.0))


def nodes(nc, io, w, N_STEPS):
    with ExitStack() as ctx:
        sb = lambda n, s: ctx.enter_context(nc.sbuf_tensor(n, s, F32))
        sem = lambda n: ctx.enter_context(nc.semaphore(n))
        x = sb("n_x", [P, 2, NG, D])
        u = sb("n_u", [P, NG, D])
        x1 = sb("n_x1", [P, NG, D])
        g = sb("n_g", [P, NG, D])
        fill = sb("n_fill", [P, NG, D])
        stats = sb("n_stats", [P, NG, 6])
        stat2 = sb("n_stat2", [P, 2, NG, 6])
        mean, negm, var = sb("n_mean", [P, NG]), sb("n_negm", [P, NG]), sb("n_var", [P, NG])
        mean2, var2 = sb("n_mean2", [P, NG]), sb("n_var2", [P, NG])
        mean3, var3 = sb("n_mean3", [P, NG]), sb("n_var3", [P, NG])
        e = sb("n_e", [P, 3, NG])
        r = sb("n_r", [P, 3, NG])
        tmp = sb("n_tmp", [P, 4, 3 * NG])
        x_in = [sem("n_x_in0"), sem("n_x_in1")]
        vec, filled, fill_out = sem("n_vec"), sem("n_filled"), sem("n_fill_out")
        negm_ready, u_ready, gv_ready = sem("n_negm_ready"), sem("n_u_ready"), sem("n_gv_ready")
        r_ready, out_ready = sem("n_r_ready"), sem("n_out_ready")
        x1_out, g_out = sem("n_x1_out"), sem("n_g_out")
        grp = lambda a: a.rearrange("(g p j) c -> g p j c", p=P, j=NG)
        xs, x1s, gs, aggs = grp(io["x"]), grp(io["x1"]), grp(io["g"]), grp(io["agg"])
        STEP = NG + MOMENTS + 1 + 2 * NG + 2 * MOMENTS + 5 + RSQRT
        PAIRS = N_STEPS // 2
        ODD = N_STEPS % 2
        tmps = lambda k: [tmp[:, i, 0:k] for i in range(4)]

        with nc.Block() as block:
            @block.sync
            def _(sp):
                def load(step, b):
                    sp.dma_start(x[:, b], xs[step]).then_inc(x_in[b], 16)

                def store(step):
                    sp.wait_ge(out_ready, step + 1)
                    sp.dma_start(x1s[step], x1[:]).then_inc(x1_out, 16)
                    sp.wait_ge(gv_ready, step + 1)
                    sp.dma_start(gs[step], g[:]).then_inc(g_out, 16)
                    sp.dma_start(aggs[step], fill[:]).then_inc(fill_out, 16)

                load(0, 0)
                load(1, 1)
                sp.wait_ge(filled, NG)
                with sp.Fori(0, PAIRS - 1) as i:
                    for b in range(2):
                        store(2 * i + b)
                        load(2 * i + b + 2, b)
                store(2 * PAIRS - 2)
                if ODD:
                    load(2 * PAIRS, 0)
                store(2 * PAIRS - 1)
                if ODD:
                    store(2 * PAIRS)
                sp.wait_ge(x1_out, 16 * N_STEPS)
                sp.wait_ge(g_out, 16 * N_STEPS)
                sp.wait_ge(fill_out, 16 * N_STEPS)

            def act_step(act, step, b):
                act.wait_ge(gv_ready, step)
                act.wait_ge(negm_ready, step + 1)
                for j in range(NG):
                    k = nc.scalar.activation(u[:, j], x[:, b, j], ACT.Relu, bias=negm[:, j:j + 1])
                    k.then_inc(u_ready, 1)
                act.wait_ge(r_ready, step + 1)
                act.wait_ge(g_out, 16 * step)
                for j in range(NG):
                    k = nc.scalar.activation(g[:, j, C0:D], u[:, j, C0:D], ACT.Copy, scale=r[:, 2, j:j + 1])
                k.then_inc(gv_ready, 1)

            def dve_step(dve, step, b, half):
                v = nc.vector
                t = Tick(dve, vec, step, STEP)
                dve.wait_ge(out_ready, step)
                dve.wait_ge(x_in[b], 16 * half + 16)
                for j in range(NG):
                    k = t.mark(v.bn_stats(stats[:, j], x[:, b, j]))
                t.wait(k)
                straight(moments(nc, t, stats[:], D, mean[:], var[:], tmps(NG)))
                t.mark(v.tensor_scalar(e[:, 0], var[:], EPS, None, ALU.add))
                v.tensor_scalar(negm[:], mean[:], -1.0, None, ALU.mult).then_inc(negm_ready, 1)
                for j in range(NG):
                    dve.wait_ge(u_ready, NG * step + j + 1)
                    t.mark(v.bn_stats(stat2[:, 0, j], u[:, j, 0:C0]))
                    k = t.mark(v.bn_stats(stat2[:, 1, j], u[:, j, C0:D]))
                t.wait(k)
                straight(moments(nc, t, stat2[:, 0], C0, mean2[:], var2[:], tmps(NG)))
                straight(moments(nc, t, stat2[:, 1], CV, mean3[:], var3[:], [tmp[:, i, NG:2 * NG] for i in range(4)]))
                t.link(v.tensor_tensor(tmp[:, 3, 0:NG], mean3[:], mean3[:], ALU.mult))
                t.mark(v.scalar_tensor_tensor(e[:, 1], e[:, 0], EPS, var2[:], ALU.mult, ALU.add))
                t.mark(v.tensor_scalar(e[:, 2], e[:, 0], EPS, None, ALU.mult))
                t.link(v.tensor_tensor(tmp[:, 3, 0:NG], tmp[:, 3, 0:NG], var3[:], ALU.add))
                t.link(v.scalar_tensor_tensor(e[:, 2], tmp[:, 3, 0:NG], 3.0, e[:, 2], ALU.mult, ALU.add))
                flat = lambda a: a.rearrange("p a b -> p (a b)")
                straight(rsqrt(nc, t, flat(r[:]), flat(e[:]), tmp[:, 0], r_ready))
                t.close()
                dve.wait_ge(r_ready, step + 1)
                dve.wait_ge(x1_out, 16 * step)
                for j in range(NG):
                    v.scalar_tensor_tensor(x1[:, j], u[:, j], r[:, 0, j:j + 1], x[:, b, j], ALU.mult, ALU.add)
                dve.wait_ge(g_out, 16 * step)
                for j in range(NG):
                    k = v.tensor_scalar(g[:, j, 0:C0], u[:, j, 0:C0], mean2[:, j:j + 1], r[:, 1, j:j + 1],
                                        ALU.subtract, ALU.mult)
                k.then_inc(out_ready, 1)

            @block.scalar
            def _(act):
                with act.Fori(0, PAIRS) as i:
                    for b in range(2):
                        act_step(act, 2 * i + b, b)
                if ODD:
                    act_step(act, N_STEPS - 1, 0)

            @block.vector
            def _(dve):
                for j in range(NG):
                    nc.vector.tensor_copy(fill[:, j], w["l1"]["fill"]).then_inc(filled, 1)
                with dve.Fori(0, PAIRS) as i:
                    for b in range(2):
                        dve_step(dve, 2 * i + b, b, i)
                if ODD:
                    dve_step(dve, N_STEPS - 1, 0, PAIRS)


class Radial:

    LN = EG + MOMENTS + 1 + RSQRT + 1

    def __init__(self, nc, io, w, ctx, T):
        self.nc, self.io, self.l, self.ident, self.groups = nc, io, w["l1"], w["ident"], T // EG
        sb = lambda n, s: ctx.enter_context(nc.sbuf_tensor("r_" + n, s, F32))
        pb = lambda n, s: ctx.enter_context(nc.psum_tensor("r_" + n, s, F32))
        sem = lambda n: ctx.enter_context(nc.semaphore("r_" + n))
        both = lambda f, n, *a: [f(f"{n}{i}", *a) for i in range(2)]
        self.rad_in = sb("rad_in", [65, EG * P])
        self.h = [sb("h1", [65, EG * P]), sb("h2", [64, EG * P])]
        self.z, self.stats, self.tmp = both(sb, "z", [P, EG, 64]), both(sb, "stats", [P, EG, 6]), both(sb, "tmp", [P, 4, EG])
        self.mean, self.var, self.factor = (both(sb, n, [P, EG]) for n in ("mean", "var", "factor"))
        self.hz, self.zt = both(pb, "hz", [P, 512]), both(pb, "zt", [64, EG * P])
        self.loaded, self.stored, self.ones_ready, self.gate_pe = (sem(n) for n in ("loaded", "stored", "ones_ready", "gate_pe"))
        self.vec, self.h_ready, self.r_ready, self.z_ready, self.zt_ready, self.ht_ready = (
            both(sem, n) for n in ("vec", "h_ready", "r_ready", "z_ready", "zt_ready", "ht_ready"))

    def copies(self, sp):
        part = lambda m, g: m[:, bass.ds(g * (EG * P), EG * P)]

        def load(g):
            sp.dma_start(self.rad_in[0:64], part(self.io["attr64"], g)).then_inc(self.loaded, 16)

        def store(g):
            sp.wait_ge(self.ht_ready[1], g + 1)
            sp.dma_start(part(self.io["rad"], g), self.h[1][:]).then_inc(self.stored, 16)

        for g in range(3):
            if g:
                sp.wait_ge(self.h_ready[0], g)
            load(g)
        with sp.Fori(0, self.groups - 3) as i:
            sp.wait_ge(self.h_ready[0], i + 3)
            load(i + 3)
            store(i)
        for g in range(self.groups - 3, self.groups):
            store(g)
        sp.wait_ge(self.stored, 16 * self.groups)

    def hidden(self, pe, g, n):
        pe.wait_ge(self.z_ready[n], g)
        if n == 0:
            pe.wait_ge(self.loaded, 16 * g + 16)
        else:
            pe.wait_ge(self.ht_ready[0], g + 1)
        inp, wt = ((self.rad_in, self.l["r1"]), (self.h[0], self.l["r2"]))[n]
        for j in range(EG):
            last = self.nc.tensor.matmul(self.hz[n][:, j * 64:(j + 1) * 64], inp[:, j * P:(j + 1) * P], wt, start=True, stop=True)
        last.then_inc(self.h_ready[n], 1)

    def turn(self, pe, g, n):
        pe.wait_ge(self.z_ready[n], g + 1)
        pe.sem_inc(self.gate_pe, 1)
        pe.wait_ge(self.ht_ready[n], g)
        pe.sem_inc(self.gate_pe, 1)
        for j in range(EG):
            last = self.nc.tensor.transpose(self.zt[n][:, j * P:(j + 1) * P], self.z[n][:, j], self.ident)
        last.then_inc(self.zt_ready[n], 1)

    def gates(self, act, g, n):
        act.wait_ge(self.zt_ready[n], g + 1)
        if n == 0:
            act.wait_ge(self.h_ready[1], g)
        else:
            act.wait_ge(self.stored, 16 * g)
        self.nc.scalar.activation(self.h[n][0:64], self.zt[n][:], ACT.Silu, bias=self.l[f"rbe{n + 1}"],
                                  scale=self.l[f"rg{n + 1}"]).then_inc(self.ht_ready[n], 1)

    def ones(self):
        self.nc.vector.memset(self.h[0][64:65], 1.0)
        self.nc.vector.memset(self.rad_in[64:65], 1.0).then_inc(self.ones_ready, 1)

    def layer_norm(self, dve, g, n):
        v, z, mean, var, factor, tmp = self.nc.vector, self.z[n], self.mean[n], self.var[n], self.factor[n], self.tmp[n]
        t = Tick(dve, self.vec[n], g, self.LN)
        wide = lambda a: a[:].unsqueeze(2).to_broadcast([P, EG, 64])
        dve.wait_ge(self.h_ready[n], g + 1)
        for j in range(EG):
            k = t.mark(v.bn_stats(self.stats[n][:, j], self.hz[n][:, j * 64:(j + 1) * 64]))
        yield
        t.wait(k)
        yield from moments(self.nc, t, self.stats[n][:], 64, mean[:], var[:], [tmp[:, i] for i in range(4)])
        c = t.mark(v.tensor_scalar(var[:], var[:], EPS, None, ALU.add))
        dve.wait_ge(self.zt_ready[n], g)
        t.mark(v.tensor_tensor(z[:], self.hz[n][:, 0:EG * 64].rearrange("p (j c) -> p j c", c=64), wide(mean), ALU.subtract))
        t.wait(c)
        yield from rsqrt(self.nc, t, factor[:], var[:], tmp[:, 0], self.r_ready[n])
        t.close()
        yield
        dve.wait_ge(self.r_ready[n], g + 1)
        v.tensor_tensor(z[:], z[:], wide(factor), ALU.mult).then_inc(self.z_ready[n], 1)


def edges(nc, io, w, flags, T, layer, vals, logits):
    H = (4, 8)[layer]
    SW, VW = C0 // H, C1 // H
    STEPS = T // EG
    KINDS = ("CBA", "BA")[layer]
    U = EG * len(KINDS)
    LAST_KIND = KINDS[0]
    K = 2 * EG
    l = w[("l0", "l1")[layer]]
    table = io[("g", "x1")[layer]]
    RADK = (16, 65)[layer]
    mrow = w[f"mrow{layer}"]
    with ExitStack() as ctx:
        name = lambda n: f"e{layer}_{n}"
        sb = lambda n, s, dt=F32: ctx.enter_context(nc.sbuf_tensor(name(n), s, dt))
        pb = lambda n, s: ctx.enter_context(nc.psum_tensor(name(n), s, F32))
        sem = lambda n: ctx.enter_context(nc.semaphore(name(n)))
        rows = sb("rows", [P, K, D])
        index = sb("index", [P, K], I32)
        yg = sb("yg", [P, 3 * EG, 6])
        rad_in = sb("rad_in", [RADK, EG * P])
        turned = sb("turned", [P, len(KINDS), RING, 3 * P])
        msg = sb("msg", [P, RING, D])
        prod = sb("prod", [P, EG, 384])
        act_a = sb("act_a", [P, EG, C0])
        value = sb("value", [P, EG, D])
        acc_b, acc_c = sb("acc_b", [P, 3, CV]), sb("acc_c", [P, 3, CV])
        dots_a, dots_b, dot = sb("dots_a", [P, CV]), sb("dots_b", [P, CV]), sb("dot", [P, C1])
        tp = pb("tp", [P, RING, 512])
        mm = pb("mm", [P, RING, 512])
        o1 = pb("o1", [P, RING, 512])
        if layer == 0:
            normed = rows
            o2 = pb("o2", [P, RING, 512])
            val = sb("val", [P, EG, 224])
            val_ready, hc_ready = sem("val_ready"), sem("hc_ready")
        else:
            u, normed = sb("u", [P, K, D]), sb("normed", [P, K, D])
            stats = sb("stats", [P, K, 6])
            stat2 = sb("stat2", [P, 2, K, 6])
            mean, negm, var = sb("mean", [P, K]), sb("negm", [P, K]), sb("var", [P, K])
            mean2, var2 = sb("mean2", [P, 2, K]), sb("var2", [P, 2, K])
            share = sb("share", [P, 2 * K])
            e, r, tmp = sb("e", [P, 2, K]), sb("r", [P, 2, K]), sb("tmp", [P, 4, 2 * K])
            edge_vec = sb("edge_vec", [P, T, 3])
            negm_ready, u_ready, ns_ready, nv_ready = sem("negm_ready"), sem("u_ready"), sem("ns_ready"), sem("nv_ready")
            r_ready = sem("r_ready")
        gathered = [sem(f"gathered{j}") for j in range(EG)]
        rad_ready, pool_gate, index_ready = sem("rad_ready"), sem("pool_gate"), sem("index_ready")
        tp_ready, mm_ready = {k: sem("tp_ready" + k) for k in KINDS}, {k: sem("mm_ready" + k) for k in KINDS}
        tp_moved, msg_ready, prod_ready, ab_ready = sem("tp_moved"), sem("msg_ready"), sem("prod_ready"), sem("ab_ready")
        value_ready, kept, logit_ready = sem("value_ready"), sem("kept"), sem("logit_ready")
        vec, zeroed, gate_pe = sem("vec"), sem("zeroed"), sem("gate_pe")
        y_ready, yg_ready = sem("y_ready"), sem("yg_ready")

        TWO = 2
        S0, SN = C1, (160, 128)[layer]
        B0 = S0 + SN

        def heads(j):
            return value[:, j].rearrange("p (h c) -> p h c", h=H)

        LAG = {"A": 0, "B": 1, "C": 2}
        DEPTH = len(KINDS)

        def kinds_at(g):
            return "".join(k for k in KINDS if 0 <= g - LAG[k] < STEPS)

        def units_before(g):
            return EG * sum(len(kinds_at(i)) for i in range(g))

        def groups(i, start):
            return {"A": i + start, "B": i + (start - 1), "C": i + (start - 2) if start > 1 or isinstance(i, int) else None,
                    "N": i + (start + 1), "since": i}

        def next_group(at, kind):
            return at[{"A": "N", "B": "A", "C": "B"}[kind]]

        LOOPED = range(DEPTH - 1, STEPS if layer == 0 else STEPS - 1)

        def run_steps(run, body):
            first = lambda g: kinds_at(g)[0] if kinds_at(g) else None
            for g in range(LOOPED.start):
                body(groups(g, 0), units_before(g), kinds_at(g), True, first(g + 1))
            with run.Fori(0, len(LOOPED)) as i:
                body(groups(i, LOOPED.start), i * U + units_before(LOOPED.start), KINDS, True, KINDS[0])
            for g in range(LOOPED.stop, STEPS + DEPTH - 1):
                body(groups(g, 0), units_before(g), kinds_at(g), False, first(g + 1))

        def units(kinds):
            return [(k, j) for j in range(EG) for k in kinds]

        with nc.Block() as block:
            @block.sync
            def _(sp):
                def load(g):
                    if layer == 0:
                        sp.dma_start(rad_in[:], io["attr16"][:, bass.ds(g * (EG * P), EG * P)]).then_inc(rad_ready, 16)
                    else:
                        sp.dma_start(rad_in[0:64], io["rad"][:, bass.ds(g * (EG * P), EG * P)]).then_inc(rad_ready, 16)

                if layer == 1:
                    sp.dma_start(edge_vec[:], io["attr3"]).then_inc(y_ready, 16)
                load(0)
                with sp.Fori(0, STEPS - 1) as g:
                    sp.wait_ge(mm_ready["A"], EG * g + EG + TWO)
                    load(g + 1)

            @block.gpsimd
            def _(pool):
                def hold(s, value):
                    pool.wait_ge(s, value)
                    pool.sem_inc(pool_gate, 1)

                bound = pool.to_reg(io["rows"] - 1)
                with pool.Fori(0, STEPS) as g:
                    for j in range(EG):
                        hold(gathered[j], 32 * g)
                    nc.gpsimd.tensor_copy(index[:, 0:EG], flags["src"][:, bass.ds(g * EG, EG)]).then_inc(index_ready, 1)
                    nc.gpsimd.tensor_copy(index[:, EG:K], flags["dst"][:, bass.ds(g * EG, EG)]).then_inc(index_ready, 1)
                    hold(index_ready, 2 * g + 2)
                    for j in range(EG):
                        if layer == 0:
                            hold(tp_ready["A"], EG * g + j + 1)
                        else:
                            hold(u_ready, K * g + 2 * j + 2)
                        for s in range(2):
                            at = index[:, s * EG + j:s * EG + j + 1].bitcast(U32)
                            nc.gpsimd.indirect_dma_start(rows[:, 2 * j + s], None, table,
                                                         bass.IndirectOffsetOnAxis(ap=at, axis=0),
                                                         bounds_check=bound).then_inc(gathered[j], 16)

            @block.tensor
            def _(pe):
                for k in KINDS:
                    pe.sem_inc(tp_ready[k], EG)
                    pe.sem_inc(mm_ready[k], TWO)
                pe.wait_ge(zeroed, 4)

                def turn(g, j, kind, n, slot):
                    pe.wait_ge(tp_moved, n + 1)
                    if kind == "A":
                        if layer == 0:
                            pe.wait_ge(gathered[j], 32 * g + 32)
                        else:
                            pe.wait_ge(ns_ready, K * g + 2 * j + 2)
                            pe.wait_ge(nv_ready, K * g + 2 * j + 2)
                        src, cuts = normed[:, 2 * j:2 * j + 2].rearrange("p s c -> p (s c)"), (0, 128, 256, 320)
                    elif kind == "B":
                        pe.wait_ge(prod_ready, EG * g + j + 1 + TWO)
                        src, cuts = prod[:, j], (0, 128, 256, 352)
                    else:
                        pe.wait_ge(val_ready, EG * g + j + 1 + TWO)
                        src, cuts = val[:, j], (0, 128, 224)
                    for c in range(len(cuts) - 1):
                        m = cuts[c + 1] - cuts[c]
                        last = nc.tensor.transpose(tp[0:m, slot, c * P:(c + 1) * P], src[:, cuts[c]:cuts[c + 1]], w["ident"])
                    last.then_inc(tp_ready[kind], 1)

                def multiply(g, j, kind, n):
                    q = j % RING
                    T0, T1, T2 = (turned[:, KINDS.index(kind), q, c * P:(c + 1) * P] for c in range(3))
                    pe.wait_ge(tp_moved, n + 1 + TWO)
                    if kind == "A":
                        if j == 0:
                            pe.wait_ge(rad_ready, 16 * g + 16)
                        pe.wait_ge(prod_ready, EG * g + j + 1)
                        o = mm[:, q]
                        nc.tensor.matmul(o[:, 0:D], T0, l["in0"], start=True, stop=False)
                        nc.tensor.matmul(o[:, 0:D], T1, l["in1"], start=False, stop=False)
                        nc.tensor.matmul(o[:, 0:D], T2[0:64], l["in2"], start=False, stop=False)
                        nc.tensor.matmul(o[:, 0:D], flags["ones"][0:1, :], mrow, start=False, stop=True)
                        last = nc.tensor.matmul(o[:, D:D + WN], rad_in[:, j * P:(j + 1) * P], l["rad"], start=True, stop=True)
                    elif kind == "B":
                        pe.wait_ge(val_ready if layer == 0 else value_ready, EG * g + j + 1)
                        o = o1[:, q]
                        nc.tensor.matmul(o[:, 0:B0], T0, l["first"], start=True, stop=True)
                        nc.tensor.matmul(o[:, S0:B0 + CV], T1, l["second"], start=False, stop=True, skip_group_check=True)
                        if layer == 1:
                            nc.tensor.matmul(o[:, S0:B0], flags["ones"][0:1, :], l["sbias"], start=False, stop=True,
                                             skip_group_check=True)
                        last = nc.tensor.matmul(o[:, B0 + CV:B0 + 2 * CV + 2 * C1], T2[0:CV], l["third"], start=False, stop=True,
                                                skip_group_check=True)
                    else:
                        pe.wait_ge(value_ready, EG * g + j + 1)
                        o = o2[:, q]
                        nc.tensor.matmul(o[:, 0:160], T0, l["out0"], start=True, stop=True)
                        last = nc.tensor.matmul(o[:, 160:416], T1[0:CV], l["out1"], start=True, stop=True)
                    last.then_inc(mm_ready[kind], 1)

                def body(at, base, kinds, norm, ahead):
                    todo = units(kinds)
                    for i, (kind, j) in enumerate(todo):
                        if i + 1 < len(todo):
                            k, jj = todo[i + 1]
                            turn(at[k], jj, k, base + (i + 1), (i + 1) % RING)
                        elif ahead:
                            turn(next_group(at, ahead), 0, ahead, base + len(todo), 0)
                        multiply(at[kind], j, kind, base + i)

                turn(0, 0, "A", 0, 0)
                run_steps(pe, body)

            @block.scalar
            def _(act):
                act.sem_inc(tp_moved, TWO)
                if layer == 1:
                    act.sem_inc(u_ready, K)

                def move(g, j, kind, n, slot):
                    cols = (2 if kind == "C" else 3) * P
                    act.wait_ge(tp_ready[kind], EG * g + j + 1 + EG)
                    act.wait_ge(mm_ready[kind], EG * g + j + 1)
                    nc.scalar.copy(turned[:, KINDS.index(kind), j % RING, 0:cols], tp[:, slot, 0:cols]).then_inc(tp_moved, 1)

                def after(g, j, kind):
                    act.wait_ge(mm_ready[kind], EG * g + j + 1 + TWO)
                    if kind == "A":
                        act.wait_ge(prod_ready, EG * g + j + 1)
                        nc.scalar.copy(msg[:, j % RING], mm[:, j % RING, 0:D]).then_inc(msg_ready, 1)
                    elif kind == "B":
                        o = o1[:, j % RING]
                        act.wait_ge(logit_ready, g)
                        if layer == 0:
                            act.wait_ge(tp_ready["C"], EG * g + j + 1)
                            nc.scalar.activation(act_a[:, j], o[:, S0:S0 + C0], ACT.Copy, scale=0.2)
                            nc.scalar.activation(val[:, j, 0:96], o[:, S0 + C0:B0], ACT.Sigmoid).then_inc(ab_ready, 1)
                        else:
                            act.wait_ge(kept, g)
                            nc.scalar.activation(act_a[:, j], o[:, S0:S0 + C0], ACT.Tanh, scale=0.5)
                            nc.scalar.copy(heads(j)[:, :, 0:SW], o[:, S0 + C0:B0].rearrange("p (h c) -> p h c", h=H)).then_inc(ab_ready, 1)
                    else:
                        act.wait_ge(kept, g)
                        act.wait_ge(yg_ready, g + (LAG["C"] + 1))
                        nc.scalar.activation(heads(j)[:, :, 0:SW], o2[:, j % RING, 0:C0].rearrange("p (h c) -> p h c", h=H),
                                             ACT.Copy, scale=yg[:, j, 0:1]).then_inc(hc_ready, 1)

                def relu(g):
                    act.wait_ge(negm_ready, g + 1)
                    act.wait_ge(ns_ready, K * g)
                    for k in range(K):
                        nc.scalar.activation(u[:, k], rows[:, k], ACT.Relu, bias=negm[:, k:k + 1]).then_inc(u_ready, 1)

                def vectors(g):
                    act.wait_ge(r_ready, g + 2)
                    for k in range(K):
                        if k % 2 == 0:
                            act.wait_ge(tp_ready["A"], EG * g + k // 2 + 1)
                        nc.scalar.activation(normed[:, k, C0:D], u[:, k, C0:D], ACT.Copy, scale=r[:, 1, k:k + 1]).then_inc(nv_ready, 1)

                def body(at, base, kinds, norm, ahead):
                    todo = units(kinds)
                    for i, (kind, j) in enumerate(todo):
                        if i + 1 < len(todo):
                            k, jj = todo[i + 1]
                            move(at[k], jj, k, base + (i + 1), (i + 1) % RING)
                        elif ahead:
                            move(next_group(at, ahead), 0, ahead, base + len(todo), 0)
                        after(at[kind], j, kind)
                        if layer == 1 and norm and kind == "A":
                            if j == 1:
                                relu(at["N"])
                            if j == 3:
                                vectors(at["N"])

                act.wait_ge(zeroed, 4)
                if layer == 1:
                    relu(0)
                    vectors(0)
                move(0, 0, "A", 0, 0)
                run_steps(act, body)

            @block.vector
            def _(dve):
                v = nc.vector
                dve.sem_inc(prod_ready, TWO)
                dve.sem_inc(value_ready, TWO)
                if layer == 0:
                    dve.sem_inc(val_ready, TWO)
                for q in range(RING):
                    v.memset(tp[:, q], 0.0).then_inc(zeroed, 1)
                y, before = flags["y"], 0
                if layer == 0:
                    v.memset(dot[:], 0.0).then_inc(zeroed, 2)
                else:
                    v.memset(share[:, 0:K], 1.0 / C0)
                    v.memset(share[:, K:], 1.0 / CV)
                    v.memset(rad_in[64:65], 1.0).then_inc(zeroed, 2)
                    dve.wait_ge(y_ready, 16)
                    t = Tick(dve, vec, 0, 0)
                    yy = edge_vec
                    sq, ln, length, inverse, spare = y[:, :, 0], *(logits[:, :, n] for n in range(4))
                    t.link(v.tensor_tensor(sq, yy[:, :, 0], yy[:, :, 0], ALU.mult))
                    for c in (1, 2):
                        t.link(v.tensor_tensor(ln, yy[:, :, c], yy[:, :, c], ALU.mult))
                        t.link(v.tensor_tensor(sq, sq, ln, ALU.add))
                    t.link(v.tensor_scalar(length, sq, 1e-12, None, ALU.add))
                    straight(rsqrt(nc, t, inverse, length, spare, r_ready))
                    dve.wait_ge(r_ready, 1)
                    for at, c in enumerate((0, 1, 2, 0, 1)):
                        t.mark(v.tensor_tensor(y[:, :, at + 1], yy[:, :, c], inverse, ALU.mult))
                    t.wait(t.n)
                    before = t.n

                vec3 = lambda a: a.rearrange("p (d c) -> p d c", d=3)
                wide = lambda a: a.unsqueeze(1).to_broadcast([P, 3, C1])

                class Vectors:

                    def __init__(self, t, acc, o, cols, at, outs):
                        self.t, self.acc, self.o, self.cols, self.y, self.outs = t, acc, o, cols, yg[:, at], outs

                    def components(self, at):
                        return self.y[:, at:at + 3].unsqueeze(2).to_broadcast([P, 3, C1])

                    def outer(self):
                        a = self.cols[0]
                        self.n = self.t.mark(v.tensor_tensor(vec3(self.acc[:, 0]), wide(self.o[:, a:a + C1]), self.components(1), ALU.mult))

                    def turned(self, i):
                        c = self.cols[2] + (1 + i) * C1
                        self.n = self.t.mark(v.tensor_tensor(vec3(self.acc[:, 1 + i]), vec3(self.o[:, c:c + CV]),
                                                             self.components(3 - i), ALU.mult))

                    def plus(self):
                        self.t.wait(self.n - 1)
                        B, acc = self.o[:, self.cols[1]:self.cols[1] + CV], self.acc[:, 0]
                        if layer == 0:
                            self.n = self.t.mark(v.scalar_tensor_tensor(acc, B, self.y[:, 0:1], acc, ALU.mult, ALU.add))
                        else:
                            self.n = self.t.mark(v.tensor_tensor(acc, B, acc, ALU.add))

                    def cross(self):
                        self.n = self.t.mark(v.tensor_tensor(self.acc[:, 1], self.acc[:, 1], self.acc[:, 2], ALU.subtract))

                    def all(self):
                        self.t.wait(self.n)
                        return v.tensor_tensor(self.outs, self.acc_as(0), self.acc_as(1), ALU.add)

                    def acc_as(self, i):
                        a = vec3(self.acc[:, i])
                        return self.acc[:, i] if self.outs.shape[1] == CV else a.rearrange("p d (h c) -> p h d c", h=H)

                VECTORS = 5

                def tile(t, at, j, kinds, more):
                    by_head = lambda: heads(j)[:, :, SW:].rearrange("p h (d c) -> p h d c", d=3)
                    b = Vectors(t, acc_b, o1[:, j % RING], (0, B0, B0 + CV), EG + j,
                                acc_b[:, 0] if layer == 0 else by_head()) if "B" in kinds else None
                    c = Vectors(t, acc_c, o2[:, j % RING], (64, 160, 256), j, by_head()) if "C" in kinds else None
                    a = "A" in kinds
                    both = [x for x in (c, b) if x]
                    if c:
                        dve.wait_ge(hc_ready, EG * at["C"] + j + 1)
                        dve.wait_ge(value_ready, EG * at["C"] + j + TWO)
                        t.mark(v.tensor_tensor(heads(j)[:, :, 0:SW], c.o[:, 96:160].rearrange("p (h c) -> p h c", h=H),
                                               heads(j)[:, :, 0:SW], ALU.add))
                    if b:
                        dve.wait_ge(ab_ready, EG * at["B"] + j + 1)
                        scalars = b.o[:, S0:S0 + C0]
                        if layer == 0:
                            t.mark(v.tensor_tensor(act_a[:, j], act_a[:, j], scalars, ALU.max))
                        else:
                            dve.wait_ge(value_ready, EG * at["B"] + j + TWO)
                            t.mark(v.scalar_tensor_tensor(act_a[:, j], act_a[:, j], 1.5, scalars, ALU.add, ALU.mult))
                    more()
                    for x in both:
                        x.outer()
                        x.turned(0)
                        more()
                    for x in both:
                        x.plus()
                        more()
                    for x in both:
                        x.turned(1)
                        more()
                    if a:
                        dve.wait_ge(msg_ready, EG * at["A"] + j + 1)
                        dve.wait_ge(tp_ready["B"], EG * at["A"] + j + 1)
                        dve.wait_ge(prod_ready, EG * at["A"] + j + TWO)
                        y, m, ww, x = yg[:, 2 * EG + j], msg[:, j % RING], mm[:, j % RING, D:D + 256], prod[:, j]
                        ms, mv = m[:, 0:C0], m[:, C0:D]
                        ka = t.mark(v.tensor_tensor(vec3(dots_a[:]), vec3(mv), y[:, 1:4].unsqueeze(2).to_broadcast([P, 3, C1]), ALU.mult))
                        more()
                    for z in both:
                        t.wait(z.n)
                        z.cross()
                        more()
                    if a:
                        t.wait(ka)
                        ka = t.mark(v.tensor_reduce(dot[:], dots_a[:].rearrange("p (d c) -> p c d", d=3), AX_X, ALU.add))
                        more()
                    if c:
                        c.all().then_inc(value_ready, 1)
                    if b:
                        step = b.all()
                        if layer == 0:
                            kb = t.mark(step)
                            dve.wait_ge(tp_ready["C"], EG * at["B"] + j + 1)
                        else:
                            step.then_inc(value_ready, 1)
                    more()
                    if a:
                        if layer == 0:
                            v.scalar_tensor_tensor(x[:, 0:C0], ww[:, 0:C0], y[:, 0:1], ms, ALU.mult, ALU.mult)
                            v.tensor_tensor(x[:, C0:2 * C0], ww[:, C0:2 * C0], ms, ALU.mult)
                        else:
                            v.tensor_tensor(x[:, 0:2 * C0].rearrange("p (n c) -> p n c", n=2), ww[:, 0:2 * C0].rearrange("p (n c) -> p n c", n=2),
                                            ms.unsqueeze(1).to_broadcast([P, 2, C0]), ALU.mult)
                        more()
                    if b and layer == 0:
                        t.wait(kb)
                        vectors = val[:, j, 128:224]
                        kb = t.mark(v.tensor_tensor(vec3(vectors), vec3(acc_b[:, 0]), wide(val[:, j, 64:96]), ALU.mult))
                    if a:
                        out = x[:, 128:384].rearrange("p (n q) -> p n q", n=2)[:, :, 0:CV].rearrange("p n (d c) -> p n d c", d=3)
                        by = ww[:, 128:256].rearrange("p (n q) -> p n q", n=2)[:, :, 0:C1].unsqueeze(2).to_broadcast([P, 2, 3, C1])
                        v.tensor_tensor(out, by, vec3(mv).unsqueeze(1).to_broadcast([P, 2, 3, C1]), ALU.mult)
                        more()
                    if b and layer == 0:
                        t.wait(kb)
                        kb = t.mark(v.tensor_tensor(vec3(dots_b[:]), vec3(vectors), b.components(1), ALU.mult))
                    if a:
                        t.wait(ka)
                        v.tensor_tensor(x[:, 224:256], ww[:, 160:192], dot[:], ALU.mult).then_inc(prod_ready, 1)
                        more()
                    if b and layer == 0:
                        t.wait(kb)
                        v.tensor_reduce(val[:, j, 96:128], dots_b[:].rearrange("p (d c) -> p c d", d=3), AX_X, ALU.add).then_inc(val_ready, 1)

                TILE = {"A": 2, "B": 1 + VECTORS + (3 if layer == 0 else 0), "C": 1 + VECTORS}

                def row_moments(t, g):
                    for k in range(K):
                        if k % 2 == 0:
                            dve.wait_ge(gathered[k // 2], 32 * g + 32)
                        n = t.mark(v.bn_stats(stats[:, k], rows[:, k]))
                    yield
                    t.wait(n)
                    yield from moments(nc, t, stats[:], D, mean[:], var[:], [tmp[:, i, 0:K] for i in range(4)])
                    v.tensor_scalar(negm[:], mean[:], -1.0, None, ALU.mult).then_inc(negm_ready, 1)
                    t.mark(v.tensor_scalar(var[:], var[:], EPS, EPS, ALU.add, ALU.mult))

                def row_factors(t, g):
                    flat = lambda a: a.rearrange("p a b -> p (a b)")
                    for k in range(K):
                        dve.wait_ge(u_ready, K * g + k + 1 + K)
                        t.mark(v.bn_stats(stat2[:, 0, k], u[:, k, 0:C0]))
                        m = t.mark(v.bn_stats(stat2[:, 1, k], u[:, k, C0:D]))
                    yield
                    t.wait(m)
                    yield from moments(nc, t, stat2[:].rearrange("p i k c -> p (i k) c"), share[:], flat(mean2[:]), flat(var2[:]),
                                       [tmp[:, i] for i in range(4)])
                    t.mark(v.tensor_tensor(tmp[:, 3, 0:K], mean2[:, 1], mean2[:, 1], ALU.mult))
                    yield from link(t, v.tensor_tensor(e[:], var2[:], var[:].unsqueeze(1).to_broadcast([P, 2, K]), ALU.add))
                    yield from link(t, v.tensor_tensor(e[:, 1], e[:, 1], tmp[:, 3, 0:K], ALU.add))
                    dve.wait_ge(nv_ready, K * g)
                    yield from rsqrt(nc, t, flat(r[:]), flat(e[:]), tmp[:, 0], r_ready)

                def row_scalars(g):
                    dve.wait_ge(r_ready, g + 2)
                    for k in range(K):
                        if k % 2 == 0:
                            dve.wait_ge(tp_ready["A"], EG * g + k // 2 + 1)
                        v.tensor_scalar(normed[:, k, 0:C0], u[:, k, 0:C0], mean2[:, 0, k:k + 1], r[:, 0, k:k + 1],
                                        ALU.subtract, ALU.mult).then_inc(ns_ready, 1)

                NORMS = 0 if layer == 0 else (K + MOMENTS + 1) + (2 * K + (MOMENTS + 1) + 3 + RSQRT)
                SUMS = 1

                def ticks(kinds, norm):
                    return EG * sum(TILE[k] for k in kinds) + (NORMS if norm else 0) + (SUMS if "B" in kinds else 0)

                def norm_at(g):
                    return layer == 1 and g < STEPS - 1

                ahead_ticks = before + NORMS
                def ticks_before(g):
                    return ahead_ticks + sum(ticks(kinds_at(i), norm_at(i)) for i in range(g))

                def body(at, base, kinds, norm, ahead):
                    g, peeled = at["A"], isinstance(base, int)
                    if peeled:
                        t = Tick(dve, vec, 0, 0, ticks_before(g))
                    else:
                        t = Tick(dve, vec, at["since"], ticks(kinds, norm), ticks_before(LOOPED.start))
                    if not peeled or g > 0:
                        dve.wait_ge(prod_ready, EG * (min(g, STEPS) if peeled else g) + TWO)
                        if layer == 0:
                            dve.wait_ge(val_ready, EG * at["B"] + TWO)
                    lo = max(3 - DEPTH, 2 - g) if peeled else 3 - DEPTH
                    hi = min(3, STEPS - g + 2) if peeled else 3
                    part = slice(lo * EG, hi * EG)
                    v.tensor_copy(yg[:, part], y[:, bass.ds(at["CBA"[lo]] * EG, (hi - lo) * EG), :]).then_inc(yg_ready, 1)
                    dve.wait_ge(yg_ready, g + 1)
                    for j in range(EG):
                        if norm and layer == 1 and j % 2 == 0:
                            pieces = (row_moments, row_factors)[j // 2](t, at["N"])
                            next(pieces)
                        tile(t, at, j, kinds, (lambda: next(pieces, None)) if norm and layer == 1 else lambda: None)
                        if norm and layer == 1 and (j == 0 or j == EG - 1):
                            straight(pieces)
                    if "B" in kinds:
                        k = t.mark(v.tensor_tensor(act_a[:], act_a[:], l["dot"].unsqueeze(1).to_broadcast([P, EG, C0]), ALU.mult))
                    if LAST_KIND in kinds:
                        done = at[LAST_KIND]
                        dve.wait_ge(value_ready, EG * done + EG + TWO)
                        v.tensor_copy(vals[:, bass.ds(done * EG, EG), :], value[:]).then_inc(kept, 1)
                    if "B" in kinds:
                        t.wait(k)
                        v.tensor_reduce(logits[:, bass.ds(at["B"] * EG, EG), :], act_a[:].rearrange("p j (h c) -> p j h c", h=H),
                                        AX_X, ALU.add).then_inc(logit_ready, 1)
                    assert t.n == ticks(kinds, norm and layer == 1), (t.n, ticks(kinds, norm))
                    if norm and layer == 1:
                        row_scalars(at["N"])

                if layer == 1:
                    t = Tick(dve, vec, 0, 0, before)
                    straight(row_moments(t, 0))
                    straight(row_factors(t, 0))
                    assert t.n == NORMS
                    row_scalars(0)
                run_steps(dve, body)


def softmax(nc, w, flags, T, layer, logits):
    H = (4, 8)[layer]
    DEN_EPS = (1e-16, 1e-12)[layer]
    with ExitStack() as ctx:
        name = lambda n: f"s{layer}_{n}"
        sb = lambda n, s, dt=F32: ctx.enter_context(nc.sbuf_tensor(name(n), s, dt))
        sem = lambda n: ctx.enter_context(nc.semaphore(name(n)))
        fwd, total = sb("fwd", [P, T, H]), sb("total", [P, T, H])
        neg_same, neg_nxt, ends = sb("neg_same", [P, T]), sb("neg_nxt", [P, T]), sb("ends", [P, T])
        edge = sb("edge", [P, 2, H])
        wide = sb("wide", [P, 2 * H, P])
        keys = sb("keys", [P, 2, P])
        eq, neg_eq = sb("eq", [P, 2, 2, P]), sb("neg_eq", [P, 2, 2, P])
        work = sb("work", [P, H, P])
        part = sb("part", [P, 2, 2, H])
        whole = sb("whole", [P, 2, H])
        open_ = sb("open", [P, 1])
        turned = ctx.enter_context(nc.psum_tensor(name("turned"), [P, 2 * H, P], F32))
        keys_t = ctx.enter_context(nc.psum_tensor(name("keys_t"), [P, 2, P], F32))
        vec, wide_ready, turned_ready = sem("vec"), sem("wide_ready"), sem("turned_ready")
        shifted, exp_ready = sem("shifted"), sem("exp_ready")
        ths = [P, T, H]

        with nc.Block() as block:
            @block.tensor
            def _(pe):
                for n in range(3):
                    pe.wait_ge(wide_ready, n + 1)
                    src, out = (keys, keys_t) if n == 0 else (wide, turned)
                    for k in range(2 if n == 0 else 2 * H):
                        last = nc.tensor.transpose(out[:, k], src[:, k], w["ident"])
                    last.then_inc(turned_ready, 1)

            @block.scalar
            def _(act):
                act.wait_ge(shifted, 1)
                nc.scalar.activation(logits[:].rearrange("p t h -> p (t h)"), fwd[:].rearrange("p t h -> p (t h)"),
                                     ACT.Exp).then_inc(exp_ready, 1)

            @block.vector
            def _(dve):
                v = nc.vector
                t = Tick(dve, vec)
                first, last, mid = flags["first"], flags["last"], flags["mid"]
                for n, key in enumerate(("head", "tail")):
                    k = v.tensor_copy(keys[:, n], flags[key][:].to_broadcast([P, P]))
                k.then_inc(wide_ready, 1)
                t.mark(v.tensor_scalar(neg_same[:], flags["same"][:], 1.0, BIG, ALU.subtract, ALU.mult))
                t.mark(v.tensor_scalar(neg_nxt[:], flags["nxt"][:], 1.0, BIG, ALU.subtract, ALU.mult))
                t.mark(v.tensor_scalar(ends[:], flags["nxt"][:], -1.0, 1.0, ALU.mult, ALU.add))
                t.mark(v.tensor_scalar(open_[:], first[:, T - 1:T], -1.0, 1.0, ALU.mult, ALU.add))
                dve.wait_ge(turned_ready, 1)
                for q, key in enumerate(("head", "tail")):
                    for n in range(2):
                        t.mark(v.tensor_scalar(eq[:, q, n], keys_t[:, n], flags[key][:], None, ALU.is_equal))
                t.done()
                t.mark(v.tensor_scalar(neg_eq[:], eq[:], 1.0, BIG, ALU.subtract, ALU.mult))
                if layer == 0:
                    t.mark(v.tensor_copy(flags["tt"][:], eq[:, 1, 1]))
                    t.link(v.tensor_tensor(work[:, 0], eq[:, 1, 1], w["low"], ALU.mult))
                    t.link(v.tensor_reduce(flags["tail_row"][:], work[:, 0], AX_X, ALU.max))
                    t.link(v.scalar_tensor_tensor(open_[:], flags["tail_row"][:], SKIP, flags["tail"][:], ALU.mult, ALU.add))
                    t.link(v.tensor_copy(flags["tail_at"][:], open_[:]))
                    t.link(v.tensor_scalar(open_[:], first[:, T - 1:T], -1.0, 1.0, ALU.mult, ALU.add))

                def across(nth, op_mask, masks, op):
                    v.tensor_copy(wide[:].rearrange("p (n h) c -> p n h c", n=2),
                                  edge[:].unsqueeze(3).to_broadcast([P, 2, H, P])).then_inc(wide_ready, 1)
                    dve.wait_ge(turned_ready, nth)
                    for q in range(2):
                        for n in range(2):
                            t.link(v.tensor_tensor(work[:], turned[:, n * H:(n + 1) * H],
                                                   masks[:, q, n].unsqueeze(1).to_broadcast([P, H, P]), op_mask))
                            t.link(v.tensor_reduce(part[:, q, n], work[:], AX_X, op))
                    t.link(v.tensor_tensor(whole[:], part[:, :, 0], part[:, :, 1], op))

                def combine():
                    bc = lambda f: f[:].unsqueeze(2).to_broadcast(ths)
                    t.link(v.tensor_tensor(total[:], total[:], bc(mid), ALU.mult))
                    for q, f in enumerate((first, last)):
                        t.link(v.tensor_tensor(fwd[:], whole[:, q].unsqueeze(1).to_broadcast(ths), bc(f), ALU.mult))
                        t.link(v.tensor_tensor(total[:], total[:], fwd[:], ALU.add))

                for h in range(H):
                    k = t.mark(v.tensor_tensor_scan(fwd[:, :, h], neg_same[:], logits[:, :, h], -BIG, ALU.add, ALU.max))
                for h in range(H):
                    t.wait(k - H + 1 + h)
                    t.mark(v.tensor_tensor_scan(total[:, ::-1, h], neg_nxt[:, ::-1], fwd[:, ::-1, h], -BIG, ALU.add, ALU.max))
                t.done()
                t.mark(v.tensor_copy(edge[:, 0], total[:, 0]))
                t.link(v.tensor_copy(edge[:, 1], total[:, T - 1]))
                across(2, ALU.add, neg_eq, ALU.max)
                combine()
                v.tensor_tensor(fwd[:], logits[:], total[:], ALU.subtract).then_inc(shifted, 1)
                dve.wait_ge(exp_ready, 1)
                for h in range(H):
                    t.mark(v.tensor_tensor_scan(fwd[:, :, h], flags["same"][:], logits[:, :, h], 0.0, ALU.mult, ALU.add))
                t.done()
                t.link(v.tensor_tensor(fwd[:], fwd[:], ends[:].unsqueeze(2).to_broadcast(ths), ALU.mult))
                for h in range(H):
                    t.mark(v.tensor_tensor_scan(total[:, ::-1, h], flags["nxt"][:, ::-1], fwd[:, ::-1, h], 0.0, ALU.mult, ALU.add))
                t.done()
                t.mark(v.tensor_scalar(edge[:, 0], total[:, 0], open_[:], None, ALU.mult))
                t.link(v.tensor_copy(edge[:, 1], total[:, T - 1]))
                across(3, ALU.mult, eq, ALU.add)
                combine()
                t.link(v.tensor_scalar(total[:], total[:], DEN_EPS, None, ALU.add))
                t.link(v.reciprocal(total[:], total[:]))
                t.link(v.tensor_tensor(logits[:], logits[:], total[:], ALU.mult))


def scatter(nc, io, w, flags, T, layer, vals, alpha):
    H = (4, 8)[layer]
    STEPS = T // EG
    l = w[("l0", "l1")[layer]]
    table = io[("x1", "agg")[layer]]
    with ExitStack() as ctx:
        name = lambda n: f"a{layer}_{n}"
        sb = lambda n, s, dt=F32: ctx.enter_context(nc.sbuf_tensor(name(n), s, dt))
        pb = lambda n, s: ctx.enter_context(nc.psum_tensor(name(n), s, F32))
        sem = lambda n: ctx.enter_context(nc.semaphore(name(n)))
        weighted = sb("weighted", [P, EG, D])
        sums = sb("sums", [P, EG, D])
        merged = sb("merged", [P, D])
        same = sb("same", [P, EG])
        index = sb("index", [P, EG], I32)
        turned = sb("turned", [P, RING, 2 * P])
        rows = sb("rows", [P, EG, D])
        tp, out = pb("tp", [P, RING, 512]), pb("out", [P, RING, 512])
        vec, zeroed, sum_ready, tp_ready = sem("vec"), sem("zeroed"), sem("sum_ready"), sem("tp_ready")
        tp_moved, out_ready, row_ready = sem("tp_moved"), sem("out_ready"), sem("row_ready")
        index_ready, pool_gate = sem("index_ready"), sem("pool_gate")
        written = [sem(f"written{j}") for j in range(EG)]
        tails_ready, merged_ready, tails_written = sem("tails_ready"), sem("merged_ready"), sem("tails_written")
        tiles = EG * STEPS
        net = Radial(nc, io, w, ctx, T) if layer == 0 else None

        def run_steps(run, step):
            step(0, 0, True)
            step(1, 1, True)
            with run.Fori(2, STEPS - 1) as g:
                step(g, 2, True)
            step(STEPS - 1, 2, False)

        with nc.Block() as block:
            if net:
                @block.sync
                def _(sp):
                    net.copies(sp)

            @block.gpsimd
            def _(pool):
                def hold(s, value):
                    pool.wait_ge(s, value)
                    pool.sem_inc(pool_gate, 1)

                bound = pool.to_reg(io["rows"] - 1)
                with pool.Fori(0, STEPS) as g:
                    for j in range(EG):
                        hold(written[j], 16 * g)
                        nc.gpsimd.tensor_copy(index[:, j:j + 1], flags["row"][:, bass.ds(g * EG + j, 1)]).then_inc(index_ready, 1)
                    for j in range(EG):
                        hold(index_ready, EG * g + j + 1)
                        hold(row_ready, EG * g + j + 1 + RING)
                        nc.gpsimd.indirect_dma_start(table, bass.IndirectOffsetOnAxis(ap=index[:, j:j + 1].bitcast(U32), axis=0),
                                                     rows[:, j], None, bounds_check=bound, oob_is_err=False,
                                                     compute_op=ALU.add).then_inc(written[j], 16)
                for j in range(EG):
                    pool.wait_ge(written[j], 16 * STEPS)
                pool.wait_ge(row_ready, tiles + 1 + RING)
                nc.gpsimd.indirect_dma_start(table, bass.IndirectOffsetOnAxis(ap=flags["tail_at"][:].bitcast(U32), axis=0),
                                             rows[:, 0], None, bounds_check=bound, oob_is_err=False,
                                             compute_op=ALU.add).then_inc(tails_written, 16)
                pool.wait_ge(tails_written, 16)

            @block.tensor
            def _(pe):
                pe.sem_inc(tp_ready, EG)

                def turn(i, j, src):
                    pe.wait_ge(tp_moved, i + 1)
                    for c, (a, b) in enumerate(((0, 128), (128, 160))):
                        last = nc.tensor.transpose(tp[0:b - a, j % RING, c * P:(c + 1) * P], src[:, a:b], w["ident"])
                    last.then_inc(tp_ready, 1)

                def turn_sums(g, j):
                    pe.wait_ge(sum_ready, EG * g + j + 1)
                    turn(EG * g + j, j, sums[:, j])

                def project(i, j):
                    pe.wait_ge(tp_moved, i + 1 + RING)
                    pe.wait_ge(row_ready, i + 1)
                    nc.tensor.matmul(out[:, j % RING, 0:D], turned[:, j % RING, 0:P], l["p0"], start=True, stop=False)
                    nc.tensor.matmul(out[:, j % RING, 0:D], turned[0:32, j % RING, P:2 * P], l["p1"],
                                     start=False, stop=True).then_inc(out_ready, 1)

                pe.wait_ge(zeroed, 3)
                def step(g, low, high):
                    if net:
                        if high:
                            net.hidden(pe, g + 1, 0)
                        if low > 0:
                            net.hidden(pe, g - 1, 1)
                    for j in range(EG):
                        if j < EG - 1 or high:
                            turn_sums(g + (j + 1) // EG, (j + 1) % EG)
                            project(EG * g + j, j)
                        if net and j == 0:
                            net.turn(pe, g, 0)
                        if net and j == 1 and low > 1:
                            net.turn(pe, g - 2, 1)

                if net:
                    pe.wait_ge(net.ones_ready, 1)
                    net.hidden(pe, 0, 0)
                turn_sums(0, 0)
                run_steps(pe, step)
                project(tiles - 1, EG - 1)
                if net:
                    net.turn(pe, STEPS - 2, 1)
                    net.hidden(pe, STEPS - 1, 1)
                    net.turn(pe, STEPS - 1, 1)
                pe.wait_ge(row_ready, tiles - 1 + RING)
                nc.tensor.matmul(out[:, 0, 256:256 + D], flags["tt"][:], sums[:, EG - 1], start=True, stop=True).then_inc(tails_ready, 1)
                pe.wait_ge(merged_ready, 1)
                turn(tiles, 0, merged[:])
                project(tiles, 0)

            @block.scalar
            def _(act):
                act.sem_inc(tp_moved, RING)
                act.sem_inc(row_ready, RING)

                def move(i, j):
                    act.wait_ge(tp_ready, i + 1 + EG)
                    nc.scalar.copy(turned[:, j % RING], tp[:, j % RING, 0:2 * P]).then_inc(tp_moved, 1)

                def keep(i, j, uses):
                    act.wait_ge(out_ready, i + 1)
                    act.wait_ge(written[j], 16 * uses)
                    nc.scalar.copy(rows[:, j], out[:, j % RING, 0:D]).then_inc(row_ready, 1)

                act.wait_ge(zeroed, 3)
                def step(g, low, high):
                    for j in range(EG):
                        if j < EG - 1 or high:
                            move(EG * g + j + 1, j + 1)
                        keep(EG * g + j, j, g)
                        if net and j == 0:
                            net.gates(act, g, 0)
                        if net and j == 1 and low > 1:
                            net.gates(act, g - 2, 1)

                move(0, 0)
                run_steps(act, step)
                if net:
                    net.gates(act, STEPS - 2, 1)
                    net.gates(act, STEPS - 1, 1)
                move(tiles, 0)
                keep(tiles, 0, STEPS)

            @block.vector
            def _(dve):
                v = nc.vector
                for q in range(RING):
                    v.memset(tp[:, q], 0.0).then_inc(zeroed, 1)
                v.memset(sums[:], 0.0).then_inc(zeroed, 1)
                dve.wait_ge(zeroed, 3)

                def add_up(g, others):
                    t = Tick(dve, vec, g, 2)
                    dve.wait_ge(sum_ready, EG * g)
                    step = bass.ds(g * EG, EG)
                    t.mark(v.tensor_copy(same[:], flags["same"][:, step]))
                    t.mark(v.tensor_tensor(weighted[:].rearrange("p j (h c) -> p j h c", h=H),
                                           vals[:, step, :].rearrange("p j (h c) -> p j h c", h=H),
                                           alpha[:, step, :].unsqueeze(3).to_broadcast([P, EG, H, D // H]), ALU.mult))
                    t.done()
                    t.close()
                    for j in range(EG):
                        if j:
                            dve.wait_ge(sum_ready, EG * g + j)
                        dve.wait_ge(tp_ready, EG * g + j + 1)
                        v.scalar_tensor_tensor(sums[:, j], sums[:, (j - 1) % EG], same[:, j:j + 1], weighted[:, j],
                                               ALU.mult, ALU.add).then_inc(sum_ready, 1)
                    straight(others)

                def together(*pieces):
                    for _ in zip_longest(*pieces):
                        yield

                def step(g, low, high):
                    norms = []
                    if net and high:
                        norms.append(net.layer_norm(dve, g + 1, 0))
                    if net and low > 0:
                        norms.append(net.layer_norm(dve, g - 1, 1))
                    add_up(g, together(*norms))

                if net:
                    net.ones()
                    straight(net.layer_norm(dve, 0, 0))
                run_steps(dve, step)
                if net:
                    straight(net.layer_norm(dve, STEPS - 1, 1))
                dve.wait_ge(tails_ready, 1)
                v.tensor_copy(merged[:], out[:, 0, 256:256 + D]).then_inc(merged_ready, 1)


def feed(nc, io, w, STEPS):
    N2 = 2 * FG
    c = w["ff"]
    FN = FG * P
    with ExitStack() as ctx:
        sb = lambda n, s, dt=F32: ctx.enter_context(nc.sbuf_tensor("f_" + n, s, dt))
        pb = lambda n, s: ctx.enter_context(nc.psum_tensor("f_" + n, s, F32))
        sem = lambda n: ctx.enter_context(nc.semaphore("f_" + n))
        x, agg, a0 = sb("x", [P, 2, N2, D]), sb("agg", [P, 2, N2, D]), sb("a0", [P, 2, N2])
        u, y = sb("u", [P, N2, D]), sb("y", [P, 2, N2, D])
        norm = sb("norm", [P, 2, N2, 161])
        res, a0_kept = sb("res", [P, 2, N2, D]), sb("a0_kept", [P, 2, N2])
        stats, stat2 = sb("stats", [P, N2, 6]), sb("stat2", [P, 2, N2, 6])
        mean, negm, var = sb("mean", [P, N2]), sb("negm", [P, N2]), sb("var", [P, N2])
        share = sb("share", [P, 2 * N2])
        mean2, var2 = sb("mean2", [P, 2, N2]), sb("var2", [P, 2, N2])
        r, r2, tmp = sb("r", [P, N2]), sb("r2", [P, 2, N2]), sb("tmp", [P, 4, 2 * N2])
        sT, vT = sb("sT", [65, 2, FN]), sb("vT", [CV, 2, FN])
        hid, gate = sb("hid", [P, 2, FN]), sb("gate", [P, 2, FN])
        f0, f1 = sb("f0", [P, 2, FN]), sb("f1", [65, 2, FN])
        o = sb("o", [P, 2, FG, D])
        pS, pV = pb("pS", [65, FN]), pb("pV", [CV, FN])
        pH, pG, p0, p1 = pb("pH", [P, FN]), pb("pG", [P, FN]), pb("p0", [P, FN]), pb("p1", [64, FN])
        pO = pb("pO", [P, 2, 512])
        x_in, o_out = [sem("x_in0"), sem("x_in1")], [sem("o_out0"), sem("o_out1")]
        vec, negm_ready, u_ready, r_ready, y_ready = sem("vec"), sem("negm_ready"), sem("u_ready"), sem("r_ready"), sem("y_ready")
        scale_ready, ns_ready, nv_ready, res_ready = sem("scale_ready"), sem("ns_ready"), sem("nv_ready"), sem("res_ready")
        s_turned, v_turned, s_moved, v_moved = sem("s_turned"), sem("v_turned"), sem("s_moved"), sem("v_moved")
        g_mm, hid_mm, fv_mm, hid_ready, gate_ready = sem("g_mm"), sem("hid_mm"), sem("fv_mm"), sem("hid_ready"), sem("gate_ready")
        f_ready, o_mm, o_ready, gate_pe, pool_gate = sem("f_ready"), sem("o_mm"), sem("o_ready"), sem("gate_pe"), sem("pool_gate")
        grp = lambda a: a.rearrange("(g p j) c -> g p j c", p=P, j=N2)
        xs, aggs, outs = grp(io["x1"]), grp(io["agg"]), grp(io["out"])
        a0s = io["a0"].rearrange("(g p j) c -> g p (j c)", p=P, j=N2)
        FRONT = N2 + MOMENTS + 1 + RSQRT + 2 * N2 + (MOMENTS + 1) + 3 + RSQRT + 1
        HALVES = 2 * STEPS

        def known(n, low, high=STEPS):
            return isinstance(n, int) and low <= n < high

        assert STEPS % 2 and STEPS > 4

        def steps(run, step, peeled=0):
            step(0, 0, True, False, False)
            step(1, 1, True, True, False)
            pairs = (STEPS - 3) // 2
            if pairs > peeled:
                with run.Fori(0, pairs - peeled) as i:
                    step(2 * i + 2, 0, True, True, True)
                    step(2 * i + 3, 1, True, True, True)
            for s in range(2 * (pairs - peeled) + 2, STEPS - 1):
                step(s, s % 2, True, True, True)
            step(STEPS - 1, 0, False, True, True)

        with nc.Block() as block:
            @block.sync
            def _(sp):
                def load(s, b):
                    sp.dma_start(x[:, b], xs[s]).then_inc(x_in[b], 16)
                    sp.dma_start(agg[:, b], aggs[s]).then_inc(x_in[b], 16)
                    sp.dma_start(a0[:, b], a0s[s]).then_inc(x_in[b], 16)

                def store(k, step, h, slot):
                    sp.wait_ge(o_ready, FG * (k + 1))
                    sp.dma_start(outs[step][:, h * FG:(h + 1) * FG], o[:, slot]).then_inc(o_out[slot], 16)

                def step(s, b, front, back, more):
                    if not known(s, STEPS - 2):
                        sp.wait_ge(res_ready, s + 1)
                        load(s + 2, b)
                    if more:
                        store(2 * s - 3, s - 2, 1, 1)
                    if back:
                        store(2 * s - 2, s - 1, 0, 0)

                load(0, 0)
                load(1, 1)
                steps(sp, step, 1)
                store(HALVES - 3, STEPS - 2, 1, 1)
                store(HALVES - 2, STEPS - 1, 0, 0)
                store(HALVES - 1, STEPS - 1, 1, 1)
                for slot in range(2):
                    sp.wait_ge(o_out[slot], 16 * STEPS)

            @block.gpsimd
            def _(pool):
                def hold(s, value):
                    pool.wait_ge(s, value)
                    pool.sem_inc(pool_gate, 1)

                def step(s, b, front, back, more):
                    hold(ns_ready, N2 * (s + 1))
                    if back:
                        hold(o_ready, FG * (2 * s - 2))
                    nc.gpsimd.tensor_copy(a0_kept[:, b], a0[:, b])
                    nc.gpsimd.tensor_tensor(res[:, b], x[:, b], y[:, b], ALU.add).then_inc(res_ready, 1)

                steps(pool, step)

            @block.vector
            def _(dve):
                v = nc.vector
                flat = lambda a: a.rearrange("p a b -> p (a b)")

                def first_moments(t, n, b, nth):
                    dve.wait_ge(x_in[b], 48 * nth + 48)
                    for j in range(N2):
                        k = t.mark(v.bn_stats(stats[:, j], x[:, b, j]))
                    yield
                    t.wait(k)
                    yield from moments(nc, t, stats[:], D, mean[:], var[:], [tmp[:, i, 0:N2] for i in range(4)])
                    v.tensor_scalar(negm[:], mean[:], -1.0, None, ALU.mult).then_inc(negm_ready, 1)
                    yield from link(t, v.tensor_scalar(var[:], var[:], EPS, None, ALU.add))
                    yield from rsqrt(nc, t, r[:], var[:], tmp[:, 0, 0:N2], r_ready)

                def sums(n, b):
                    dve.wait_ge(r_ready, 2 * n + 1)
                    for j in range(N2):
                        dve.wait_ge(u_ready, N2 * n + j + 1)
                        v.scalar_tensor_tensor(y[:, b, j], u[:, j], r[:, j:j + 1], agg[:, b, j],
                                               ALU.mult, ALU.add).then_inc(y_ready, 1)

                def sum_moments(t, n, b):
                    for j in range(N2):
                        dve.wait_ge(y_ready, N2 * n + j + 1)
                        t.mark(v.bn_stats(stat2[:, 0, j], y[:, b, j, 0:C0]))
                        k = t.mark(v.bn_stats(stat2[:, 1, j], y[:, b, j, C0:D]))
                    t.wait(k)

                def factors(t, n, b):
                    yield from moments(nc, t, stat2[:].rearrange("p i j c -> p (i j) c"), share[:], flat(mean2[:]), flat(var2[:]),
                                       [tmp[:, k] for k in range(4)])
                    yield from link(t, v.tensor_tensor(tmp[:, 3, 0:N2], mean2[:, 1], mean2[:, 1], ALU.mult))
                    yield from link(t, v.tensor_tensor(var2[:, 1], var2[:, 1], tmp[:, 3, 0:N2], ALU.add))
                    yield from link(t, v.tensor_scalar(var2[:], var2[:], EPS, None, ALU.add))
                    dve.wait_ge(nv_ready, N2 * n)
                    yield from rsqrt(nc, t, flat(r2[:]), flat(var2[:]), tmp[:, 0], r_ready)
                    yield
                    dve.wait_ge(r_ready, 2 * n + 2)
                    if not known(n, 0, 2):
                        dve.wait_ge(s_turned, 2 * n - 2)
                    t.mark(v.tensor_copy(norm[:, b, :, C0], a0[:, b]))
                    t.close()
                    v.tensor_tensor(r2[:], r2[:], a0[:, b].unsqueeze(1).to_broadcast([P, 2, N2]), ALU.mult).then_inc(scale_ready, 1)

                def scalars(n, b):
                    dve.wait_ge(scale_ready, n + 1)
                    for j in range(N2):
                        v.tensor_scalar(norm[:, b, j, 0:C0], y[:, b, j, 0:C0], mean2[:, 0, j:j + 1], r2[:, 0, j:j + 1],
                                        ALU.subtract, ALU.mult).then_inc(ns_ready, 1)

                def gated(k, slot):
                    dve.wait_ge(fv_mm, k + 1)
                    dve.wait_ge(gate_ready, k + 1)
                    if not known(k, 0, 1):
                        dve.wait_ge(o_mm, FG * (k - 1))
                    v.scalar_tensor_tensor(f0[:, slot], gate[:, slot], 1.0, p0[:], ALU.add, ALU.mult)
                    v.scalar_tensor_tensor(f1[0:64, slot], gate[0:64, slot], 1.0, p1[:], ALU.add, ALU.mult).then_inc(f_ready, 1)

                def outputs(k, step, b, h, uses):
                    dve.wait_ge(res_ready, step + 1)
                    dve.wait_ge(o_out[h], 16 * uses)
                    for j in range(FG):
                        dve.wait_ge(o_mm, FG * k + (j // 2) * 2 + 2)
                        i = h * FG + j
                        v.scalar_tensor_tensor(o[:, h, j], pO[:, j // 2, (j % 2) * D:(j % 2 + 1) * D], a0_kept[:, b, i:i + 1],
                                               res[:, b, i], ALU.mult, ALU.add).then_inc(o_ready, 1)
                        yield

                def step(s, b, front, back, more):
                    t = Tick(dve, vec, s + 1, FRONT)
                    n, o = s + 1, 1 - b
                    earlier = outputs(2 * s - 3, s - 2, b, 1, s - 2) if more else iter(())
                    later = outputs(2 * s - 2, s - 1, o, 0, s - 1) if back else iter(())
                    if front:
                        among(first_moments(t, n, o, (s + 1) // 2 if known(s, 0) else nth[b]), earlier)
                    straight(earlier)
                    if front:
                        if back:
                            dve.wait_ge(res_ready, s)
                        sums(n, o)
                    if back:
                        gated(2 * s - 1, 1)
                    if front:
                        sum_moments(t, n, o)
                        among(factors(t, n, o), later)
                    straight(later)
                    gated(2 * s, 0)
                    if front:
                        scalars(n, o)

                def among(pieces, others):
                    for _ in pieces:
                        next(others, None)

                v.memset(f1[64:65], 1.0)
                v.memset(share[:, 0:N2], 1.0 / C0)
                v.memset(share[:, N2:], 1.0 / CV)
                t = Tick(dve, vec, 0, FRONT)
                straight(first_moments(t, 0, 0, 0))
                sums(0, 0)
                sum_moments(t, 0, 0)
                straight(factors(t, 0, 0))
                scalars(0, 0)
                nth = {}
                step(0, 0, True, False, False)
                step(1, 1, True, True, False)
                with dve.Fori(0, (STEPS - 3) // 2) as i:
                    nth[0], nth[1] = i + 1, i + 2
                    step(2 * i + 2, 0, True, True, True)
                    step(2 * i + 3, 1, True, True, True)
                step(STEPS - 1, 0, False, True, True)
                straight(outputs(HALVES - 3, STEPS - 2, 1, 1, STEPS - 2))
                gated(HALVES - 1, 1)
                for h in range(2):
                    straight(outputs(HALVES - 2 + h, STEPS - 1, 0, h, STEPS - 1))

            @block.tensor
            def _(pe):
                def turn(k, step, b, h):
                    for part, ready, moved, rows, a, done in ((pS, ns_ready, s_moved, 65, 0, s_turned),
                                                              (pV, nv_ready, v_moved, CV, 65, v_turned)):
                        pe.wait_ge(ready, N2 * step + (h + 1) * FG)
                        pe.sem_inc(gate_pe, 1)
                        pe.wait_ge(moved, k)
                        pe.sem_inc(gate_pe, 1)
                        for j in range(FG):
                            last = nc.tensor.transpose(part[:, j * P:(j + 1) * P], norm[:, b, h * FG + j, a:a + rows], w["ident"])
                        last.then_inc(done, 1)

                def hidden(k, slot):
                    pe.wait_ge(s_moved, k + 1)
                    pe.wait_ge(gate_ready, k)
                    nc.tensor.matmul(pG[:], c["s"][:, 128:256], sT[:, slot], start=True, stop=True).then_inc(g_mm, 1)
                    pe.wait_ge(hid_ready, k)
                    nc.tensor.matmul(pH[:], c["s"][:, 0:128], sT[:, slot], start=True, stop=True).then_inc(hid_mm, 1)
                    pe.wait_ge(v_moved, k + 1)
                    pe.wait_ge(f_ready, k)
                    nc.tensor.matmul(p0[:], c["v0"], vT[:, slot], start=True, stop=True)
                    nc.tensor.matmul(p1[:], c["v1"], vT[:, slot], start=True, stop=True).then_inc(fv_mm, 1)

                def output(k, slot):
                    pe.wait_ge(hid_ready, k + 1)
                    pe.wait_ge(f_ready, k + 1)
                    pe.wait_ge(o_ready, FG * k)
                    for j in range(FG):
                        at = slice(j * P, (j + 1) * P)
                        out = pO[:, j // 2, (j % 2) * D:(j % 2 + 1) * D]
                        nc.tensor.matmul(out[:, 0:C0], hid[:, slot, at], c["o"], start=True, stop=True)
                        nc.tensor.matmul(out[:, C0:D], f0[:, slot, at], c["ov0"], start=False, stop=True, skip_group_check=True)
                        nc.tensor.matmul(out, f1[:, slot, at], c["ov1"], start=False, stop=True,
                                         skip_group_check=True).then_inc(o_mm, 1)

                def step(s, b, front, back, more):
                    if back:
                        hidden(2 * s - 1, 1)
                    turn(2 * s, s, b, 0)
                    if back:
                        output(2 * s - 2, 0)
                    turn(2 * s + 1, s, b, 1)
                    hidden(2 * s, 0)
                    if back:
                        output(2 * s - 1, 1)

                steps(pe, step)
                hidden(HALVES - 1, 1)
                output(HALVES - 2, 0)
                output(HALVES - 1, 1)

            @block.scalar
            def _(act):
                def move(k, slot):
                    act.wait_ge(s_turned, k + 1)
                    nc.scalar.copy(sT[:, slot], pS[:]).then_inc(s_moved, 1)
                    act.wait_ge(v_turned, k + 1)
                    if not known(k, 0, 2):
                        act.wait_ge(fv_mm, k - 1)
                    nc.scalar.copy(vT[:, slot], pV[:]).then_inc(v_moved, 1)

                def gate_of(k, slot):
                    act.wait_ge(g_mm, k + 1)
                    if not known(k, 0, 2):
                        act.wait_ge(f_ready, k - 1)
                        act.wait_ge(o_mm, FG * (k - 1))
                    nc.scalar.activation(gate[:, slot], pG[:], ACT.Tanh, scale=0.5).then_inc(gate_ready, 1)

                def hidden_of(k, slot):
                    act.wait_ge(hid_mm, k + 1)
                    nc.scalar.activation(hid[:, slot], pH[:], ACT.Silu).then_inc(hid_ready, 1)

                def relu(n, b):
                    act.wait_ge(negm_ready, n + 1)
                    act.wait_ge(y_ready, N2 * n)
                    for j in range(N2):
                        nc.scalar.activation(u[:, j], x[:, b, j], ACT.Relu, bias=negm[:, j:j + 1]).then_inc(u_ready, 1)

                def vectors(n, b):
                    act.wait_ge(scale_ready, n + 1)
                    if not known(n, 0, 2):
                        act.wait_ge(v_turned, 2 * n - 2)
                    for j in range(N2):
                        nc.scalar.activation(norm[:, b, j, C0 + 1:], y[:, b, j, C0:D], ACT.Copy,
                                             scale=r2[:, 1, j:j + 1]).then_inc(nv_ready, 1)

                def step(s, b, front, back, more):
                    if back:
                        gate_of(2 * s - 1, 1)
                    if front:
                        relu(s + 1, 1 - b)
                    if back:
                        hidden_of(2 * s - 1, 1)
                    move(2 * s, 0)
                    move(2 * s + 1, 1)
                    gate_of(2 * s, 0)
                    hidden_of(2 * s, 0)
                    if front:
                        vectors(s + 1, 1 - b)

                relu(0, 0)
                vectors(0, 0)
                steps(act, step)
                gate_of(HALVES - 1, 1)
                hidden_of(HALVES - 1, 1)


def build(nc, io, N_ROWS, T):
    with ExitStack() as ctx:
        sb = lambda n, s, dt=F32: ctx.enter_context(nc.sbuf_tensor(n, s, dt))
        w = {}
        for key, table in (("all", W_ALL), ("l0", W0), ("l1", W1), ("ff", W2)):
            tile = sb(f"weights_{key}", [P, offsets(table)[1]])
            w["t_" + key] = tile[:]
            w[key] = views(tile, table)
        w["ident"], w["low"] = w["all"]["ident"], w["all"]["low"]
        w["mrow0"], w["mrow1"] = sb("message_bias0", [1, D])[:], sb("message_bias1", [1, D])[:]
        flags = {n: sb(n, [P, T + EG], I32) for n in ("src", "dst", "row")}
        flags |= {n: sb(n, [P, T]) for n in ("same", "nxt", "first", "last", "mid")}
        flags |= {n: sb(n, [P, 1]) for n in ("head", "tail", "tail_row")}
        flags["tail_at"] = sb("tail_at", [P, 1], I32)
        flags["tt"] = sb("tails_equal", [P, P])
        flags["y"] = sb("edge_y", [P, T, 6])
        flags["ones"] = sb("ones", [1, P])
        w["ones"] = flags["ones"]
        io["rows"] = N_ROWS
        prepare(nc, io, w, flags, T)
        nodes(nc, io, w, N_ROWS // (P * NG))
        for layer in range(2):
            with ExitStack() as own:
                H = (4, 8)[layer]
                logits = own.enter_context(nc.sbuf_tensor(f"logits{layer}", [P, T, H], F32))
                vals = own.enter_context(nc.sbuf_tensor(f"vals{layer}", [P, T, D], F32))
                edges(nc, io, w, flags, T, layer, vals, logits)
                softmax(nc, w, flags, T, layer, logits)
                scatter(nc, io, w, flags, T, layer, vals, logits)
        feed(nc, io, w, N_ROWS // (P * 2 * FG))


def place(table, parts):
    at, cols = offsets(table)
    out = np.zeros((P, cols), np.float32)
    for name, pieces in parts.items():
        a, rows, n = at[name]
        for r, c, m in pieces:
            m = np.asarray(m)
            m = m.reshape(-1, 1) if m.ndim == 1 else m
            assert r + m.shape[0] <= rows and c + m.shape[1] <= n, name
            out[r:r + m.shape[0], a + c:a + c + m.shape[1]] = m
    return out


def by_component(m, rows="cd", cols="dc", comps=(0, 1, 2)):
    C, K = m.shape
    n = len(comps)
    out = np.zeros((C, 3, n, K), np.float32)
    for at, d in enumerate(comps):
        out[:, d, at, :] = m
    if rows == "dc":
        out = out.transpose(1, 0, 2, 3)
    if cols == "cd":
        out = out.transpose(0, 1, 3, 2)
    out = out.reshape(3 * C, n * K)
    return out


def value_rows(H, ps, pv):
    SW, VW = C0 // H, C1 // H
    out = np.zeros((H, D // H, D), np.float32)
    out[:, 0:SW, 0:C0] = ps.reshape(H, SW, C0)
    for d in range(3):
        out[:, SW + d * VW:SW + (d + 1) * VW, C0 + d::3] = pv.reshape(H, VW, C1)
    return out.reshape(D, D)


def input_rows(s_src, s_dst, v_src, v_dst):
    out = np.zeros((2 * D, D), np.float32)
    for k, (s, v) in enumerate(((s_src, v_src), (s_dst, v_dst))):
        out[k * D:k * D + C0, 0:C0] = s
        out[k * D + C0:(k + 1) * D, C0:D] = by_component(v)
    return out


def columns(s, v):
    one = np.concatenate([s, np.repeat(v, 3)])
    return np.concatenate([one, one])


def cut(rows):
    return {k: rows[a:b] for k, (a, b) in enumerate(((0, 128), (128, 256), (256, 320)))}


def kernel(**inputs):
    import concourse.bacc as bacc
    from concourse.bass_utils import run_bass_kernel_spmd as run

    a = {k: np.ascontiguousarray(v) for k, v in inputs.items()}
    N, E = a["x"].shape[0], a["src"].shape[0]
    unit = P * max(NG, 2 * FG)
    N_ROWS = -(-N // unit) * unit
    T = -(-E // (P * EG)) * EG
    E_ROWS = P * T
    assert N_ROWS > N
    f32 = np.float32
    L0 = {k[7:]: v for k, v in a.items() if k.startswith("L0_gnn_")}
    L1 = {k[7:]: v for k, v in a.items() if k.startswith("L1_gnn_")}

    def padded(m, rows, fill=0):
        out = np.full((rows, *m.shape[1:]), fill, m.dtype)
        out[:m.shape[0]] = m
        return out

    def by_tile(m):
        return np.ascontiguousarray(padded(m, E_ROWS).reshape(P, T, -1).transpose(2, 1, 0).reshape(m.shape[1], -1))

    spread2 = lambda v: np.broadcast_to(v, (P, v.shape[-1]))
    none = np.zeros(C1, f32)
    in0, g0, b0 = (cut(m) for m in (input_rows(L0["Ws_src"], L0["Ws_dst"], L0["Wv_src"], L0["Wv_dst"]),
                                    columns(L0["gamma_s"], L0["gamma_v"]), columns(L0["beta_s"], none)))
    in1, g1, b1 = (cut(m) for m in (input_rows(L1["msrc_ws"], L1["mdst_ws"], L1["msrc_wv"], L1["mdst_wv"]),
                                    columns(L1["ln1_w0"], L1["ln1_w1"]), columns(L1["ln1_b0"], none)))
    wv, wl, wlin = L0["Wv_val"], L0["Wv_vlin"], L1["lin_wv"]
    val0 = np.concatenate([L0["W_alpha"], L0["Ws_val"]], 1)
    svT = L0["Ws_val"].T
    p0, p1 = value_rows(4, L0["Wps"], L0["Wpv"]), value_rows(8, L1["proj_ws"], L1["proj_wv"])
    diag = lambda m: by_component(m, "dc", "dc")
    around = lambda m: np.concatenate([diag(m), diag(m)[:, 0:2 * C1]], 1)
    w_l0 = place(W0, {
        **{f"in{k}": [(0, 0, in0[k])] for k in range(3)}, **{f"gam{k}": [(0, 0, g0[k])] for k in range(3)},
        **{f"beta{k}": [(0, 0, b0[k])] for k in range(3)}, "rad": [(0, 0, L0["W_rbf"])],
        "first": [(64, 0, wv[0:64]), (0, C1, val0[0:64])], "second": [(96, 0, val0[64:96]), (0, 160, diag(wv[64:96]))],
        "svT": [(0, 0, svT[:, 0:64]), (0, 96, svT[:, 64:96])], "wg": [(0, 0, L0["Wg"])],
        "third": [(0, 0, around(wv[96:128]))],
        "out0": [(0, 0, L0["Ws_vlin"][0:64]), (0, 64, wl[0:64]), (96, 96, L0["Ws_vlin"][64:96])],
        "out0s": [(0, 0, np.broadcast_to(L0["w2_ss"][:, None], (C0, C0))), (0, 64, np.broadcast_to(L0["w2_sv"][:, None], (C0, C1)))],
        "dots": [(96, 0, L0["w2_vv0"])], "out1": [(0, 0, diag(wl[64:96])), (0, CV, around(wl[96:128]))],
        "b2s": [(0, 0, np.tile(L0["w2_vs"], 3))], "c2s": [(0, 0, np.tile(L0["w2_vv1"], 3))],
        "p0": [(0, 0, p0[0:128])], "p1": [(0, 0, p0[128:160])], "dot": [(0, 0, spread2(L0["alpha_dot"].reshape(1, -1)))]})
    w_l1 = place(W1, {
        **{f"in{k}": [(0, 0, in1[k])] for k in range(3)}, **{f"gam{k}": [(0, 0, g1[k])] for k in range(3)},
        **{f"beta{k}": [(0, 0, b1[k])] for k in range(3)}, "mbias": [(0, 0, L1["mdst_bs"][None])],
        "r1": [(0, 0, L1["rw1"]), (64, 0, L1["rb1"][None])], "r2": [(0, 0, L1["rw2"]), (64, 0, L1["rb2"][None])],
        "rad": [(0, 0, L1["rw3"]), (64, 0, L1["roff"][None])],
        **{k: [(0, 0, L1[k])] for k in ("rg1", "rbe1", "rg2", "rbe2")},
        "first": [(64, 0, wlin[0:64]), (0, C1, L1["lin_ws"][0:64])],
        "second": [(96, 0, L1["lin_ws"][64:96]), (0, P, diag(wlin[64:96]))],
        "sbias": [(0, 0, L1["lin_bs"][None])], "third": [(0, 0, around(wlin[96:128]))],
        "p0": [(0, 0, p1[0:128])], "p1": [(0, 0, p1[128:160])], "dot": [(0, 0, spread2(L1["alpha_dot"].reshape(1, -1)))],
        "fill": [(0, 0, spread2(L1["proj_bs"][None]))]})
    f1s, f1v, f2v = np.concatenate([L1["f1_ws"], L1["f1_ws"][:, 128:]], 1), L1["f1_wv"], L1["f2_wv"]
    f1b = np.concatenate([L1["f1_bs"], L1["f1_bs"][128:]])
    pick = by_component(f1v, "cd", "dc")
    back = by_component(f2v, "dc", "cd")
    w_ff = place(W2, {
        "s": [(0, 0, f1s), (64, 0, f1b[None])], "gs": [(0, 0, L1["ln2_w0"])],
        "b0": [(0, 64, L1["ln2_b0"]), (64, 64, np.ones((1, 1), f32))],
        "v0": [(0, 0, pick[:, 0:128])], "v1": [(0, 0, pick[:, 128:192])], "gv": [(0, 0, np.repeat(L1["ln2_w1"], 3))],
        "o": [(0, 0, L1["f2_ws"])], "ov0": [(0, 0, back[0:128])],
        "ov1": [(0, C0, back[128:192]), (64, 0, L1["f2_bs"][None])]})
    w_all = place(W_ALL, {"ident": [(0, 0, np.eye(P, dtype=f32))], "low": [(0, 0, np.tril(np.ones((P, P), f32), -1))]})

    arrays = dict(
        x=padded(a["x"], N_ROWS), a0=padded(a["node_vec1"], N_ROWS),
        src=padded(a["src"], E_ROWS, N).reshape(P, T), dst=padded(a["dst"], E_ROWS, N).reshape(P, T),
        attr16=by_tile(a["edge_attr_16"]), attr64=by_tile(a["edge_attr_64"]),
        attr4=padded(a["edge_attr_4"], E_ROWS).reshape(P, T, 4), attr3=padded(a["edge_attr_3"], E_ROWS).reshape(P, T, 3),
        w_all=w_all, w_l0=w_l0, w_l1=w_l1, w_ff=w_ff)
    nc = bacc.Bacc("TRN2", target_bir_lowering=False, num_devices=1)
    io = {}
    for name, m in arrays.items():
        io[name] = nc.dram_tensor(f"in_{name}", m.shape, mybir.dt.from_np(m.dtype), kind="ExternalInput").ap()
    for name in ("x1", "g", "agg"):
        io[name] = nc.dram_tensor(f"table_{name}", (N_ROWS, D), F32).ap()
    io["rad"] = nc.dram_tensor("table_rad", (64, E_ROWS), F32).ap()
    io["out"] = nc.dram_tensor("out", (N_ROWS, D), F32, kind="ExternalOutput").ap()
    build(nc, io, N_ROWS, T)
    got = run(nc, [{f"in_{k}": m for k, m in arrays.items()}], core_ids=[0]).results[0]["out"]
    return got[:N]
```
